# Optimizing a Trainium2 kernel written in Bass

```python
import numpy as np
import jax
import jax.numpy as jnp

def _softmax(x, axis=-1):
    return jax.nn.softmax(x, axis=axis)

def _gelu(x):
    return jax.nn.gelu(x, approximate=True)

def _silu(x):
    return jax.nn.silu(x)

def _sigmoid(x):
    return jax.nn.sigmoid(x)

def _layernorm(x, axis=-1, eps=1e-05):
    m = jnp.mean(x, axis=axis, keepdims=True)
    v = jnp.var(x, axis=axis, keepdims=True)
    return (x - m) / jnp.sqrt(v + eps)

def _scatter_add(tgt, idx, src, axis=0):
    return tgt.at[idx].add(src)

def _segment_sum(src, seg, n):
    return jax.ops.segment_sum(src, seg, n)
kernel_name = 'mk_perceiver_d1_seqx_r8_8b3013'

def setup_inputs(seed: int=0):
    np.random.seed(seed)
    _w = jnp.asarray

    def _rec_inputs():
        import jax
        import jax.numpy as jnp
        _rk = jax.random.key(seed)
        x = 0.0002417 + 0.9998 * jax.random.normal(jax.random.fold_in(_rk, 1), (16, 32, 128), jnp.float32)
        _lenS = 32 - jax.random.randint(jax.random.fold_in(_rk, 7), (16,), 0, max(1, 32 // 4) + 1, jnp.int32)
        _lenS2 = 512 - jax.random.randint(jax.random.fold_in(_rk, 8), (16,), 0, max(1, 512 // 4) + 1, jnp.int32)
        _ctx_1024P = jax.random.normal(jax.random.fold_in(_rk, 11), (16, 16, 128), jnp.float32)
        _ctx_1024c = jax.random.dirichlet(jax.random.fold_in(_rk, 511), 0.3 * jnp.ones((16,), jnp.float32), (16, 512))
        _ctx_1024t = jnp.einsum('bsk,bkd->bsd', _ctx_1024c, _ctx_1024P)
        _ctx_1024t = _ctx_1024t * jax.lax.rsqrt(jnp.mean(jnp.square(_ctx_1024t)) + 1e-12) * 0.953939
        ctx_1024 = 7.22013e-05 + 1.00017 * (_ctx_1024t + 0.3 * jax.random.normal(jax.random.fold_in(_rk, 611), (16, 512, 128), jnp.float32))
        _validS = jnp.arange(32)[None, :] < _lenS[:, None]
        _validS2 = jnp.arange(512)[None, :] < _lenS2[:, None]
        _causal = jnp.tril(jnp.ones((32, 32), dtype=bool))
        mask_1x1xSxS2_fk1 = jnp.where(jnp.broadcast_to(_validS2[0:1, None, None, :], (1, 1, 32, 512)), 1.0, 0.0).astype(jnp.float32)
        return (x, ctx_1024, mask_1x1xSxS2_fk1)
    x, ctx_1024, mask_1x1xSxS2_fk1 = _rec_inputs()

    def _L0_xattn_setup():
        import jax, jax.numpy as jnp
        import numpy as np
        D_MODEL = 128
        NUM_HEADS = 16
        DEPTH = D_MODEL // NUM_HEADS
        BATCH = 4
        SEQ = 256
        NEG_BIG = -1000000000.0

        def _split_heads(x, b, s):
            return x.reshape(b, s, NUM_HEADS, DEPTH).transpose(0, 2, 1, 3)
        key = jax.random.key(seed)
        ks = jax.random.split(key, 12)
        f = lambda k, shape, scale=1.0: jax.random.normal(k, shape, dtype=jnp.float32) * scale
        inv = 1.0 / np.sqrt(D_MODEL)
        mask = jnp.triu(jnp.ones((SEQ, SEQ), dtype=jnp.float32), k=1)[None, None, :, :]
        return {'v': f(ks[0], (BATCH, SEQ, D_MODEL)), 'k': f(ks[1], (BATCH, SEQ, D_MODEL)), 'q': f(ks[2], (BATCH, SEQ, D_MODEL)), 'mask': mask, 'wq_w': f(ks[3], (D_MODEL, D_MODEL), inv), 'wq_b': jnp.zeros((D_MODEL,), jnp.float32), 'wk_w': f(ks[4], (D_MODEL, D_MODEL), inv), 'wk_b': jnp.zeros((D_MODEL,), jnp.float32), 'wv_w': f(ks[5], (D_MODEL, D_MODEL), inv), 'wv_b': jnp.zeros((D_MODEL,), jnp.float32), 'wo_w': f(ks[6], (D_MODEL, D_MODEL), inv), 'wo_b': jnp.zeros((D_MODEL,), jnp.float32)}
    _L0_xattn_all = _L0_xattn_setup()
    _L0_xattn_in = {k: v for k, v in _L0_xattn_all.items() if k in ('wq_w', 'wq_b', 'wk_w', 'wk_b', 'wv_w', 'wv_b', 'wo_w', 'wo_b')}
    del _L0_xattn_all

    def _L0_attn_setup():
        import jax, jax.numpy as jnp
        import numpy as np
        D_MODEL, D_INNER, D_STATE, DT_RANK, D_CONV = (128, 256, 16, 64, 4)
        BATCH, SEQLEN = (2, 128)

        def _silu(x):
            return x * jax.nn.sigmoid(x)

        def _branch(xz, conv_w, conv_b, Wx, Wdt, bdt, A_log, D):
            d_inner = conv_w.shape[0]
            n = A_log.shape[1]
            dt_rank = Wdt.shape[1]
            x, z = jnp.split(xz, 2, axis=1)
            x = jax.lax.conv_general_dilated(x, conv_w, window_strides=(1,), padding=[(conv_w.shape[-1] - 1, 0)], feature_group_count=d_inner, dimension_numbers=('NCH', 'OIH', 'NCH')) + conv_b[None, :, None]
            x = _silu(x).transpose(0, 2, 1)
            x_dbl = x @ Wx.T
            dt = jax.nn.softplus(x_dbl[..., :dt_rank] @ Wdt.T + bdt)
            B = x_dbl[..., dt_rank:dt_rank + n]
            C = x_dbl[..., dt_rank + n:]
            A = -jnp.exp(A_log)
            deltaA = jnp.exp(jnp.einsum('bld,dn->bldn', dt, A))
            dBu = dt[..., None] * B[:, :, None, :] * x[..., None]

            def step(carry, inp):
                dA_t, dBu_t, C_t = inp
                carry = dA_t * carry + dBu_t
                y_t = jnp.einsum('bdn,bn->bd', carry, C_t)
                return (carry, y_t)
            init = jnp.zeros((x.shape[0], d_inner, n), x.dtype)
            _, ys = jax.lax.scan(step, init, (deltaA.transpose(1, 0, 2, 3), dBu.transpose(1, 0, 2, 3), C.transpose(1, 0, 2)))
            y = ys.transpose(1, 0, 2) + x * D
            return y * _silu(z.transpose(0, 2, 1))
        key = jax.random.key(seed)
        ks = jax.random.split(key, 12)
        s = 0.02
        A_init = jnp.tile(jnp.arange(1, D_STATE + 1, dtype=jnp.float32)[None, :], (D_INNER, 1))
        return {'hidden': jax.random.normal(ks[0], (BATCH, SEQLEN, D_MODEL), jnp.float32), 'W_in': s * jax.random.normal(ks[1], (2 * D_INNER, D_MODEL), jnp.float32), 'conv_w': s * jax.random.normal(ks[2], (D_INNER, 1, D_CONV), jnp.float32), 'conv_b': s * jax.random.normal(ks[3], (D_INNER,), jnp.float32), 'Wx': s * jax.random.normal(ks[4], (DT_RANK + 2 * D_STATE, D_INNER), jnp.float32), 'Wdt': s * jax.random.normal(ks[5], (D_INNER, DT_RANK), jnp.float32), 'bdt': s * jax.random.normal(ks[6], (D_INNER,), jnp.float32), 'A_log': jnp.log(A_init), 'D': jnp.ones((D_INNER,), jnp.float32), 'conv_w_b': s * jax.random.normal(ks[7], (D_INNER, 1, D_CONV), jnp.float32), 'conv_b_b': s * jax.random.normal(ks[8], (D_INNER,), jnp.float32), 'Wx_b': s * jax.random.normal(ks[9], (DT_RANK + 2 * D_STATE, D_INNER), jnp.float32), 'Wdt_b': s * jax.random.normal(ks[10], (D_INNER, DT_RANK), jnp.float32), 'bdt_b': s * jax.random.normal(ks[11], (D_INNER,), jnp.float32), 'A_b_log': jnp.log(A_init), 'D_b': jnp.ones((D_INNER,), jnp.float32), 'W_out': s * jax.random.normal(jax.random.fold_in(key, 99), (D_MODEL, D_INNER), jnp.float32)}
    _L0_attn_all = _L0_attn_setup()
    _L0_attn_in = {k: v for k, v in _L0_attn_all.items() if k in ('W_in', 'conv_w', 'conv_b', 'Wx', 'Wdt', 'bdt', 'A_log', 'D', 'conv_w_b', 'conv_b_b', 'Wx_b', 'Wdt_b', 'bdt_b', 'A_b_log', 'D_b', 'W_out')}
    del _L0_attn_all

    def _L0_ffn_setup():
        import jax, jax.numpy as jnp
        import numpy as np
        B, S, D, H, E, K = (2, 128, 128, 64, 16, 4)
        HS = 2 * H

        def silu(z):
            return z * jax.nn.sigmoid(z)
        key = jax.random.key(seed)
        ks = jax.random.split(key, 8)
        sc = lambda fan_in: 1.0 / np.sqrt(fan_in)
        x = jax.random.normal(ks[0], (B, S, D), jnp.float32)
        gate_w = jax.random.normal(ks[1], (E, D), jnp.float32) * sc(D)
        ws_in = jax.random.normal(ks[2], (D, HS), jnp.float32) * sc(D)
        vs_in = jax.random.normal(ks[3], (D, HS), jnp.float32) * sc(D)
        ws_out = jax.random.normal(ks[4], (HS, D), jnp.float32) * sc(HS)
        e_win = jax.random.normal(ks[5], (E, D, H), jnp.float32) * sc(D)
        e_vin = jax.random.normal(ks[6], (E, D, H), jnp.float32) * sc(D)
        e_wout = jax.random.normal(ks[7], (E, H, D), jnp.float32) * sc(H)
        return {'x': x, 'gate_w': gate_w, 'ws_in': ws_in, 'vs_in': vs_in, 'ws_out': ws_out, 'e_win': e_win, 'e_vin': e_vin, 'e_wout': e_wout}
    _L0_ffn_all = _L0_ffn_setup()
    _L0_ffn_in = {k: v for k, v in _L0_ffn_all.items() if k in ('gate_w', 'ws_in', 'vs_in', 'ws_out', 'e_win', 'e_vin', 'e_wout')}
    del _L0_ffn_all
    return {'x': x, 'ctx_1024': ctx_1024, 'mask_1x1xSxS2_fk1': mask_1x1xSxS2_fk1, 'L0_xattn_wq_w': _L0_xattn_in['wq_w'], 'L0_xattn_wq_b': _L0_xattn_in['wq_b'], 'L0_xattn_wk_w': _L0_xattn_in['wk_w'], 'L0_xattn_wk_b': _L0_xattn_in['wk_b'], 'L0_xattn_wv_w': _L0_xattn_in['wv_w'], 'L0_xattn_wv_b': _L0_xattn_in['wv_b'], 'L0_xattn_wo_w': _L0_xattn_in['wo_w'], 'L0_xattn_wo_b': _L0_xattn_in['wo_b'], 'L0_attn_W_in': _L0_attn_in['W_in'], 'L0_attn_conv_w': _L0_attn_in['conv_w'], 'L0_attn_conv_b': _L0_attn_in['conv_b'], 'L0_attn_Wx': _L0_attn_in['Wx'], 'L0_attn_Wdt': _L0_attn_in['Wdt'], 'L0_attn_bdt': _L0_attn_in['bdt'], 'L0_attn_A_log': _L0_attn_in['A_log'], 'L0_attn_D': _L0_attn_in['D'], 'L0_attn_conv_w_b': _L0_attn_in['conv_w_b'], 'L0_attn_conv_b_b': _L0_attn_in['conv_b_b'], 'L0_attn_Wx_b': _L0_attn_in['Wx_b'], 'L0_attn_Wdt_b': _L0_attn_in['Wdt_b'], 'L0_attn_bdt_b': _L0_attn_in['bdt_b'], 'L0_attn_A_b_log': _L0_attn_in['A_b_log'], 'L0_attn_D_b': _L0_attn_in['D_b'], 'L0_attn_W_out': _L0_attn_in['W_out'], 'L0_ffn_gate_w': _L0_ffn_in['gate_w'], 'L0_ffn_ws_in': _L0_ffn_in['ws_in'], 'L0_ffn_vs_in': _L0_ffn_in['vs_in'], 'L0_ffn_ws_out': _L0_ffn_in['ws_out'], 'L0_ffn_e_win': _L0_ffn_in['e_win'], 'L0_ffn_e_vin': _L0_ffn_in['e_vin'], 'L0_ffn_e_wout': _L0_ffn_in['e_wout']}

def reference(x, ctx_1024, mask_1x1xSxS2_fk1, L0_xattn_wq_w, L0_xattn_wq_b, L0_xattn_wk_w, L0_xattn_wk_b, L0_xattn_wv_w, L0_xattn_wv_b, L0_xattn_wo_w, L0_xattn_wo_b, L0_attn_W_in, L0_attn_conv_w, L0_attn_conv_b, L0_attn_Wx, L0_attn_Wdt, L0_attn_bdt, L0_attn_A_log, L0_attn_D, L0_attn_conv_w_b, L0_attn_conv_b_b, L0_attn_Wx_b, L0_attn_Wdt_b, L0_attn_bdt_b, L0_attn_A_b_log, L0_attn_D_b, L0_attn_W_out, L0_ffn_gate_w, L0_ffn_ws_in, L0_ffn_vs_in, L0_ffn_ws_out, L0_ffn_e_win, L0_ffn_e_vin, L0_ffn_e_wout):
    import jax
    import jax.numpy as jnp

    def _L0_xattn_ref(v, k, q, mask, wq_w, wq_b, wk_w, wk_b, wv_w, wv_b, wo_w, wo_b):
        import jax, jax.numpy as jnp
        import numpy as np
        D_MODEL = 128
        NUM_HEADS = 16
        DEPTH = D_MODEL // NUM_HEADS
        BATCH = 4
        SEQ = 256
        NEG_BIG = -1000000000.0

        def _split_heads(x, b, s):
            return x.reshape(b, s, NUM_HEADS, DEPTH).transpose(0, 2, 1, 3)
        b, sq, _ = q.shape
        sk = k.shape[1]
        qh = _split_heads(q @ wq_w + wq_b, b, sq)
        kh = _split_heads(k @ wk_w + wk_b, b, sk)
        vh = _split_heads(v @ wv_w + wv_b, b, sk)
        logits = jnp.einsum('bhqd,bhkd->bhqk', qh, kh) / jnp.sqrt(jnp.float32(DEPTH))
        logits = logits + mask * NEG_BIG
        attn = jax.nn.softmax(logits, axis=-1)
        out = jnp.einsum('bhqk,bhkd->bhqd', attn, vh)
        out = out.transpose(0, 2, 1, 3).reshape(b, sq, D_MODEL)
        return out @ wo_w + wo_b

    def _L0_attn_ref(hidden, W_in, conv_w, conv_b, Wx, Wdt, bdt, A_log, D, conv_w_b, conv_b_b, Wx_b, Wdt_b, bdt_b, A_b_log, D_b, W_out):
        import jax, jax.numpy as jnp
        import numpy as np
        D_MODEL, D_INNER, D_STATE, DT_RANK, D_CONV = (128, 256, 16, 64, 4)
        BATCH, SEQLEN = (2, 128)

        def _silu(x):
            return x * jax.nn.sigmoid(x)

        def _branch(xz, conv_w, conv_b, Wx, Wdt, bdt, A_log, D):
            d_inner = conv_w.shape[0]
            n = A_log.shape[1]
            dt_rank = Wdt.shape[1]
            x, z = jnp.split(xz, 2, axis=1)
            x = jax.lax.conv_general_dilated(x, conv_w, window_strides=(1,), padding=[(conv_w.shape[-1] - 1, 0)], feature_group_count=d_inner, dimension_numbers=('NCH', 'OIH', 'NCH')) + conv_b[None, :, None]
            x = _silu(x).transpose(0, 2, 1)
            x_dbl = x @ Wx.T
            dt = jax.nn.softplus(x_dbl[..., :dt_rank] @ Wdt.T + bdt)
            B = x_dbl[..., dt_rank:dt_rank + n]
            C = x_dbl[..., dt_rank + n:]
            A = -jnp.exp(A_log)
            deltaA = jnp.exp(jnp.einsum('bld,dn->bldn', dt, A))
            dBu = dt[..., None] * B[:, :, None, :] * x[..., None]

            def step(carry, inp):
                dA_t, dBu_t, C_t = inp
                carry = dA_t * carry + dBu_t
                y_t = jnp.einsum('bdn,bn->bd', carry, C_t)
                return (carry, y_t)
            init = jnp.zeros((x.shape[0], d_inner, n), x.dtype)
            _, ys = jax.lax.scan(step, init, (deltaA.transpose(1, 0, 2, 3), dBu.transpose(1, 0, 2, 3), C.transpose(1, 0, 2)))
            y = ys.transpose(1, 0, 2) + x * D
            return y * _silu(z.transpose(0, 2, 1))
        xz = (hidden @ W_in.T).transpose(0, 2, 1)
        out_f = _branch(xz, conv_w, conv_b, Wx, Wdt, bdt, A_log, D)
        out_b = _branch(xz[..., ::-1], conv_w_b, conv_b_b, Wx_b, Wdt_b, bdt_b, A_b_log, D_b)
        out = (out_f + out_b[:, ::-1]) / 2.0
        return out @ W_out.T

    def _L0_ffn_ref(x, gate_w, ws_in, vs_in, ws_out, e_win, e_vin, e_wout):
        import jax, jax.numpy as jnp
        import numpy as np
        B, S, D, H, E, K = (2, 128, 128, 64, 16, 4)
        HS = 2 * H

        def silu(z):
            return z * jax.nn.sigmoid(z)
        b, s, d = x.shape
        T = b * s
        xf = x.reshape(T, d)
        g = jax.nn.sigmoid(xf @ gate_w.T)
        topv, topi = jax.lax.top_k(g, K)
        wn = topv / jnp.sum(topv, axis=-1, keepdims=True)
        combine = jnp.zeros_like(g).at[jnp.arange(T)[:, None], topi].add(wn)
        hin = jnp.einsum('td,edh->eth', xf, e_win)
        vin = jnp.einsum('td,edh->eth', xf, e_vin)
        h = silu(hin) * vin * combine.T[:, :, None]
        routed = jnp.einsum('eth,ehd->td', h, e_wout)
        shared = silu(xf @ ws_in) * (xf @ vs_in) @ ws_out
        return (shared + routed).reshape(b, s, d)
    x = x + _L0_xattn_ref(ctx_1024, ctx_1024, _layernorm(x, axis=-1), mask_1x1xSxS2_fk1, L0_xattn_wq_w, L0_xattn_wq_b, L0_xattn_wk_w, L0_xattn_wk_b, L0_xattn_wv_w, L0_xattn_wv_b, L0_xattn_wo_w, L0_xattn_wo_b)
    x = x + _L0_attn_ref(_layernorm(x, axis=-1), L0_attn_W_in, L0_attn_conv_w, L0_attn_conv_b, L0_attn_Wx, L0_attn_Wdt, L0_attn_bdt, L0_attn_A_log, L0_attn_D, L0_attn_conv_w_b, L0_attn_conv_b_b, L0_attn_Wx_b, L0_attn_Wdt_b, L0_attn_bdt_b, L0_attn_A_b_log, L0_attn_D_b, L0_attn_W_out)
    x = x + _L0_ffn_ref(_layernorm(x, axis=-1), L0_ffn_gate_w, L0_ffn_ws_in, L0_ffn_vs_in, L0_ffn_ws_out, L0_ffn_e_win, L0_ffn_e_vin, L0_ffn_e_wout)
    return x

_drawn_inputs = setup_inputs


def setup_inputs(seed=0):
    import zlib

    import numpy as np

    out = dict(_drawn_inputs(seed))
    spreads = {'L0_xattn_wq_b': (0.0, 0.1),
     'L0_xattn_wk_b': (0.0, 0.8),
     'L0_xattn_wv_b': (0.0, 0.1),
     'L0_xattn_wo_b': (0.0, 0.1),
     'L0_attn_D': (1.0, 0.6),
     'L0_attn_D_b': (1.0, 0.6)}
    factors = {'L0_attn_W_in': 8.0,
     'L0_attn_conv_w': 8.0,
     'L0_attn_conv_b': 8.0,
     'L0_attn_Wx': 8.0,
     'L0_attn_Wdt': 8.0,
     'L0_attn_bdt': 8.0,
     'L0_attn_A_log': 8.0,
     'L0_attn_conv_w_b': 8.0,
     'L0_attn_conv_b_b': 8.0,
     'L0_attn_Wx_b': 8.0,
     'L0_attn_Wdt_b': 8.0,
     'L0_attn_bdt_b': 8.0,
     'L0_attn_A_b_log': 8.0,
     'L0_attn_W_out': 8.0}
    for name, (base, spread) in spreads.items():
        noise = np.random.default_rng([zlib.crc32(name.encode()), seed]).standard_normal(out[name].shape)
        drawn = base * np.exp(spread * noise) if base else spread * noise
        out[name] = jnp.asarray(drawn.astype(out[name].dtype))
    for name, factor in factors.items():
        out[name] = (out[name] * factor).astype(out[name].dtype)
    return out
```

```python
from contextlib import ExitStack

import concourse.bass as bass
from concourse import mybir

F32 = mybir.dt.float32
BF16 = mybir.dt.bfloat16
ALU = mybir.AluOpType
ACT = mybir.ActivationFunctionType
AX = mybir.AxisListType

P = 128
EPS = 1e-5
NEG_BIG = -1e9


def perceiver_block(nc: bass.Bass, a: dict, out: bass.AP):
    B, S, D = a["x"].shape
    K = a["ctx_1024"].shape[1]
    T = B * S
    TT = T // P
    H = 16
    DH = D // H
    G = 4
    HG = H // G
    KC = K // P
    DI = a["L0_attn_W_in"].shape[0] // 2
    NH = DI // P
    N = a["L0_attn_A_log"].shape[1]
    R = a["L0_attn_Wdt"].shape[1]
    TAPS = a["L0_attn_conv_w"].shape[2]
    PAD = TAPS - 1
    E, _, HE = a["L0_ffn_e_win"].shape
    TOPK = 4
    EP = E * HE // P
    SCALE = float(DH) ** -0.5
    PAIRS = B // 2
    NP = N // 2
    DIRS = 2
    assert T == 512 and D == P and HG * S == P and K == 512 and 2 * N == 32

    with ExitStack() as ctx:
        def sb(name, shape, dt=F32):
            return ctx.enter_context(nc.sbuf_tensor(name, shape, dt))

        def sem(name):
            return ctx.enter_context(nc.semaphore(name))

        bank = [ctx.enter_context(nc.psum_tensor(f"bank{i}", [P, 512], F32)) for i in range(8)]

        ident = sb("ident", [P, P])
        headmask = sb("headmask", [P, H])
        groupmask = sb("groupmask", [P, HG])
        pick = sb("pick", [P, 32])
        pick_bc = sb("pick_bc", [P, 2 * N, P], BF16)
        pick_ex = sb("pick_ex", [P, E, HE], BF16)
        earlier = sb("earlier", [P, E, E])

        wq = sb("wq", [P, D])
        wk = sb("wk", [P, D])
        wv = sb("wv", [P, D])
        wo = sb("wo", [P, D])
        bq = sb("bq", [P, 1])
        bk = sb("bk", [P, 1])
        bv = sb("bv", [P, D])
        bo = sb("bo", [P, D])
        mask_in = sb("mask_in", [P, K])
        mask_neg = sb("mask_neg", [P, KC, P])
        w_in_rows = sb("w_in_rows", [P, 2 * NH, D])
        w_in = sb("w_in", [P, 2 * NH, P])
        wx_rows = sb("wx_rows", [R + 2 * N, DIRS, DI])
        wx_dt = sb("wx_dt", [P, DIRS, NH, R])
        wx_bc = sb("wx_bc", [P, DIRS, NH, 4, 2 * N])
        wdt_rows = sb("wdt_rows", [P, DIRS, NH, R])
        wdt = sb("wdt", [R, DIRS, NH, P])
        w_out_rows = sb("w_out_rows", [P, DI])
        w_out = sb("w_out", [P, NH, P])
        conv_w = sb("conv_w", [P, DIRS, NH, TAPS])
        conv_b = sb("conv_b", [P, DIRS, NH])
        bdt = sb("bdt", [P, DIRS, NH])
        a_log = sb("a_log", [P, DIRS, NH, N])
        a_exp = sb("a_exp", [P, DIRS, NH, N])
        a_neg = sb("a_neg", [P, DIRS, NH, N])
        d_skip = sb("d_skip", [P, DIRS, NH])
        gate_rows = sb("gate_rows", [E, D])
        gate_w = sb("gate_w", [P, E])
        ws_in = sb("ws_in", [P, P])
        vs_in = sb("vs_in", [P, P])
        ws_out = sb("ws_out", [P, D])
        e_win = sb("e_win", [P, E, HE])
        e_vin = sb("e_vin", [P, E, HE])
        e_wout = sb("e_wout", [P, EP, D])

        x_rows = sb("x_rows", [P, TT, D])
        xb_rows = sb("xb_rows", [P, TT, D])
        x1_rows = sb("x1_rows", [P, TT, D])
        x2_rows = sb("x2_rows", [P, TT, D])
        y_rows = sb("y_rows", [P, TT, D])
        norm_rows = sb("norm_rows", [P, TT, D])
        norm_cols = sb("norm_cols", [P, T])
        stats = sb("stats", [P, TT, 6])
        moments = sb("moments", [P, TT, 2])
        ln_var = sb("ln_var", [P, TT])
        rstd = sb("rstd", [P, TT])
        newton = sb("newton", [P, 3, TT])
        q_cols = sb("q_cols", [P, T])
        heads_cols = sb("heads_cols", [P, T])

        def two(name, shape):
            t = sb(name, [P, 2, *shape])
            return t, [t[:, u] for u in range(2)]

        ctx_rows_all, ctx_rows = two("ctx_rows", [KC, D])
        ctx_cols = sb("ctx_cols", [P, K])
        k_cols_all, k_cols = two("k_cols", [K])
        v_rows_all, v_rows = two("v_rows", [KC, D])
        q_block = [sb(f"q_block{u}", [P, H, S]) for u in range(2)]
        masked_all, masked = two("masked", [K])
        probs_all, probs = two("probs", [K])
        probs_t_all, probs_t = two("probs_t", [G, KC, P])
        neg_max = [sb(f"neg_max{u}", [P, G]) for u in range(2)]
        row_sum = [sb(f"row_sum{u}", [P, G]) for u in range(2)]
        row_inv = [sb(f"row_inv{u}", [P, G]) for u in range(2)]
        row_inv_wide = [sb(f"row_inv_wide{u}", [P, G, S]) for u in range(2)]
        turnstile = [sb(f"turnstile{s}", [P, 1]) for s in range(4)]
        own_inv = sb("own_inv", [P, HG, S])
        own_out = sb("own_out", [P, HG, S])

        x_pad = sb("x_pad", [P, NH, B, S + 2 * PAD])
        z_act = sb("z_act", [P, NH, T])
        conv = sb("conv", [P, DIRS, NH, T])
        u_cols = sb("u_cols", [P, DIRS, NH, T])
        dt_low = sb("dt_low", [R, DIRS, T])
        bc_parts = [sb(f"bc_parts{d}", [P, T], BF16) for d in range(DIRS)]
        bc_rest = sb("bc_rest", [P, DIRS, T])
        bc_mid = sb("bc_mid", [P, DIRS, T], BF16)
        bc_low = sb("bc_low", [P, DIRS, T])
        sp_abs = sb("sp_abs", [P, DIRS, NH, T])
        sp_exp = sb("sp_exp", [P, DIRS, NH, T])
        sp_ln = sb("sp_ln", [P, DIRS, NH, T])
        sp_pos = probs_t_all[:, 0].rearrange("p g c m -> p (g c m)").rearrange("p (d h t) -> p d h t", d=DIRS, h=NH)
        dt_cols = sb("dt_cols", [P, DIRS, NH, T])
        dtu = conv
        decay = [[sb(f"decay{d}_{u}", [P, NH * T]) for u in range(2)] for d in range(DIRS)]
        feed, state, read = ([t[:, u].rearrange("p h t -> p (h t)") for u in range(2)] for t in (sp_abs, sp_exp, sp_ln))
        skip, gated = (probs_t_all[:, 1, 2 * n:2 * n + 2].rearrange("p g c m -> p g (c m)") for n in range(2))

        gates = sb("gates", [P, TT, E])
        beats, ties = (t[:, :, :].rearrange("p u k -> p (u k)").rearrange("p (t e f) -> p t e f", t=TT, e=E)
                       for t in (masked_all, probs_all))
        rank = sb("rank", [P, TT, E])
        kept = sb("kept", [P, TT, E])
        kept_sum = sb("kept_sum", [P, TT])
        kept_inv = sb("kept_inv", [P, TT])
        combine = sb("combine", [P, TT, E])
        comb_parts = sb("comb_parts", [P, T], BF16)
        comb_hi, comb_mid = (bc_mid[0:E, n, :] for n in range(2))
        comb_rest = bc_rest[0:E, :, :]
        comb_cols = bc_low[0:E, 0, :]
        act_in = [k_cols_all[:, u, :] for u in range(2)]
        mixed, hidden = ([t[:, u].rearrange("p c d -> p (c d)") for u in range(2)] for t in (ctx_rows_all, v_rows_all))

        x_in, attn_w_in, mask_loaded, mamba_w_in, ffn_w_in = (
            sem(n) for n in ("x_in", "attn_w_in", "mask_loaded", "mamba_w_in", "ffn_w_in"))
        ctx_in = [sem("ctx_in0"), sem("ctx_in1")]
        out_written = sem("out_written")
        consts_step, ident_built, consts_built, pads_cleared, bo_added = (
            sem(n) for n in ("consts_step", "ident_built", "consts_built", "pads_cleared", "bo_added"))
        picks_spread, groupmask_built, mask_scaled, a_ready = (
            sem(n) for n in ("picks_spread", "groupmask_built", "mask_scaled", "a_ready"))
        dve_step, act_step = sem("dve_step"), sem("act_step")
        ln_moments, ln_rstd, ln_rows, ln_turned, ln_cols = (
            sem(n) for n in ("ln_moments", "ln_rstd", "ln_rows", "ln_turned", "ln_cols"))
        weights_turned, weights_kept = sem("weights_turned"), sem("weights_kept")
        q_projected, q_ready, q_blocked = sem("q_projected"), sem("q_ready"), sem("q_blocked")
        ctx_turned, ctx_kept, k_projected, k_ready, v_projected, v_ready = (
            sem(n) for n in ("ctx_turned", "ctx_kept", "k_projected", "k_ready", "v_projected", "v_ready"))
        scores_done, masked_ready, probs_ready, p_turned, pt_even, pt_odd = (
            sem(n) for n in ("scores_done", "masked_ready", "probs_ready", "p_turned", "pt_even", "pt_odd"))
        inv_ready, attended, own_step, heads_ready = (
            sem(n) for n in ("inv_ready", "attended", "own_step", "heads_ready"))
        attn_out, x1_ready, xz_done, x_padded, z_ready, conv_done, u_ready = (
            sem(n) for n in ("attn_out", "x1_ready", "xz_done", "x_padded", "z_ready", "conv_done", "u_ready"))
        xdbl_done, dt_low_kept, bc_split, dt_raw, sp_ready, pos_ready, dt_ready, dtu_ready = (
            sem(n) for n in ("xdbl_done", "dt_low_kept", "bc_split", "dt_raw", "sp_ready", "pos_ready",
                             "dt_ready", "dtu_ready"))
        b_spread, c_spread, decayed, fed, scanned, was_read, summed, skip_ready = (
            sem(n) for n in ("b_spread", "c_spread", "decayed", "fed", "scanned", "was_read", "summed",
                             "skip_ready"))
        y_done, gated_ready, mamba_out, x2_ready = (
            sem(n) for n in ("y_done", "gated_ready", "mamba_out", "x2_ready"))
        gate_done, gates_ready, combine_ready, combine_turned, comb_split = (
            sem(n) for n in ("gate_done", "gates_ready", "combine_ready", "combine_turned", "comb_split"))
        h_done, h_act, h_mixed, h_ready, comb_spread, h_used, ffn_done, y_ready = (
            sem(n) for n in ("h_done", "h_act", "h_mixed", "h_ready", "comb_spread", "h_used", "ffn_done",
                             "y_ready"))

        score_bank, turn_bank, proj_bank, out_bank = bank[0:2], bank[2:4], bank[4:6], bank[6:8]
        rows_of = lambda t: t.rearrange("b s d -> (b s) d").rearrange("(t p) d -> p t d", p=P)
        column = lambda v: v.rearrange("(p o) -> p o", o=1)
        halves = lambda v: v.rearrange("(h p) -> p h", p=P)
        MAMBA = [("L0_attn_conv_w", "L0_attn_conv_b", "L0_attn_Wx", "L0_attn_Wdt", "L0_attn_bdt",
                  "L0_attn_A_log", "L0_attn_D"),
                 ("L0_attn_conv_w_b", "L0_attn_conv_b_b", "L0_attn_Wx_b", "L0_attn_Wdt_b",
                  "L0_attn_bdt_b", "L0_attn_A_b_log", "L0_attn_D_b")]
        ATTN_LOADS, MAMBA_LOADS, FFN_LOADS = 8, 2 + 8 * DIRS, 7

        block = ctx.enter_context(nc.Block())

        @block.sync
        def _(sp):
            def load_ctx(b, u, late):
                if late:
                    sp.wait_ge(ctx_turned, b - 1)
                src = a["ctx_1024"][bass.ds(b, 1)].rearrange("o (p c) d -> (o p) c d", c=KC)
                sp.dma_start(ctx_rows[u][:, :, :], src).then_inc(ctx_in[u], 16)

            sp.dma_start(x_rows[:, :, :], rows_of(a["x"])).then_inc(x_in, 16)
            load_ctx(0, 0, False)
            for t, name in ((wk, "wk"), (wv, "wv"), (wq, "wq"), (wo, "wo")):
                sp.dma_start(t[:, :], a[f"L0_xattn_{name}_w"]).then_inc(attn_w_in, 16)
            load_ctx(1, 1, False)
            sp.dma_start(w_in_rows[:, :, :], a["L0_attn_W_in"].rearrange("(c p) d -> p c d", p=P)).then_inc(mamba_w_in, 16)
            sp.dma_start(w_out_rows[:, :], a["L0_attn_W_out"]).then_inc(mamba_w_in, 16)
            for d, (cw, cb, wx, wd, bd, al, ds) in enumerate(MAMBA):
                sp.dma_start(wx_rows[:, d, :], a[wx]).then_inc(mamba_w_in, 16)
                sp.dma_start(wdt_rows[:, d, :, :], a[wd].rearrange("(h p) r -> p h r", p=P)).then_inc(mamba_w_in, 16)
                sp.dma_start(conv_w[:, d, :, :], a[cw].rearrange("(h p) o j -> p h (o j)", p=P)).then_inc(mamba_w_in, 16)
                sp.dma_start(a_log[:, d, :, :], a[al].rearrange("(h p) n -> p h n", p=P)).then_inc(mamba_w_in, 16)
                sp.dma_start(conv_b[:, d, :], halves(a[cb]), allow_slow_non_contiguous=True).then_inc(mamba_w_in, 16)
                sp.dma_start(bdt[:, d, :], halves(a[bd]), allow_slow_non_contiguous=True).then_inc(mamba_w_in, 16)
                sp.dma_start(d_skip[:, d, :], halves(a[ds]), allow_slow_non_contiguous=True).then_inc(mamba_w_in, 16)
                sp.dma_start(gate_rows[:, :], a["L0_ffn_gate_w"]).then_inc(mamba_w_in, 16) if d == 0 else \
                    sp.dma_start(ws_out[:, :], a["L0_ffn_ws_out"]).then_inc(mamba_w_in, 16)
            with sp.Fori(1, PAIRS) as i:
                for u in range(2):
                    load_ctx(2 * i + u, u, True)
            sp.dma_start(e_win[:, :, :], a["L0_ffn_e_win"].rearrange("e d h -> d e h")).then_inc(ffn_w_in, 16)
            sp.dma_start(e_vin[:, :, :], a["L0_ffn_e_vin"].rearrange("e d h -> d e h")).then_inc(ffn_w_in, 16)
            sp.dma_start(e_wout[:, :, :], a["L0_ffn_e_wout"].rearrange("(j e) h d -> (e h) j d", j=EP)).then_inc(ffn_w_in, 16)
            sp.dma_start(ws_in[:, :], a["L0_ffn_ws_in"]).then_inc(ffn_w_in, 16)
            sp.dma_start(vs_in[:, :], a["L0_ffn_vs_in"]).then_inc(ffn_w_in, 16)
            sp.wait_ge(y_ready, 1)
            sp.dma_start(rows_of(out), y_rows[:, :, :]).then_inc(out_written, 16)
            sp.wait_ge(out_written, 16)

        @block.gpsimd
        def _(pool):
            built = [0]

            def link(ins):
                built[0] += 1
                ins.then_inc(consts_step, 1)
                pool.wait_ge(consts_step, built[0])

            def where(t, pattern, base, step, compare, fill):
                return nc.gpsimd.affine_select(out=t, in_=t, compare_op=compare, fill=fill, base=base,
                                               pattern=pattern, channel_multiplier=step)

            link(pool.memset(ident[:, :], 0.0))
            where(ident[:, :], [[-1, P]], 0, 1, ALU.not_equal, 1.0).then_inc(ident_built, 1)
            link(pool.memset(headmask[:, :], 1.0))
            link(where(headmask[:, :], [[-DH, H]], 0, 1, ALU.is_ge, 0.0))
            link(where(headmask[:, :], [[DH, H]], DH - 1, -1, ALU.is_ge, 0.0))
            link(pool.memset(pick[:, :], 0.0))
            for part in range(3):
                link(where(pick[:, :], [[-1, 32]], -32 * part, 1, ALU.not_equal, 1.0))
            link(pool.memset(earlier[:, :, :], 1.0))
            where(earlier[:, :, :], [[1, E], [-1, E]], -1, 0, ALU.is_ge, 0.0).then_inc(consts_built, 1)
            pool.memset(x_pad[:, :, :, :], 0.0).then_inc(pads_cleared, 1)
            for d in range(DIRS):
                first = 0 if d == 0 else S - 1
                for u in range(2):
                    t = decay[d][u][:, :].rearrange("p (b s) -> p b s", s=S)
                    pool.memset(t[:, :, first:first + 1], 0.0).then_inc(pads_cleared, 1)

            pool.wait_ge(x_in, 16)
            pool.wait_ge(attn_w_in, 16 * ATTN_LOADS)
            pool.tensor_tensor(xb_rows[:, :, :], x_rows[:, :, :],
                               bo[:, :].unsqueeze(1).to_broadcast([P, TT, D]), ALU.add).then_inc(bo_added, 1)

            def block_q(b, u, late):
                if late:
                    pool.wait_ge(scores_done, G * (b - 1))
                pool.tensor_tensor(q_block[u][:, :, :],
                                   q_cols[:, bass.ds(b * S, S)].unsqueeze(1).to_broadcast([P, H, S]),
                                   headmask[:, :].unsqueeze(2).to_broadcast([P, H, S]),
                                   ALU.mult).then_inc(q_blocked, 1)

            pool.wait_ge(q_ready, 1)
            for u in range(2):
                block_q(u, u, False)
            with pool.Fori(1, PAIRS) as i:
                for u in range(2):
                    block_q(2 * i + u, u, True)

        @block.tensor
        def _(pe):
            def turn_norm(n):
                to = bank[(2, 1, 5)[n]]
                pe.wait_ge(ln_rows, n + 1)
                for t in range(TT):
                    last = pe.transpose(to[:, t * P:(t + 1) * P], norm_rows[:, t, :], ident[:, :])
                last.then_inc(ln_turned, 1)

            def turn_ctx(b, u, i, late):
                pe.wait_ge(ctx_in[u], 16 * (i + 1))
                if late:
                    pe.wait_ge(v_ready, b)
                for c in range(KC):
                    last = pe.transpose(proj_bank[0][:, c * P:(c + 1) * P], ctx_rows[u][:, c, :], ident[:, :])
                last.then_inc(ctx_turned, 1)

            def project_k(b):
                pe.wait_ge(ctx_kept, b + 1)
                pe.wait_ge(k_ready, b)
                pe.matmul(proj_bank[1][:, :], wk[:, :], ctx_cols[:, :], start=True, stop=True).then_inc(k_projected, 1)

            def project_v(b):
                for c in range(KC):
                    last = pe.matmul(proj_bank[0][:, c * P:(c + 1) * P], ctx_cols[:, c * P:(c + 1) * P],
                                     wv[:, :], start=True, stop=True)
                last.then_inc(v_projected, 1)

            def score(b, u, g, late):
                if g == 0:
                    pe.wait_ge(q_blocked, b + 1)
                    pe.wait_ge(k_ready, b + 1)
                if late or g >= 2:
                    pe.wait_ge(masked_ready, G * b + g - 1)
                pe.matmul(score_bank[g % 2][:, :], q_block[u][:, g * HG:(g + 1) * HG, :],
                          k_cols[u][:, :], start=True, stop=True).then_inc(scores_done, 1)

            def turn_p(b, g, late):
                pe.wait_ge(probs_ready, G * b + g + 1)
                if late or g >= 2:
                    pe.wait_ge((pt_even, pt_odd)[g % 2], 2 * b + g // 2)
                for c in range(KC):
                    last = pe.transpose(turn_bank[g % 2][:, c * P:(c + 1) * P],
                                        probs[g % 2][:, c * P:(c + 1) * P], ident[:, :])
                last.then_inc(p_turned, 1)

            def attend(b, u, late):
                pe.wait_ge(pt_even, 2 * b + 2)
                pe.wait_ge(pt_odd, 2 * b + 2)
                pe.wait_ge(v_ready, b + 1)
                pe.wait_ge(inv_ready, b + 1)
                if late:
                    pe.wait_ge(heads_ready, b)
                pe.matmul(out_bank[u][:, P:2 * P], row_inv_wide[u][:, :, :], ident[:, :], start=True, stop=True)
                for c in range(KC):
                    for g in range(G):
                        rows = slice(g * 32, g * 32 + 32)
                        last = pe.matmul(out_bank[u][rows, 0:P], v_rows[u][:, c, rows], probs_t[u][:, g, c, :],
                                         start=(c == 0), stop=(c == KC - 1))
                last.then_inc(attended, 1)

            def turn_weights():
                pe.wait_ge(mamba_w_in, 16 * MAMBA_LOADS)
                for c in range(2 * NH):
                    last = pe.transpose(bank[6][:, c * P:(c + 1) * P], w_in_rows[:, c, :], ident[:, :])
                last.then_inc(weights_turned, 1)
                W = R + 2 * N
                for d in range(DIRS):
                    for h in range(NH):
                        at = (d * NH + h) * W
                        last = pe.transpose(bank[7][:, at:at + W], wx_rows[:, d, h * P:(h + 1) * P], ident[0:W, 0:W])
                last.then_inc(weights_turned, 1)
                pe.wait_ge(ln_cols, 1)
                for h in range(NH):
                    pe.transpose(bank[2][:, h * P:(h + 1) * P], w_out_rows[:, h * P:(h + 1) * P], ident[:, :])
                pe.transpose(bank[2][:, NH * P:NH * P + E], gate_rows[:, :], ident[0:E, 0:E]).then_inc(weights_turned, 1)
                pe.wait_ge(q_ready, 1)
                for d in range(DIRS):
                    for h in range(NH):
                        at = (d * NH + h) * P
                        last = pe.transpose(bank[3][0:R, at:at + P], wdt_rows[:, d, h, :], ident[:, :])
                last.then_inc(weights_turned, 1)

            pe.wait_ge(ident_built, 1)
            turn_ctx(0, 0, 0, False)
            turn_norm(0)
            pe.wait_ge(attn_w_in, 16 * ATTN_LOADS)
            pe.wait_ge(ln_cols, 1)
            pe.matmul(bank[3][:, :], wq[:, :], norm_cols[:, :], start=True, stop=True).then_inc(q_projected, 1)
            pe.wait_ge(ctx_kept, 1)
            pe.matmul(proj_bank[1][:, :], wk[:, :], ctx_cols[:, :], start=True, stop=True).then_inc(k_projected, 1)
            project_v(0)
            turn_weights()
            pe.wait_ge(weights_kept, 4)

            def sequence(b, u, i, late, last_one, first=False):
                nxt = (b + 1, 1 - u, i + u)
                score(b, u, 0, late)
                score(b, u, 1, late)
                if not last_one:
                    turn_ctx(*nxt, True)
                turn_p(b, 0, late)
                score(b, u, 2, late)
                if not last_one:
                    project_k(b + 1)
                turn_p(b, 1, late)
                score(b, u, 3, late)
                if late or u:
                    attend(b - 1, 1 - u, late and not first)
                turn_p(b, 2, late)
                if not last_one:
                    project_v(b + 1)
                turn_p(b, 3, late)

            sequence(0, 0, 0, False, False)
            sequence(1, 1, 0, True, False, first=True)
            with pe.Fori(1, PAIRS - 1) as i:
                for u in range(2):
                    sequence(2 * i + u, u, i, True, False)
            sequence(B - 2, 0, PAIRS - 1, True, False)
            sequence(B - 1, 1, PAIRS - 1, True, True)
            attend(B - 1, 1, True)

            pe.wait_ge(heads_ready, B + 1)
            for t in range(TT):
                last = pe.matmul(bank[0][:, t * P:(t + 1) * P], heads_cols[:, t * P:(t + 1) * P], wo[:, :],
                                 start=True, stop=True)
            last.then_inc(attn_out, 1)

            turn_norm(1)
            pe.wait_ge(ln_cols, 2)
            for c in range(2 * NH):
                pe.matmul(bank[2 + c][:, :], w_in[:, c, :], norm_cols[:, :], start=True, stop=True).then_inc(xz_done, 1)
            for d in range(DIRS):
                pe.wait_ge(u_ready, NH * (d + 1))
                for h in range(NH):
                    last = pe.matmul(bank[6 + d][0:R, :], wx_dt[:, d, h, :], u_cols[:, d, h, :],
                                     start=(h == 0), stop=(h == NH - 1))
                last.then_inc(xdbl_done, 1)
                for h in range(NH):
                    last = pe.matmul(bank[d][:, :], wx_bc[:, d, h, :, :], u_cols[:, d, h, :],
                                     start=(h == 0), stop=(h == NH - 1))
                last.then_inc(xdbl_done, 1)
                pe.wait_ge(dt_low_kept, d + 1)
                for h in range(NH):
                    if d == 0:
                        pe.wait_ge(x_padded, h + 1)
                    else:
                        pe.wait_ge(z_ready, h + 1)
                    pe.matmul(bank[2 + d * NH + h][:, :], wdt[:, d, h, :], dt_low[:, d, :],
                              start=True, stop=True).then_inc(dt_raw, 1)

            pe.wait_ge(skip_ready, 1)
            for h in range(NH):
                pe.matmul(bank[6 + h][:, :], ident[:, :], skip[:, h, :], start=True, stop=False)

            def spread(d, n, k, u, late):
                if late:
                    pe.wait_ge(fed, k - 1)
                pe.matmul(bank[u][:, :], pick_bc[:, bass.ds(n, 1), :].rearrange("p o m -> p (o m)"),
                          bc_parts[d][:, :], start=True, stop=True).then_inc(b_spread, 1)
                if late:
                    pe.wait_ge(was_read, k - 1)
                pe.matmul(bank[2 + u][:, :], pick_bc[:, bass.ds(n + N, 1), :].rearrange("p o m -> p (o m)"),
                          bc_parts[d][:, :], start=True, stop=True).then_inc(c_spread, 1)

            def add_up(k, u, stop):
                pe.wait_ge(was_read, k + 1)
                for h in range(NH):
                    last = pe.matmul(bank[6 + h][:, :], ident[:, :], read[u][:, h * T:(h + 1) * T],
                                     start=False, stop=stop)
                last.then_inc(summed, 1)

            pe.wait_ge(bc_split, DIRS)
            pe.wait_ge(pos_ready, DIRS * NH)
            pe.wait_ge(sp_ready, DIRS * NH)
            pe.wait_ge(picks_spread, 2)
            for u in range(2):
                spread(0, u, u, u, False)
            with pe.Fori(0, NP - 1) as i:
                for u in range(2):
                    spread(0, 2 * i + 2 + u, 2 * i + 2 + u, u, True)
                    add_up(2 * i + u, u, False)
            for u in range(2):
                spread(1, u, N + u, u, True)
                add_up(N - 2 + u, u, False)
            with pe.Fori(0, NP - 1) as i:
                for u in range(2):
                    spread(1, 2 * i + 2 + u, N + 2 * i + 2 + u, u, True)
                    add_up(N + 2 * i + u, u, False)
            for u in range(2):
                add_up(2 * N - 2 + u, u, u == 1)
            pe.wait_ge(gated_ready, 1)
            for t in range(TT):
                for h in range(NH):
                    last = pe.matmul(bank[4][:, t * P:(t + 1) * P], gated[:, h, t * P:(t + 1) * P], w_out[:, h, :],
                                     start=(h == 0), stop=(h == NH - 1))
            last.then_inc(mamba_out, 1)

            turn_norm(2)
            pe.wait_ge(ln_cols, 3)
            pe.wait_ge(x2_ready, 1)
            for t in range(TT):
                last = pe.matmul(bank[4][:, t * E:(t + 1) * E], norm_cols[:, t * P:(t + 1) * P], gate_w[:, :],
                                 start=True, stop=True)
            last.then_inc(gate_done, 1)
            pe.wait_ge(ffn_w_in, 16 * (FFN_LOADS - 2))

            def hidden_in(j):
                if j >= 2:
                    pe.wait_ge(h_act, j - 1)
                    pe.wait_ge(h_mixed, j - 1)
                win = e_win[:, 2 * j:2 * j + 2, :] if j < EP else ws_in[:, :]
                vin = e_vin[:, 2 * j:2 * j + 2, :] if j < EP else vs_in[:, :]
                pe.matmul(bank[j % 2][:, :], win, norm_cols[:, :], start=True, stop=True)
                pe.matmul(bank[2 + j % 2][:, :], vin, norm_cols[:, :], start=True, stop=True).then_inc(h_done, 1)

            def spread_combine(j):
                if j >= 2:
                    pe.wait_ge(h_ready, j - 1)
                pe.matmul(bank[6 + j % 2][:, :], pick_ex[:, 2 * j:2 * j + 2, :], comb_parts[:, :],
                          start=True, stop=True).then_inc(comb_spread, 1)

            def hidden_out(j, first, stop):
                pe.wait_ge(h_ready, j + 1)
                w = e_wout[:, j, :] if j < EP else ws_out[:, :]
                for t in range(TT):
                    last = pe.matmul(bank[5][:, t * P:(t + 1) * P], hidden[j % 2][:, t * P:(t + 1) * P], w,
                                     start=(first and t == 0), stop=stop, skip_group_check=True)
                last.then_inc(h_used, 1)

            hidden_in(0)
            hidden_in(1)
            pe.wait_ge(combine_ready, 1)
            for t in range(TT):
                last = pe.transpose(bank[4][0:E, t * P:(t + 1) * P], combine[:, t, :], ident[:, :])
            last.then_inc(combine_turned, 1)
            pe.wait_ge(comb_split, 1)
            for j in range(EP + 1):
                if j < EP:
                    spread_combine(j)
                if j >= 1:
                    hidden_out(j - 1, j == 1, False)
                if j + 2 <= EP:
                    hidden_in(j + 2)
            hidden_out(EP, False, True)

        @block.scalar
        def _(act):
            act.dma_start(bq[:, :], column(a["L0_xattn_wq_b"])).then_inc(attn_w_in, 16)
            act.dma_start(bk[:, :], column(a["L0_xattn_wk_b"])).then_inc(attn_w_in, 16)
            act.dma_start(bv[:, :], a["L0_xattn_wv_b"].partition_broadcast(P)).then_inc(attn_w_in, 16)
            act.dma_start(bo[:, :], a["L0_xattn_wo_b"].partition_broadcast(P)).then_inc(attn_w_in, 16)
            for g in range(HG):
                act.dma_start(mask_in[g * S:(g + 1) * S, :],
                              a["mask_1x1xSxS2_fk1"].rearrange("a b s k -> (a b s) k")).then_inc(mask_loaded, 16)
            nc.scalar.preload_act_table_set("natural_log_exp_and_others")

            def inv_std(n):
                act.wait_ge(ln_moments, n + 1)
                act.activation(ln_var[:, :], moments[:, :, 1], ACT.Ln, bias=EPS).then_inc(act_step, 1)
                act.wait_ge(act_step, n + 1)
                act.activation(rstd[:, :], ln_var[:, :], ACT.Exp, scale=-0.5).then_inc(ln_rstd, 1)

            def keep_ctx(b, late):
                act.wait_ge(ctx_turned, b + 1)
                if late:
                    act.wait_ge(v_projected, b)
                act.copy(ctx_cols[:, :], proj_bank[0][:, :]).then_inc(ctx_kept, 1)

            def keep_k(b, u, late):
                act.wait_ge(k_projected, b + 1)
                if late:
                    act.wait_ge(scores_done, G * (b - 1))
                act.activation(k_cols[u][:, :], proj_bank[1][:, :], ACT.Identity, bias=bk[:, 0:1]).then_inc(k_ready, 1)

            def exponentials(b, u, g, late):
                act.wait_ge(masked_ready, G * b + g + 1)
                if late or g >= 2:
                    act.wait_ge(p_turned, G * b + g - 1)
                if late and g == 0:
                    act.wait_ge(inv_ready, b - 1)
                act.activation(probs[g % 2][:, :], masked[g % 2][:, :], ACT.Exp, bias=neg_max[u][:, g:g + 1],
                               scale=-1.0, accum_out=row_sum[u][:, g:g + 1]).then_inc(probs_ready, 1)

            def keep_pt(b, u, g, late):
                act.wait_ge(p_turned, G * b + g + 1)
                if late and g == 0:
                    act.wait_ge(attended, b - 1)
                act.copy(probs_t[u][:, g, :, :], turn_bank[0][:, :].rearrange("p (c m) -> p c m", c=KC)).then_inc(pt_even, 1)

            keep_ctx(0, False)
            inv_std(0)
            act.wait_ge(attn_w_in, 16 * ATTN_LOADS)
            keep_k(0, 0, False)
            act.wait_ge(weights_turned, 1)
            act.copy(w_in[:, :, :], bank[6][:, :].rearrange("p (c m) -> p c m", m=P)).then_inc(weights_kept, 1)
            act.wait_ge(weights_turned, 2)
            W = R + 2 * N
            turned = bank[7][:, 0:DIRS * NH * W].rearrange("p (d h w) -> p d h w", d=DIRS, h=NH)
            act.copy(wx_dt[:, :, :, :], turned[:, :, :, 0:R]).then_inc(act_step, 1)
            for d in range(DIRS):
                for h in range(NH):
                    last = act.copy(wx_bc[:, d, h, :, :], turned[:, d, h, R:W].unsqueeze(1).to_broadcast([P, 4, 2 * N]))
            last.then_inc(weights_kept, 1)
            act.wait_ge(weights_turned, 3)
            act.copy(w_out[:, :, :], bank[2][:, 0:NH * P].rearrange("p (h m) -> p h m", h=NH)).then_inc(act_step, 1)
            act.copy(gate_w[:, :], bank[2][:, NH * P:NH * P + E]).then_inc(weights_kept, 1)
            act.wait_ge(weights_turned, 4)
            act.copy(wdt[:, :, :, :], bank[3][0:R, :].rearrange("p (d h m) -> p d h m", d=DIRS, h=NH)).then_inc(weights_kept, 1)
            act.wait_ge(mamba_w_in, 16 * MAMBA_LOADS)
            act.activation(a_exp[:, :, :, :], a_log[:, :, :, :], ACT.Exp).then_inc(act_step, 1)
            act.wait_ge(act_step, 4)
            act.mul(a_neg[:, :, :, :], a_exp[:, :, :, :], -1.0).then_inc(a_ready, 1)

            def sequence(b, u, late, last_one):
                exponentials(b, u, 0, late)
                if not last_one:
                    keep_ctx(b + 1, True)
                exponentials(b, u, 1, late)
                keep_pt(b, u, 0, late)
                exponentials(b, u, 2, late)
                if not last_one:
                    keep_k(b + 1, 1 - u, late or u == 1)
                exponentials(b, u, 3, late)
                keep_pt(b, u, 2, late)

            sequence(0, 0, False, False)
            def second():
                for g in range(G):
                    act.wait_ge(masked_ready, G + g + 1)
                    act.wait_ge(p_turned, G + g - 1)
                    act.activation(probs[g % 2][:, :], masked[g % 2][:, :], ACT.Exp, bias=neg_max[1][:, g:g + 1],
                                   scale=-1.0, accum_out=row_sum[1][:, g:g + 1]).then_inc(probs_ready, 1)
                    if g == 0:
                        keep_ctx(2, True)
                    if g == 1:
                        keep_pt(1, 1, 0, False)
                    if g == 2:
                        keep_k(2, 0, True)
                keep_pt(1, 1, 2, False)
            second()
            with act.Fori(1, PAIRS - 1) as i:
                for u in range(2):
                    sequence(2 * i + u, u, True, False)
            sequence(B - 2, 0, True, False)
            sequence(B - 1, 1, True, True)

            act.wait_ge(consts_built, 1)
            act.copy(pick_bc[:, :, :], pick[:, :].unsqueeze(2).to_broadcast([P, 2 * N, P])).then_inc(picks_spread, 1)
            act.copy(pick_ex[:, :, :], pick[:, 0:E].unsqueeze(2).to_broadcast([P, E, HE])).then_inc(picks_spread, 1)

            inv_std_steps = 5
            act.wait_ge(ln_moments, 2)
            act.activation(ln_var[:, :], moments[:, :, 1], ACT.Ln, bias=EPS).then_inc(act_step, 1)
            act.wait_ge(act_step, inv_std_steps)
            act.activation(rstd[:, :], ln_var[:, :], ACT.Exp, scale=-0.5).then_inc(ln_rstd, 1)
            act.wait_ge(pads_cleared, 1 + 2 * DIRS)
            for h in range(NH):
                act.wait_ge(xz_done, h + 1)
                act.copy(x_pad[:, h, :, PAD:PAD + S], bank[2 + h][:, :].rearrange("p (b s) -> p b s", s=S)).then_inc(x_padded, 1)
            for h in range(NH):
                act.wait_ge(xz_done, NH + h + 1)
                act.activation(z_act[:, h, :], bank[2 + NH + h][:, :], ACT.Silu).then_inc(z_ready, 1)
            for d in range(DIRS):
                for h in range(NH):
                    act.wait_ge(conv_done, d * NH + h + 1)
                    act.activation(u_cols[:, d, h, :], conv[:, d, h, :], ACT.Silu).then_inc(u_ready, 1)
                act.wait_ge(xdbl_done, 2 * d + 1)
                act.copy(dt_low[:, d, :], bank[6 + d][0:R, :]).then_inc(dt_low_kept, 1)
            for d in range(DIRS):
                for h in range(NH):
                    act.wait_ge(dt_raw, d * NH + h + 1)
                    act.activation(sp_abs[:, d, h, :], bank[2 + d * NH + h][:, :], ACT.Abs,
                                   bias=bdt[:, d, h:h + 1]).then_inc(sp_ready, 1)
            for d in range(DIRS):
                for h in range(NH):
                    act.wait_ge(sp_ready, DIRS * NH)
                    act.activation(sp_exp[:, d, h, :], sp_abs[:, d, h, :], ACT.Exp, scale=-1.0).then_inc(sp_ready, 1)
            for d in range(DIRS):
                for h in range(NH):
                    act.wait_ge(sp_ready, DIRS * NH + d * NH + h + 1)
                    act.activation(sp_ln[:, d, h, :], sp_exp[:, d, h, :], ACT.Ln, bias=1.0).then_inc(sp_ready, 1)

            def decays(d, n, k, u, late):
                if late:
                    act.wait_ge(scanned, k - 1)
                for h in range(NH):
                    steps = slice(1, S) if d == 0 else slice(0, S - 1)
                    src = dt_cols[:, d, h, :].rearrange("p (b s) -> p b s", s=S)[:, :, steps]
                    dst = decay[d][u][:, h * T:(h + 1) * T].rearrange("p (b s) -> p b s", s=S)[:, :, steps]
                    act.activation(dst, src, ACT.Exp, scale=a_neg[:, d, h, bass.ds(n, 1)]).then_inc(decayed, 1)

            act.wait_ge(a_ready, 1)
            for d in range(DIRS):
                act.wait_ge(dt_ready, d + 1)
                for u in range(2):
                    decays(d, u, N * d + u, u, d == 1)
                with act.Fori(1, NP) as i:
                    for u in range(2):
                        decays(d, 2 * i + u, N * d + 2 * i + u, u, True)

            act.wait_ge(ln_moments, 3)
            act.activation(ln_var[:, :], moments[:, :, 1], ACT.Ln, bias=EPS).then_inc(act_step, 1)
            act.wait_ge(act_step, inv_std_steps + 1)
            act.activation(rstd[:, :], ln_var[:, :], ACT.Exp, scale=-0.5).then_inc(ln_rstd, 1)
            act.wait_ge(gate_done, 1)
            act.activation(gates[:, :, :], bank[4][:, 0:TT * E].rearrange("p (t e) -> p t e", e=E),
                           ACT.Sigmoid).then_inc(gates_ready, 1)
            for j in range(EP + 1):
                act.wait_ge(h_done, j + 1)
                if j >= 2:
                    act.wait_ge(h_mixed, j - 1)
                act.activation(act_in[j % 2][:, :], bank[j % 2][:, :], ACT.Silu).then_inc(h_act, 1)

        @block.vector
        def _(dve):
            steps = [0]

            def link(ins):
                steps[0] += 1
                ins.then_inc(dve_step, 1)
                dve.wait_ge(dve_step, steps[0])

            def layer_norm(n, rows):
                if n:
                    dve.wait_ge(ln_turned, n)
                for t in range(TT):
                    last = dve.bn_stats(stats[:, t, :], rows[:, t, :])
                link(last)
                for t in range(TT):
                    last = dve.bn_aggr(moments[:, t, :], stats[:, t, :])
                last.then_inc(ln_moments, 1)
                dve.wait_ge(ln_moments, n + 1)
                link(dve.tensor_scalar(newton[:, 0, :], moments[:, :, 1], EPS, None, ALU.add))
                dve.wait_ge(ln_rstd, n + 1)
                link(dve.tensor_tensor(newton[:, 1, :], rstd[:, :], rstd[:, :], ALU.mult))
                link(dve.tensor_tensor(newton[:, 1, :], newton[:, 1, :], newton[:, 0, :], ALU.mult))
                link(dve.tensor_scalar(newton[:, 1, :], newton[:, 1, :], -0.5, 1.5, ALU.mult, ALU.add))
                link(dve.tensor_tensor(newton[:, 2, :], newton[:, 1, :], rstd[:, :], ALU.mult))
                for t in range(TT):
                    last = dve.tensor_scalar(norm_rows[:, t, :], rows[:, t, :], moments[:, t, 0:1],
                                             newton[:, 2, t:t + 1], ALU.subtract, ALU.mult)
                last.then_inc(ln_rows, 1)
                dve.wait_ge(ln_turned, n + 1)
                dve.tensor_copy(norm_cols[:, :], bank[(2, 1, 5)[n]][:, :]).then_inc(ln_cols, 1)

            def mask_scores(b, u, g, late):
                dve.wait_ge(scores_done, G * b + g + 1)
                if late or g >= 2:
                    dve.wait_ge(probs_ready, G * b + g - 1)
                dve.memset(turnstile[g][:, :], 0.0)
                dve.tensor_tensor_reduce(masked[g % 2][:, :].rearrange("p (c m) -> p c m", c=KC),
                                         score_bank[g % 2][:, :].rearrange("p (c m) -> p c m", c=KC),
                                         mask_neg[:, :, :], -1.0, 3.0e38, ALU.add, ALU.min,
                                         neg_max[u][:, g:g + 1]).then_inc(masked_ready, 1)

            def keep_v(b, u, late):
                dve.wait_ge(v_projected, b + 1)
                if late:
                    dve.wait_ge(attended, b - 1)
                dve.tensor_tensor(v_rows[u][:, :, :], proj_bank[0][:, :].rearrange("p (c d) -> p c d", c=KC),
                                  bv[:, :].unsqueeze(1).to_broadcast([P, KC, D]), ALU.add).then_inc(v_ready, 1)

            def keep_pt(b, u, g, late):
                dve.wait_ge(p_turned, G * b + g + 1)
                if late and g == 1:
                    dve.wait_ge(attended, b - 1)
                dve.tensor_copy(probs_t[u][:, g, :, :], turn_bank[1][:, :].rearrange("p (c m) -> p c m", c=KC)).then_inc(pt_odd, 1)

            def invert_sums(b, u, late):
                dve.wait_ge(probs_ready, G * b + G)
                if late:
                    dve.wait_ge(attended, b - 1)
                dve.reciprocal(row_inv[u][:, :], row_sum[u][:, :]).then_inc(own_step, 1)

            def spread_sums(b, u):
                dve.wait_ge(own_step, 3 * b + 1)
                dve.tensor_copy(row_inv_wide[u][:, :, :],
                                row_inv[u][:, :].unsqueeze(2).to_broadcast([P, G, S])).then_inc(inv_ready, 1)

            def own_heads(b, u):
                dve.wait_ge(attended, b + 1)
                at = lambda lo: out_bank[u][:, lo:lo + P].rearrange("p (h s) -> p h s", h=HG)
                dve.tensor_tensor(own_inv[:, :, :], at(P),
                                  groupmask[:, :].unsqueeze(2).to_broadcast([P, HG, S]), ALU.mult).then_inc(own_step, 1)
                dve.wait_ge(own_step, 3 * b + 2)
                dve.tensor_tensor(own_out[:, :, :], at(0), own_inv[:, :, :], ALU.mult).then_inc(own_step, 1)
                dve.wait_ge(own_step, 3 * b + 3)
                dve.tensor_reduce(heads_cols[:, bass.ds(b * S, S)], own_out[:, :, :].rearrange("p h s -> p s h"),
                                  AX.X, ALU.add).then_inc(heads_ready, 1)

            dve.wait_ge(x_in, 16)
            layer_norm(0, x_rows)
            dve.wait_ge(q_projected, 1)
            dve.wait_ge(attn_w_in, 16 * ATTN_LOADS)
            dve.tensor_scalar(q_cols[:, :], bank[3][:, :], bq[:, 0:1], SCALE, ALU.add, ALU.mult).then_inc(q_ready, 1)
            dve.wait_ge(consts_built, 1)
            dve.tensor_reduce(groupmask[:, :], headmask[:, :].rearrange("p (g h) -> p h g", g=G), AX.X,
                              ALU.add).then_inc(heads_ready, 1)
            dve.wait_ge(heads_ready, 1)
            dve.wait_ge(mask_loaded, 16 * HG)
            dve.tensor_scalar(mask_neg[:, :, :], mask_in[:, :].rearrange("p (m c) -> p c m", c=KC),
                              NEG_BIG, None, ALU.mult).then_inc(mask_scaled, 1)
            keep_v(0, 0, False)
            dve.wait_ge(mask_scaled, 1)

            def sequence(b, u, late, last_one, first=False):
                mask_scores(b, u, 0, late)
                mask_scores(b, u, 1, late)
                mask_scores(b, u, 2, late)
                keep_pt(b, u, 1, late and not first)
                mask_scores(b, u, 3, late)
                if late or u:
                    own_heads(b - 1, 1 - u)
                if not last_one:
                    keep_v(b + 1, 1 - u, late)
                keep_pt(b, u, 3, late)
                invert_sums(b, u, late and not first)
                spread_sums(b, u)

            sequence(0, 0, False, False)
            sequence(1, 1, True, False, first=True)
            with dve.Fori(1, PAIRS - 1) as i:
                for u in range(2):
                    sequence(2 * i + u, u, True, False)
            sequence(B - 2, 0, True, False)
            sequence(B - 1, 1, True, True)
            own_heads(B - 1, 1)
            dve.wait_ge(attn_out, 1)
            dve.wait_ge(bo_added, 1)
            link(dve.tensor_tensor(x1_rows[:, :, :], bank[0][:, :].rearrange("p (t d) -> p t d", t=TT),
                                   xb_rows[:, :, :], ALU.add))

            layer_norm(1, x1_rows)
            for d in range(DIRS):
                for h in range(NH):
                    dve.wait_ge(x_padded, h + 1)
                    acc = conv[:, d, h, :].rearrange("p (b s) -> p b s", s=S)
                    w = lambda j: conv_w[:, d, h, j:j + 1]
                    link(dve.tensor_scalar(acc, x_pad[:, h, :, PAD:PAD + S], w(PAD), conv_b[:, d, h:h + 1],
                                           ALU.mult, ALU.add))
                    for back in range(1, TAPS):
                        at = PAD - back if d == 0 else PAD + back
                        ins = dve.scalar_tensor_tensor(acc, x_pad[:, h, :, at:at + S], w(PAD - back), acc,
                                                       ALU.mult, ALU.add)
                        if back < TAPS - 1:
                            link(ins)
                    ins.then_inc(conv_done, 1)
            dve.wait_ge(u_ready, DIRS * NH)
            for h in range(NH):
                link(dve.tensor_scalar(skip[:, h, :], u_cols[:, 0, h, :], d_skip[:, 0, h:h + 1], None, ALU.mult))
                link(dve.scalar_tensor_tensor(skip[:, h, :], u_cols[:, 1, h, :], d_skip[:, 1, h:h + 1],
                                              skip[:, h, :], ALU.mult, ALU.add))
            dve.tensor_copy(stats[:, 0, 0:1], skip[:, 0, 0:1]).then_inc(skip_ready, 1)
            for d in range(DIRS):
                dve.wait_ge(xdbl_done, 2 * d + 2)
                link(dve.tensor_copy(bc_parts[d][:, :], bank[d][:, :]))
                link(dve.tensor_tensor(bc_rest[:, d, :], bank[d][:, :], bc_parts[d][:, :], ALU.subtract))
                link(dve.tensor_copy(bc_mid[:, d, :], bc_rest[:, d, :]))
                link(dve.tensor_tensor(bc_low[:, d, :], bc_rest[:, d, :], bc_mid[:, d, :], ALU.subtract))
                dve.tensor_copy(bc_parts[d][32:64, :], bc_mid[32:64, d, :])
                dve.tensor_copy(bc_parts[d][64:96, :], bc_low[64:96, d, :]).then_inc(bc_split, 1)
            for d in range(DIRS):
                for h in range(NH):
                    dve.wait_ge(dt_raw, d * NH + h + 1)
                    dve.wait_ge(sp_ready, d * NH + h + 1)
                    dve.tensor_scalar(sp_pos[:, d, h, :], bank[2 + d * NH + h][:, :], bdt[:, d, h:h + 1], 0.0,
                                      ALU.add, ALU.max).then_inc(pos_ready, 1)
            for d in range(DIRS):
                dve.wait_ge(sp_ready, DIRS * NH + (d + 1) * NH)
                link(dve.tensor_scalar(dt_cols[:, d, :, :], sp_exp[:, d, :, :], 1.0, -1.0, ALU.add, ALU.add))
                link(dve.tensor_tensor(dt_cols[:, d, :, :], sp_exp[:, d, :, :], dt_cols[:, d, :, :], ALU.subtract))
                dve.wait_ge(sp_ready, 2 * DIRS * NH + (d + 1) * NH)
                link(dve.tensor_tensor(dt_cols[:, d, :, :], dt_cols[:, d, :, :], sp_ln[:, d, :, :], ALU.add))
                dve.wait_ge(pos_ready, DIRS * NH)
                dve.tensor_tensor(dt_cols[:, d, :, :], dt_cols[:, d, :, :], sp_pos[:, d, :, :], ALU.add).then_inc(dt_ready, 1)
                dve.wait_ge(dt_ready, d + 1)
                link(dve.tensor_tensor(dtu[:, d, :, :], dt_cols[:, d, :, :], u_cols[:, d, :, :], ALU.mult))

            both = lambda t: t.rearrange("p (h t) -> p h t", h=NH)
            ends = lambda t, d: t[:, :] if d == 0 else t[:, ::-1]

            def feed_states(d, k, u, late):
                dve.wait_ge(b_spread, k + 1)
                if late:
                    dve.wait_ge(scanned, k - 1)
                dve.tensor_tensor(both(feed[u][:, :]), dtu[:, d, :, :],
                                  bank[u][:, :].unsqueeze(1).to_broadcast([P, NH, T]), ALU.mult).then_inc(fed, 1)

            def scan(d, k, u, late):
                dve.wait_ge(decayed, NH * (k + 1))
                dve.wait_ge(fed, k + 1)
                if late:
                    dve.wait_ge(was_read, k - 1)
                dve.tensor_tensor_scan(ends(state[u], d), ends(decay[d][u], d), ends(feed[u], d), 0.0,
                                       ALU.mult, ALU.add).then_inc(scanned, 1)

            def read_states(d, k, u, late):
                dve.wait_ge(c_spread, k + 1)
                dve.wait_ge(scanned, k + 1)
                if late:
                    dve.wait_ge(summed, k - 1)
                dve.tensor_tensor(both(read[u][:, :]), both(state[u][:, :]),
                                  bank[2 + u][:, :].unsqueeze(1).to_broadcast([P, NH, T]), ALU.mult).then_inc(was_read, 1)

            def pair(d, k, late):
                for u in range(2):
                    feed_states(d, k + u, u, late)
                for u in range(2):
                    scan(d, k + u, u, late)
                for u in range(2):
                    read_states(d, k + u, u, late)

            for d in range(DIRS):
                pair(d, N * d, d == 1)
                with dve.Fori(1, NP) as i:
                    pair(d, N * d + 2 * i, True)
            dve.wait_ge(summed, 2 * N)
            dve.wait_ge(z_ready, NH)
            for h in range(NH):
                last = dve.tensor_tensor(gated[:, h, :], bank[6 + h][:, :], z_act[:, h, :], ALU.mult)
            last.then_inc(gated_ready, 1)
            dve.wait_ge(mamba_out, 1)
            dve.scalar_tensor_tensor(x2_rows[:, :, :], bank[4][:, :].rearrange("p (t d) -> p t d", t=TT), 0.5,
                                     x1_rows[:, :, :], ALU.mult, ALU.add).then_inc(x2_ready, 1)
            dve.wait_ge(x2_ready, 1)

            layer_norm(2, x2_rows)
            dve.wait_ge(gates_ready, 1)
            for t in range(TT):
                mine = gates[:, t, :].unsqueeze(2).to_broadcast([P, E, E])
                other = gates[:, t, :].unsqueeze(1).to_broadcast([P, E, E])
                dve.tensor_tensor(beats[:, t, :, :], other, mine, ALU.is_gt)
                last = dve.tensor_tensor(ties[:, t, :, :], other, mine, ALU.is_equal)
            link(last)
            link(dve.tensor_tensor(ties[:, :, :, :], ties[:, :, :, :],
                                   earlier[:, :, :].unsqueeze(1).to_broadcast([P, TT, E, E]), ALU.mult))
            link(dve.tensor_tensor(beats[:, :, :, :], beats[:, :, :, :], ties[:, :, :, :], ALU.add))
            link(dve.tensor_reduce(rank[:, :, :], beats[:, :, :, :], AX.X, ALU.add))
            link(dve.scalar_tensor_tensor(kept[:, :, :], rank[:, :, :], float(TOPK), gates[:, :, :], ALU.is_lt, ALU.mult))
            link(dve.tensor_reduce(kept_sum[:, :], kept[:, :, :], AX.X, ALU.add))
            link(dve.reciprocal(kept_inv[:, :], kept_sum[:, :]))
            dve.tensor_tensor(combine[:, :, :], kept[:, :, :],
                              kept_inv[:, :].unsqueeze(2).to_broadcast([P, TT, E]), ALU.mult).then_inc(combine_ready, 1)
            link(dve.memset(comb_parts[:, :], 0.0))
            dve.wait_ge(combine_turned, 1)
            link(dve.tensor_copy(comb_cols, bank[4][0:E, :]))
            link(dve.tensor_copy(comb_hi, comb_cols))
            link(dve.tensor_tensor(comb_rest[:, 0, :], comb_cols, comb_hi, ALU.subtract))
            link(dve.tensor_copy(comb_mid, comb_rest[:, 0, :]))
            link(dve.tensor_tensor(comb_rest[:, 1, :], comb_rest[:, 0, :], comb_mid, ALU.subtract))
            dve.tensor_copy(comb_parts[0:E, :], comb_hi)
            dve.tensor_copy(comb_parts[32:32 + E, :], comb_mid)
            dve.tensor_copy(comb_parts[64:64 + E, :], comb_rest[:, 1, :]).then_inc(comb_split, 1)
            for j in range(EP + 1):
                dve.wait_ge(h_act, j + 1)
                if j >= 2:
                    dve.wait_ge(h_used, j - 1)
                to = mixed if j < EP else hidden
                ins = dve.tensor_tensor(to[j % 2][:, :], bank[2 + j % 2][:, :], act_in[j % 2][:, :], ALU.mult)
                if j < EP:
                    ins.then_inc(h_mixed, 1)
                    dve.wait_ge(h_mixed, j + 1)
                    dve.wait_ge(comb_spread, j + 1)
                    dve.tensor_tensor(hidden[j % 2][:, :], bank[6 + j % 2][:, :], mixed[j % 2][:, :],
                                      ALU.mult).then_inc(h_ready, 1)
                else:
                    ins.then_inc(h_ready, 1)
            dve.wait_ge(h_used, EP + 1)
            dve.tensor_tensor(y_rows[:, :, :], bank[5][:, :].rearrange("p (t d) -> p t d", t=TT), x2_rows[:, :, :],
                              ALU.add).then_inc(y_ready, 1)


_INS = ['x', 'ctx_1024', 'mask_1x1xSxS2_fk1', 'L0_xattn_wq_w', 'L0_xattn_wq_b', 'L0_xattn_wk_w', 'L0_xattn_wk_b',
        'L0_xattn_wv_w', 'L0_xattn_wv_b', 'L0_xattn_wo_w', 'L0_xattn_wo_b', 'L0_attn_W_in', 'L0_attn_conv_w',
        'L0_attn_conv_b', 'L0_attn_Wx', 'L0_attn_Wdt', 'L0_attn_bdt', 'L0_attn_A_log', 'L0_attn_D',
        'L0_attn_conv_w_b', 'L0_attn_conv_b_b', 'L0_attn_Wx_b', 'L0_attn_Wdt_b', 'L0_attn_bdt_b',
        'L0_attn_A_b_log', 'L0_attn_D_b', 'L0_attn_W_out', 'L0_ffn_gate_w', 'L0_ffn_ws_in', 'L0_ffn_vs_in',
        'L0_ffn_ws_out', 'L0_ffn_e_win', 'L0_ffn_e_vin', 'L0_ffn_e_wout']


def kernel(**inputs):
    import numpy as _np
    import concourse.bacc as _bacc
    from concourse import mybir as _mybir
    from concourse.bass_utils import run_bass_kernel_spmd as _run

    nc = _bacc.Bacc("TRN2", target_bir_lowering=False, num_devices=1)
    arrays, args = {}, {}
    for name in _INS:
        v = _np.ascontiguousarray(inputs[name])
        arrays[f"in_{name}_dram"] = v
        args[name] = nc.dram_tensor(f"in_{name}_dram", v.shape, _mybir.dt.from_np(v.dtype), kind="ExternalInput").ap()
    out = nc.dram_tensor("out_0_dram", (16, 32, 128), _mybir.dt.float32, kind="ExternalOutput").ap()
    perceiver_block(nc, args, out)
    r = _run(nc, [arrays], core_ids=[0])
    return r.results[0]["out_0_dram"]
```

```python
from contextlib import ExitStack

import concourse.bass as bass
from concourse import mybir

F32 = mybir.dt.float32
F32R = mybir.dt.float32r
BF16 = mybir.dt.bfloat16
ALU = mybir.AluOpType
ACT = mybir.ActivationFunctionType
AX = mybir.AxisListType

P = 128
EPS = 1e-5
NEG_BIG = -1e9


def perceiver_block(nc: bass.Bass, a: dict, out: bass.AP):
    B, S, D = a["x"].shape
    K = a["ctx_1024"].shape[1]
    T = B * S
    TT = T // P
    H = 16
    DH = D // H
    G = 4
    HG = H // G
    KC = K // P
    DI = a["L0_attn_W_in"].shape[0] // 2
    NH = DI // P
    N = a["L0_attn_A_log"].shape[1]
    R = a["L0_attn_Wdt"].shape[1]
    TAPS = a["L0_attn_conv_w"].shape[2]
    PAD = TAPS - 1
    E, _, HE = a["L0_ffn_e_win"].shape
    TOPK = 4
    EP = E * HE // P
    SCALE = float(DH) ** -0.5
    PAIRS = B // 2
    NP = N // 2
    DIRS = 2
    assert T == 512 and D == P and HG * S == P and K == 512 and 2 * N == 32

    with ExitStack() as ctx:
        def sb(name, shape, dt=F32):
            return ctx.enter_context(nc.sbuf_tensor(name, shape, dt))

        def sem(name):
            return ctx.enter_context(nc.semaphore(name))

        duo = [ctx.enter_context(nc.psum_tensor(f"duo{i}", [P, 2, 512], F32)) for i in range(4)]
        bank = [duo[i // 2][:, i % 2, :] for i in range(8)]

        ident = sb("ident", [P, P])
        headmask = sb("headmask", [P, H])
        groupmask = sb("groupmask", [P, HG])
        pick = sb("pick", [P, 32])
        pick_bc = sb("pick_bc", [P, 2 * N, P], BF16)
        pick_ex = sb("pick_ex", [P, E, HE], BF16)
        mixmask = sb("mixmask", [P, H // 2])
        earlier = sb("earlier", [P, E, E])

        wq = sb("wq", [P, D])
        wk = sb("wk", [P, D])
        wv = sb("wv", [P, D])
        wo = sb("wo", [P, D])
        bq = sb("bq", [P, 1])
        bk = sb("bk", [P, 1])
        bv = sb("bv", [P, 1])
        bo = sb("bo", [P, D])
        mask_in = sb("mask_in", [P, K])
        mask_neg = sb("mask_neg", [P, KC, P])
        w_in_rows = sb("w_in_rows", [P, 2 * NH, D])
        w_in = sb("w_in", [P, 2 * NH, P])
        wx_rows = sb("wx_rows", [R + 2 * N, DIRS, DI])
        wx_dt = sb("wx_dt", [P, DIRS, NH, R])
        wx_bc = sb("wx_bc", [P, DIRS, NH, 4, 2 * N])
        wdt_rows = sb("wdt_rows", [P, DIRS, NH, R])
        wdt = sb("wdt", [R, DIRS, NH, P])
        w_out_rows = sb("w_out_rows", [P, DI])
        w_out = sb("w_out", [P, NH, P])
        conv_w = sb("conv_w", [P, DIRS, NH, TAPS])
        conv_b = sb("conv_b", [P, DIRS, NH])
        bdt = sb("bdt", [P, DIRS, NH])
        a_log = sb("a_log", [P, DIRS, NH, N])
        a_exp = sb("a_exp", [P, DIRS, NH, N])
        a_neg = sb("a_neg", [P, DIRS, NH, N])
        d_skip = sb("d_skip", [P, DIRS, NH])
        gate_rows = sb("gate_rows", [E, D])
        gate_w = sb("gate_w", [P, E])
        ws_in = sb("ws_in", [P, P])
        vs_in = sb("vs_in", [P, P])
        ws_out = sb("ws_out", [P, D])
        e_win = sb("e_win", [P, E, HE])
        e_vin = sb("e_vin", [P, E, HE])
        e_wout = sb("e_wout", [P, EP, D])

        x_rows = sb("x_rows", [P, TT, D])
        xb_rows = sb("xb_rows", [P, TT, D])
        x1_rows = sb("x1_rows", [P, TT, D])
        x2_rows = sb("x2_rows", [P, TT, D])
        y_rows = sb("y_rows", [P, TT, D])
        norm_rows = sb("norm_rows", [P, TT, D])
        norm_cols = sb("norm_cols", [P, T])
        stats = sb("stats", [P, TT, 6])
        moments = sb("moments", [P, TT, 2])
        ln_var = sb("ln_var", [P, TT])
        rstd = sb("rstd", [P, TT])
        newton = sb("newton", [P, 3, TT])
        q_cols = sb("q_cols", [P, T])
        heads_cols = sb("heads_cols", [P, T])

        def two(name, shape):
            t = sb(name, [P, 2, *shape])
            return t, [t[:, u] for u in range(2)]

        ctx_rows_all, ctx_rows = two("ctx_rows", [KC, D])
        ctx_cols = sb("ctx_cols", [P, K])
        HALF = P // 2
        k_high = [sb(f"k_high{u}", [P, K], F32R) for u in range(2)]
        k_mix = [sb(f"k_mix{u}", [P, 2, K], F32R) for u in range(2)]
        q_high = sb("q_high", [P, T], F32R)
        q_parts = sb("q_parts", [P, 2, T], F32R)
        v_rows_all, v_rows = two("v_rows", [KC, D])
        q_block = [sb(f"q_block{u}", [P, H, S], F32R) for u in range(2)]
        q_mix = [sb(f"q_mix{u}", [P, H, S], F32R) for u in range(2)]
        masked_all, masked = two("masked", [K])
        probs_all, probs = two("probs", [K])
        probs_t_all, probs_t = two("probs_t", [G, KC, P])
        neg_max = [sb(f"neg_max{u}", [P, G]) for u in range(2)]
        row_sum = [sb(f"row_sum{u}", [P, G]) for u in range(2)]
        row_inv = [sb(f"row_inv{u}", [P, G]) for u in range(2)]
        row_inv_wide = [sb(f"row_inv_wide{u}", [P, G, S]) for u in range(2)]
        turnstile = [sb(f"turnstile{s}", [P, 1]) for s in range(4)]
        own_inv = sb("own_inv", [P, HG, S])
        own_out = sb("own_out", [P, HG, S])

        norm_pad = sb("norm_pad", [P, B, S + 2 * PAD])
        zeros = sb("zeros", [P, NH * B])
        z_cols = sb("z_cols", [P, NH, T])
        z_act = probs_t_all[:, 1, 2:4].rearrange("p g c m -> p g (c m)")
        u_cols = sb("u_cols", [P, DIRS, NH, T])
        dt_low = sb("dt_low", [R, DIRS, T])
        bc_parts = [sb(f"bc_parts{d}", [P, T], BF16) for d in range(DIRS)]
        bc_rest = sb("bc_rest", [P, DIRS, T])
        bc_mid = sb("bc_mid", [P, DIRS, T], BF16)
        feed_all = sb("feed", [P, 2, NH * T])
        state_all = sb("state", [P, 2, NH * T])
        read_all = sb("read", [P, 2, NH * T])
        sp_pos = probs_t_all[:, 0].rearrange("p g c m -> p (g c m)").rearrange("p (d h t) -> p d h t", d=DIRS, h=NH)
        dt_cols = sb("dt_cols", [P, DIRS, NH, T])
        dtu = sb("dtu", [P, DIRS, NH, T])
        w_conv_rows = dt_cols[:, 0, :, :].rearrange("p h (j m) -> p h j m", j=TAPS)
        w_conv = state_all[:, 0, :].rearrange("p (h j m) -> p h j m", h=NH, j=TAPS)
        b_wide = [sb(f"b_wide{u}", [P, T]) for u in range(2)]
        both = lambda t: t.rearrange("p (h t) -> p h t", h=NH)
        feed, state, read = ([t[:, u, :] for u in range(2)] for t in (feed_all, state_all, read_all))
        states = state + [t.rearrange("p u k -> p (u k)") for t in (masked_all, probs_all)]
        flat = lambda t: t.rearrange("p u c d -> p (u c d)")
        sp_abs, sp_exp, sp_ln = ([both(t[:, 1, :]), both(other)] for t, other in (
            (feed_all, flat(ctx_rows_all)), (state_all, flat(v_rows_all)),
            (read_all, probs_t_all[:, 1, 0:2].rearrange("p g c m -> p (g c m)"))))
        gated = probs_t_all[:, 1, 0:2].rearrange("p g c m -> p g (c m)")
        skip_parts = [both(t.rearrange("p u k -> p (u k)")) for t in (masked_all, probs_all)]

        gates = sb("gates", [P, TT, E])
        beats, ties = (t[:, :, :].rearrange("p u k -> p (u k)").rearrange("p (t e f) -> p t e f", t=TT, e=E)
                       for t in (masked_all, probs_all))
        rank = sb("rank", [P, TT, E])
        kept = sb("kept", [P, TT, E])
        kept_sum = sb("kept_sum", [P, TT])
        kept_inv = sb("kept_inv", [P, TT])
        combine = sb("combine", [P, TT, E])
        comb_parts = sb("comb_parts", [P, T], BF16)
        comb_mid = bc_mid[0:E, 0, :]
        comb_rest = bc_rest[0:E, 0, :]
        act_in, v_in = [q_cols, heads_cols], b_wide
        mixed = [t[:, u, h * T:(h + 1) * T] for t in (feed_all, state_all, read_all) for u in range(2) for h in range(NH)]
        hidden = [v_rows_all[:, u].rearrange("p c d -> p (c d)") for u in range(2)]

        x_in, attn_w_in, out_w_in, mask_loaded, mamba_w_in, ffn_w_in = (
            sem(n) for n in ("x_in", "attn_w_in", "out_w_in", "mask_loaded", "mamba_w_in", "ffn_w_in"))
        ctx_in = [sem("ctx_in0"), sem("ctx_in1")]
        out_written = sem("out_written")
        consts_step, ident_built, consts_built, pads_cleared, bo_added = (
            sem(n) for n in ("consts_step", "ident_built", "consts_built", "pads_cleared", "bo_added"))
        picks_spread, groupmask_built, mask_scaled, a_ready = (
            sem(n) for n in ("picks_spread", "groupmask_built", "mask_scaled", "a_ready"))
        dve_step, act_step = sem("dve_step"), sem("act_step")
        ln_moments, ln_rstd, ln_rows, ln_turned, ln_cols = (
            sem(n) for n in ("ln_moments", "ln_rstd", "ln_rows", "ln_turned", "ln_cols"))
        weights_turned, weights_kept = sem("weights_turned"), sem("weights_kept")
        q_projected, q_ready, q_split, q_parts_kept, q_blocked = (
            sem(n) for n in ("q_projected", "q_ready", "q_split", "q_parts_kept", "q_blocked"))
        ctx_turned, ctx_kept, k_projected, k_ready, v_projected, v_ready = (
            sem(n) for n in ("ctx_turned", "ctx_kept", "k_projected", "k_ready", "v_projected", "v_ready"))
        k_low_ready, k_moved = sem("k_low_ready"), [sem("k_moved0"), sem("k_moved1")]
        bv_added = sem("bv_added")
        scores_done, masked_ready, probs_ready, p_turned, pt_even, pt_odd = (
            sem(n) for n in ("scores_done", "masked_ready", "probs_ready", "p_turned", "pt_even", "pt_odd"))
        inv_ready, attended, own_step, heads_ready = (
            sem(n) for n in ("inv_ready", "attended", "own_step", "heads_ready"))
        attn_out, x_done, z_done, z_kept, z_ready = (
            sem(n) for n in ("attn_out", "x_done", "z_done", "z_kept", "z_ready"))
        conv_done, u_ready = ([sem(f"{n}{d}") for d in range(DIRS)] for n in ("conv_done", "u_ready"))
        low_done, dt_low_kept, bc_done, bc_high, bc_rested, bc_middle, bc_split = (
            sem(n) for n in ("low_done", "dt_low_kept", "bc_done", "bc_high", "bc_rested", "bc_middle", "bc_split"))
        dt_raw, abs_ready, exp_ready, ln_ready, pos_ready, sp_summed, dt_ready, dtu_ready = (
            sem(n) for n in ("dt_raw", "abs_ready", "exp_ready", "ln_ready", "pos_ready", "sp_summed",
                             "dt_ready", "dtu_ready"))
        taps_in, conv_turned, conv_kept, conv_step, b_kept = (
            sem(n) for n in ("taps_in", "conv_turned", "conv_kept", "conv_step", "b_kept"))
        b_spread, c_spread, decayed, fed, scanned, was_read, summed, skip_ready = (
            sem(n) for n in ("b_spread", "c_spread", "decayed", "fed", "scanned", "was_read", "summed",
                             "skip_ready"))
        skip_summed = sem("skip_summed")
        halves_done, gated_ready, mamba_out, x2_ready = (
            sem(n) for n in ("halves_done", "gated_ready", "mamba_out", "x2_ready"))
        gate_done, gates_ready, combine_ready, combine_turned, comb_split = (
            sem(n) for n in ("gate_done", "gates_ready", "combine_ready", "combine_turned", "comb_split"))
        h_done, h_act, v_kept, h_mixed, h_ready, comb_spread, h_used, y_ready = (
            sem(n) for n in ("h_done", "h_act", "v_kept", "h_mixed", "h_ready", "comb_spread", "h_used",
                             "y_ready"))

        score_bank, turn_bank, proj_bank, out_bank, v_bank = bank[0:2], bank[2:4], bank[4:6], bank[6], bank[7]
        rows_of = lambda t: t.rearrange("b s d -> (b s) d").rearrange("(t p) d -> p t d", p=P)
        column = lambda v: v.rearrange("(p o) -> p o", o=1)
        halves = lambda v: v.rearrange("(h p) -> p h", p=P)
        MAMBA = [("L0_attn_conv_w", "L0_attn_conv_b", "L0_attn_Wx", "L0_attn_Wdt", "L0_attn_bdt",
                  "L0_attn_A_log", "L0_attn_D"),
                 ("L0_attn_conv_w_b", "L0_attn_conv_b_b", "L0_attn_Wx_b", "L0_attn_Wdt_b",
                  "L0_attn_bdt_b", "L0_attn_A_b_log", "L0_attn_D_b")]
        ATTN_LOADS, OUT_LOADS, MAMBA_LOADS, FFN_LOADS = 5, 3, 2 + 8 * DIRS, 7

        block = ctx.enter_context(nc.Block())

        @block.sync
        def _(sp):
            def load_ctx(b, u, late):
                if late:
                    sp.wait_ge(ctx_turned, b - 1)
                src = a["ctx_1024"][bass.ds(b, 1)].rearrange("o (p c) d -> (o p) c d", c=KC)
                sp.dma_start(ctx_rows[u][:, :, :], src).then_inc(ctx_in[u], 16)

            sp.dma_start(x_rows[:, :, :], rows_of(a["x"])).then_inc(x_in, 16)
            load_ctx(0, 0, False)
            sp.dma_start(wk[:, :], a["L0_xattn_wk_w"]).then_inc(attn_w_in, 16)
            sp.dma_start(bk[:, :], column(a["L0_xattn_wk_b"])).then_inc(attn_w_in, 16)
            sp.dma_start(wq[:, :], a["L0_xattn_wq_w"]).then_inc(attn_w_in, 16)
            sp.dma_start(bq[:, :], column(a["L0_xattn_wq_b"])).then_inc(attn_w_in, 16)
            sp.dma_start(wv[:, :], a["L0_xattn_wv_w"]).then_inc(attn_w_in, 16)
            load_ctx(1, 1, False)
            for g in range(HG):
                sp.dma_start(mask_in[g * S:(g + 1) * S, :],
                             a["mask_1x1xSxS2_fk1"].rearrange("a b s k -> (a b s) k")).then_inc(mask_loaded, 16)

            def move_k(b, u):
                sp.wait_ge(k_ready, b + 1)
                sp.dma_start(k_mix[u][HALF:P, 0, :].bitcast(F32), k_high[u][0:HALF, :].bitcast(F32)).then_inc(k_moved[u], 16)
                sp.dma_start(k_mix[u][0:HALF, 1, :].bitcast(F32), k_high[u][HALF:P, :].bitcast(F32)).then_inc(k_moved[u], 16)

            for u in range(2):
                load_ctx(2 + u, u, True)
                move_k(u, u)
            sp.dma_start(wo[:, :], a["L0_xattn_wo_w"]).then_inc(out_w_in, 16)
            sp.dma_start(bv[:, :], column(a["L0_xattn_wv_b"])).then_inc(out_w_in, 16)
            sp.dma_start(bo[:, :], a["L0_xattn_wo_b"].partition_broadcast(P)).then_inc(out_w_in, 16)
            sp.dma_start(w_in_rows[:, :, :], a["L0_attn_W_in"].rearrange("(c p) d -> p c d", p=P)).then_inc(mamba_w_in, 16)
            sp.dma_start(w_out_rows[:, :], a["L0_attn_W_out"]).then_inc(mamba_w_in, 16)
            for d, (cw, cb, wx, wd, bd, al, ds) in enumerate(MAMBA):
                sp.dma_start(wx_rows[:, d, :], a[wx]).then_inc(mamba_w_in, 16)
                sp.dma_start(wdt_rows[:, d, :, :], a[wd].rearrange("(h p) r -> p h r", p=P)).then_inc(mamba_w_in, 16)
                sp.dma_start(conv_w[:, d, :, :], a[cw].rearrange("(h p) o j -> p h (o j)", p=P)).then_inc(mamba_w_in, 16)
                sp.dma_start(a_log[:, d, :, :], a[al].rearrange("(h p) n -> p h n", p=P)).then_inc(mamba_w_in, 16)
                sp.dma_start(conv_b[:, d, :], halves(a[cb]), allow_slow_non_contiguous=True).then_inc(mamba_w_in, 16)
                sp.dma_start(bdt[:, d, :], halves(a[bd]), allow_slow_non_contiguous=True).then_inc(mamba_w_in, 16)
                sp.dma_start(d_skip[:, d, :], halves(a[ds]), allow_slow_non_contiguous=True).then_inc(mamba_w_in, 16)
                sp.dma_start(gate_rows[:, :], a["L0_ffn_gate_w"]).then_inc(mamba_w_in, 16) if d == 0 else \
                    sp.dma_start(ws_out[:, :], a["L0_ffn_ws_out"]).then_inc(mamba_w_in, 16)
            with sp.Fori(2, PAIRS) as i:
                for u in range(2):
                    load_ctx(2 * i + u, u, True)
                    move_k(2 * i - 2 + u, u)
            for u in range(2):
                move_k(B - 2 + u, u)
            sp.dma_start(e_win[:, :, :], a["L0_ffn_e_win"].rearrange("e d h -> d e h")).then_inc(ffn_w_in, 16)
            sp.dma_start(e_vin[:, :, :], a["L0_ffn_e_vin"].rearrange("e d h -> d e h")).then_inc(ffn_w_in, 16)
            sp.dma_start(e_wout[:, :, :], a["L0_ffn_e_wout"].rearrange("(j e) h d -> (e h) j d", j=EP)).then_inc(ffn_w_in, 16)
            sp.dma_start(ws_in[:, :], a["L0_ffn_ws_in"]).then_inc(ffn_w_in, 16)
            sp.dma_start(vs_in[:, :], a["L0_ffn_vs_in"]).then_inc(ffn_w_in, 16)
            sp.wait_ge(y_ready, 1)
            sp.dma_start(rows_of(out), y_rows[:, :, :]).then_inc(out_written, 16)
            sp.wait_ge(out_written, 16)

        @block.gpsimd
        def _(pool):
            built = [0]

            def link(ins):
                built[0] += 1
                ins.then_inc(consts_step, 1)
                pool.wait_ge(consts_step, built[0])

            def where(t, pattern, base, step, compare, fill):
                return nc.gpsimd.affine_select(out=t, in_=t, compare_op=compare, fill=fill, base=base,
                                               pattern=pattern, channel_multiplier=step)

            link(pool.memset(ident[:, :], 0.0))
            where(ident[:, :], [[-1, P]], 0, 1, ALU.not_equal, 1.0).then_inc(ident_built, 1)
            link(pool.memset(headmask[:, :], 1.0))
            link(where(headmask[:, :], [[-DH, H]], 0, 1, ALU.is_ge, 0.0))
            link(where(headmask[:, :], [[DH, H]], DH - 1, -1, ALU.is_ge, 0.0))
            link(pool.tensor_tensor(mixmask[:, :], headmask[:, 0:H // 2], headmask[:, H // 2:H], ALU.add))
            link(pool.memset(pick[:, :], 0.0))
            for part in range(3):
                link(where(pick[:, :], [[-1, 32]], -32 * part, 1, ALU.not_equal, 1.0))
            link(pool.memset(earlier[:, :, :], 1.0))
            where(earlier[:, :, :], [[1, E], [-1, E]], -1, 0, ALU.is_ge, 0.0).then_inc(consts_built, 1)
            pool.memset(norm_pad[:, :, :], 0.0).then_inc(pads_cleared, 1)
            pool.memset(zeros[:, :], 0.0).then_inc(pads_cleared, 1)

            def block_q(b, u, late, first=False):
                if late:
                    pool.wait_ge(scores_done, G * (b - 1))
                pool.tensor_tensor(q_block[u][:, :, :],
                                   q_high[:, bass.ds(b * S, S)].unsqueeze(1).to_broadcast([P, H, S]),
                                   headmask[:, :].unsqueeze(2).to_broadcast([P, H, S]), ALU.mult)
                if first:
                    pool.wait_ge(q_split, 2)
                    pool.wait_ge(q_parts_kept, 1)
                for m in range(2):
                    last = pool.tensor_tensor(q_mix[u][:, m * H // 2:(m + 1) * H // 2, :],
                                              q_parts[:, m, bass.ds(b * S, S)].unsqueeze(1).to_broadcast([P, H // 2, S]),
                                              mixmask[:, :].unsqueeze(2).to_broadcast([P, H // 2, S]), ALU.mult)
                last.then_inc(q_blocked, 1)

            pool.wait_ge(q_split, 1)
            for u in range(2):
                block_q(u, u, False, u == 0)
            with pool.Fori(1, PAIRS) as i:
                for u in range(2):
                    block_q(2 * i + u, u, True)
            pool.wait_ge(x_in, 16)
            pool.wait_ge(out_w_in, 16 * OUT_LOADS)
            pool.tensor_tensor(xb_rows[:, :, :], x_rows[:, :, :],
                               bo[:, :].unsqueeze(1).to_broadcast([P, TT, D]), ALU.add).then_inc(bo_added, 1)
            pool.wait_ge(mamba_w_in, 16 * MAMBA_LOADS)
            for h in range(NH):
                pool.tensor_tensor(w_conv_rows[:, h, :, :],
                                   w_in_rows[:, h, :].unsqueeze(1).to_broadcast([P, TAPS, D]),
                                   conv_w[:, 0, h, :].unsqueeze(2).to_broadcast([P, TAPS, D]),
                                   ALU.mult).then_inc(taps_in, 1)
            pool.tensor_copy(pick_bc[:, :, :], pick[:, :].unsqueeze(2).to_broadcast([P, 2 * N, P])).then_inc(picks_spread, 1)
            pool.tensor_copy(pick_ex[:, :, :], pick[:, 0:E].unsqueeze(2).to_broadcast([P, E, HE])).then_inc(picks_spread, 1)

            for d in (1, 0):
                pool.wait_ge(u_ready[d], NH)
                pool.tensor_tensor(skip_parts[d], u_cols[:, d, :, :],
                                   d_skip[:, d, :].unsqueeze(2).to_broadcast([P, NH, T]), ALU.mult).then_inc(skip_ready, 1)

            def sum_softplus(d):
                for h in range(NH):
                    pool.wait_ge(pos_ready, NH * d + h + 1)
                    pool.wait_ge(ln_ready, NH * d + h + 1)
                    pool.tensor_tensor(sp_pos[:, d, h, :], sp_pos[:, d, h, :], sp_ln[d][:, h, :],
                                       ALU.add).then_inc(sp_summed, 1)

            def feed_states(d, k, u, late):
                pool.wait_ge(b_kept, k + 1)
                if late:
                    pool.wait_ge(scanned, k - 1)
                pool.tensor_tensor(both(feed[u]), dtu[:, d, :, :],
                                   b_wide[u][:, :].unsqueeze(1).to_broadcast([P, NH, T]), ALU.mult).then_inc(fed, 1)

            sum_softplus(0)
            for d in range(DIRS):
                pool.wait_ge(dtu_ready, NH * (d + 1))
                for u in range(2):
                    feed_states(d, N * d + u, u, d == 1)
                if d == 0:
                    sum_softplus(1)
                with pool.Fori(1, NP) as i:
                    for u in range(2):
                        feed_states(d, N * d + 2 * i + u, u, True)

            pool.wait_ge(halves_done, NH)
            for j in range(EP + 1):
                pool.wait_ge(h_act, j + 1)
                pool.wait_ge(v_kept, j + 1)
                pool.tensor_tensor(mixed[j], act_in[j % 2][:, :], v_in[j % 2][:, :], ALU.mult).then_inc(h_mixed, 1)

        @block.tensor
        def _(pe):
            def keep_warm(to, products):
                for _ in range(products):
                    pe.matmul(to[:, 0:P], ident[:, :], ident[:, :], start=True, stop=True)

            def turn_norm(n):
                to = bank[(2, 1, 5)[n]]
                for t in range(TT):
                    pe.wait_ge(ln_rows, TT * n + t + 1)
                    last = pe.transpose(to[:, t * P:(t + 1) * P], norm_rows[:, t, :], ident[:, :])
                last.then_inc(ln_turned, 1)

            def turn_ctx(b, u, i, late):
                pe.wait_ge(ctx_in[u], 16 * (i + 1))
                if late:
                    pe.wait_ge(ctx_kept, b)
                for c in range(KC):
                    last = pe.transpose(proj_bank[0][:, c * P:(c + 1) * P], ctx_rows[u][:, c, :], ident[:, :])
                last.then_inc(ctx_turned, 1)

            def project_k(b):
                pe.wait_ge(ctx_kept, b + 1)
                pe.wait_ge(k_low_ready, b)
                pe.matmul(proj_bank[1][:, :], wk[:, :], ctx_cols[:, :], start=True, stop=True).then_inc(k_projected, 1)

            def project_v(b, late):
                if late:
                    pe.wait_ge(v_ready, b)
                for c in range(KC):
                    last = pe.matmul(v_bank[:, c * P:(c + 1) * P], ctx_cols[:, c * P:(c + 1) * P],
                                     wv[:, :], start=True, stop=True)
                last.then_inc(v_projected, 1)

            def score(b, u, i, g, late):
                if g == 0:
                    pe.wait_ge(q_blocked, b + 1)
                    pe.wait_ge(k_ready, b + 1)
                    pe.wait_ge(k_low_ready, b + 1)
                    pe.wait_ge(k_moved[u], 32 * (i + 1))
                if late or g >= 2:
                    pe.wait_ge(masked_ready, G * b + g - 1)
                pe.matmul(score_bank[g % 2][:, :], q_block[u][:, g * HG:(g + 1) * HG, :],
                          k_high[u][:, :], start=True, stop=False)
                pe.matmul(score_bank[g % 2][:, :], q_mix[u][:, g * HG:(g + 1) * HG, :],
                          k_mix[u][:, g // 2, :], start=False, stop=True).then_inc(scores_done, 1)

            def turn_p(b, g, late):
                pe.wait_ge(probs_ready, G * b + g + 1)
                if late or g >= 2:
                    pe.wait_ge((pt_even, pt_odd)[g % 2], 2 * b + g // 2)
                for c in range(KC):
                    last = pe.transpose(turn_bank[g % 2][:, c * P:(c + 1) * P],
                                        probs[g % 2][:, c * P:(c + 1) * P], ident[:, :])
                last.then_inc(p_turned, 1)

            def attend(b, u):
                pe.wait_ge(pt_even, 2 * b + 2)
                pe.wait_ge(pt_odd, 2 * b + 2)
                pe.wait_ge(v_ready, b + 1)
                pe.wait_ge(inv_ready, b + 1)
                pe.wait_ge(heads_ready, b + 1)
                pe.matmul(out_bank[:, P:2 * P], row_inv_wide[u][:, :, :], ident[:, :], start=True, stop=True)
                for c in range(KC):
                    for g in range(G):
                        rows = slice(g * 32, g * 32 + 32)
                        last = pe.matmul(out_bank[rows, 0:P], v_rows[u][:, c, rows], probs_t[u][:, g, c, :],
                                         start=(c == 0), stop=(c == KC - 1))
                last.then_inc(attended, 1)

            def turn_weights():
                pe.wait_ge(mamba_w_in, 16 * MAMBA_LOADS)
                for c in range(2 * NH):
                    last = pe.transpose(bank[4][:, c * P:(c + 1) * P], w_in_rows[:, c, :], ident[:, :])
                last.then_inc(weights_turned, 1)
                W = R + 2 * N
                for d in range(DIRS):
                    for h in range(NH):
                        at = (d * NH + h) * W
                        last = pe.transpose(bank[5][:, at:at + W], wx_rows[:, d, h * P:(h + 1) * P], ident[0:W, 0:W])
                last.then_inc(weights_turned, 1)
                for h in range(NH):
                    pe.transpose(bank[7][:, h * P:(h + 1) * P], w_out_rows[:, h * P:(h + 1) * P], ident[:, :])
                pe.transpose(bank[7][:, NH * P:NH * P + E], gate_rows[:, :], ident[0:E, 0:E]).then_inc(weights_turned, 1)
                for d in range(DIRS):
                    for h in range(NH):
                        at = (d * NH + h) * P
                        last = pe.transpose(bank[3][0:R, at:at + P], wdt_rows[:, d, h, :], ident[:, :])
                last.then_inc(weights_turned, 1)

            pe.wait_ge(ident_built, 1)
            keep_warm(bank[0], 6)
            turn_ctx(0, 0, 0, False)
            keep_warm(bank[0], 3)
            pe.wait_ge(attn_w_in, 16 * ATTN_LOADS)
            pe.wait_ge(ctx_kept, 1)
            pe.matmul(proj_bank[1][:, :], wk[:, :], ctx_cols[:, :], start=True, stop=True).then_inc(k_projected, 1)
            turn_norm(0)
            project_v(0, False)
            pe.wait_ge(ln_cols, 1)
            pe.matmul(bank[3][:, :], wq[:, :], norm_cols[:, :], start=True, stop=True).then_inc(q_projected, 1)
            turn_ctx(1, 1, 0, True)
            project_k(1)

            def sequence(b, u, i, late, left):
                score(b, u, i, 0, late)
                score(b, u, i, 1, late)
                if late:
                    turn_p(b - 1, 3, True)
                if left:
                    project_v(b + 1, True)
                score(b, u, i, 2, late)
                turn_p(b, 0, late)
                score(b, u, i, 3, late)
                if left == 2:
                    turn_ctx(b + 2, u, i + 1, True)
                if late:
                    attend(b - 1, 1 - u)
                turn_p(b, 1, late)
                turn_p(b, 2, late)
                if left == 2:
                    project_k(b + 2)

            sequence(0, 0, 0, False, 2)
            sequence(1, 1, 0, True, 2)
            with pe.Fori(1, PAIRS - 1) as i:
                for u in range(2):
                    sequence(2 * i + u, u, i, True, 2)
            sequence(B - 2, 0, PAIRS - 1, True, 1)
            sequence(B - 1, 1, PAIRS - 1, True, 0)
            turn_p(B - 1, 3, True)
            attend(B - 1, 1)
            turn_weights()

            pe.wait_ge(bv_added, 1)
            pe.wait_ge(out_w_in, 16 * OUT_LOADS)
            for t in range(TT):
                last = pe.matmul(bank[0][:, t * P:(t + 1) * P], heads_cols[:, t * P:(t + 1) * P], wo[:, :],
                                 start=True, stop=True)
            last.then_inc(attn_out, 1)

            for h in range(NH):
                pe.wait_ge(taps_in, h + 1)
                for j in range(TAPS):
                    last = pe.transpose(bank[2 + 4 * h][:, j * P:(j + 1) * P], w_conv_rows[:, h, j, :], ident[:, :])
                last.then_inc(conv_turned, 1)
            pe.wait_ge(weights_kept, 3)
            keep_warm(bank[7], 14)
            turn_norm(1)
            pe.wait_ge(ln_cols, 2)
            here = norm_pad[:, :, PAD:PAD + S]
            pe.wait_ge(weights_kept, 4)
            pe.wait_ge(conv_kept, NH)
            for h in range(NH):
                pe.matmul(bank[2 + h], w_in[:, h, :], here, start=True, stop=True).then_inc(x_done, 1)
            for h in range(NH):
                for back in range(TAPS):
                    last = pe.matmul(bank[h], w_conv[:, h, PAD - back, :], norm_pad[:, :, PAD - back:PAD - back + S],
                                     start=(back == 0), stop=(back == TAPS - 1))
                last.then_inc(conv_done[0], 1)

            def project_z(h):
                pe.matmul(bank[4 + h], w_in[:, NH + h, :], here, start=True, stop=True).then_inc(z_done, 1)

            def project_u(d):
                pe.wait_ge(u_ready[d], NH)
                for h in range(NH):
                    last = pe.matmul(bank[6 + d][0:R, :], wx_dt[:, d, h, :], u_cols[:, d, h, :],
                                     start=(h == 0), stop=(h == NH - 1))
                last.then_inc(low_done, 1)
                pe.wait_ge(z_kept, d + 1)
                for h in range(NH):
                    last = pe.matmul(bank[4 + d], wx_bc[:, d, h, :, :], u_cols[:, d, h, :],
                                     start=(h == 0), stop=(h == NH - 1))
                last.then_inc(bc_done, 1)

            def project_dt(d):
                pe.wait_ge(dt_low_kept, d + 1)
                for h in range(NH):
                    pe.matmul(bank[2 * d + h], wdt[:, d, h, :], dt_low[:, d, :],
                              start=True, stop=True).then_inc(dt_raw, 1)

            project_z(0)
            project_u(0)
            project_dt(0)
            project_z(1)
            project_u(1)
            pe.wait_ge(picks_spread, 2)
            pe.wait_ge(bc_split, 1)
            pe.matmul(bank[4], pick_bc[:, 0, :], bc_parts[0][:, :], start=True, stop=True).then_inc(b_spread, 1)
            project_dt(1)

            def spread_b(d, n, k):
                pe.wait_ge(b_kept, k)
                pe.matmul(bank[4], pick_bc[:, bass.ds(n, 1), :].rearrange("p o m -> p (o m)"),
                          bc_parts[d][:, :], start=True, stop=True).then_inc(b_spread, 1)

            def spread_c(d, n, k):
                pe.wait_ge(was_read, k)
                pe.matmul(bank[5], pick_bc[:, bass.ds(n + N, 1), :].rearrange("p o m -> p (o m)"),
                          bc_parts[d][:, :], start=True, stop=True).then_inc(c_spread, 1)

            def add_up(k, u, stop):
                pe.wait_ge(was_read, k + 1)
                for h in range(NH):
                    last = pe.matmul(bank[6 + h], ident[:, :], read[u][:, h * T:(h + 1) * T],
                                     start=False, stop=stop)
                last.then_inc(summed, 1)

            pe.wait_ge(bc_rested, DIRS)
            pe.matmul(bank[5], pick_bc[:, N, :], bc_parts[0][:, :], start=True, stop=True).then_inc(c_spread, 1)
            spread_b(0, 1, 1)
            pe.wait_ge(skip_ready, DIRS)
            pe.wait_ge(dt_low_kept, DIRS)
            for h in range(NH):
                for d in range(DIRS):
                    last = pe.matmul(bank[6 + h], ident[:, :], skip_parts[d][:, h, :], start=(d == 0), stop=False)
            last.then_inc(skip_summed, 1)

            spread_b(0, 2, 2)
            spread_b(0, 3, 3)

            def unit(k, u, d_b, n_b, d_c, n_c):
                spread_c(d_c, n_c, k + 1)
                if n_b is not None:
                    spread_b(d_b, n_b, k + 4)
                add_up(k, u, False)

            for d in range(DIRS):
                with pe.Fori(0, NP - 2) as i:
                    for u in range(2):
                        unit(N * d + 2 * i + u, u, d, 2 * i + u + 4, d, 2 * i + u + 1)
                if d == 0:
                    pe.wait_ge(bc_split, DIRS)
                for n in range(N - 4, N - 1):
                    unit(N * d + n, n % 2, 1, n + 4 - N if d == 0 else None, d, n + 1)
                if d == 0:
                    unit(N - 1, 1, 1, 3, 1, 0)
            pe.wait_ge(was_read, 2 * N)
            for h in range(NH):
                pe.matmul(bank[6 + h], ident[:, :], read[1][:, h * T:(h + 1) * T],
                          start=False, stop=True).then_inc(halves_done, 1)
            pe.wait_ge(gated_ready, 1)
            for t in range(TT):
                for h in range(NH):
                    last = pe.matmul(bank[4][:, t * P:(t + 1) * P], gated[:, h, t * P:(t + 1) * P], w_out[:, h, :],
                                     start=(h == 0), stop=(h == NH - 1))
            last.then_inc(mamba_out, 1)

            keep_warm(bank[0], 17)
            turn_norm(2)
            pe.wait_ge(ln_cols, 3)
            pe.wait_ge(x2_ready, 1)
            for t in range(TT):
                last = pe.matmul(bank[4][:, t * E:(t + 1) * E], norm_cols[:, t * P:(t + 1) * P], gate_w[:, :],
                                 start=True, stop=True)
            last.then_inc(gate_done, 1)
            pe.wait_ge(ffn_w_in, 16 * (FFN_LOADS - 2))

            def hidden_in(j):
                if j >= 2:
                    pe.wait_ge(h_act, j - 1)
                    pe.wait_ge(v_kept, j - 1)
                win = e_win[:, 2 * j:2 * j + 2, :] if j < EP else ws_in[:, :]
                vin = e_vin[:, 2 * j:2 * j + 2, :] if j < EP else vs_in[:, :]
                pe.matmul(bank[j % 2][:, :], win, norm_cols[:, :], start=True, stop=True)
                pe.matmul(bank[2 + j % 2][:, :], vin, norm_cols[:, :], start=True, stop=True).then_inc(h_done, 1)

            def spread_combine(j):
                if j >= 2:
                    pe.wait_ge(h_ready, j - 1)
                pe.matmul(bank[6 + j % 2][:, :], pick_ex[:, 2 * j:2 * j + 2, :], comb_parts[:, :],
                          start=True, stop=True).then_inc(comb_spread, 1)

            def hidden_out(j, first, stop):
                if j < EP:
                    pe.wait_ge(h_ready, j + 1)
                else:
                    pe.wait_ge(h_mixed, EP + 1)
                w = e_wout[:, j, :] if j < EP else ws_out[:, :]
                left = hidden[j % 2] if j < EP else mixed[EP]
                for t in range(TT):
                    last = pe.matmul(bank[5][:, t * P:(t + 1) * P], left[:, t * P:(t + 1) * P], w,
                                     start=(first and t == 0), stop=stop, skip_group_check=True)
                last.then_inc(h_used, 1)

            for j in range(EP - 1):
                hidden_in(j)
                if j == EP // 2:
                    pe.wait_ge(combine_ready, 1)
                    for t in range(TT):
                        last = pe.transpose(bank[4][0:E, t * P:(t + 1) * P], combine[:, t, :], ident[:, :])
                    last.then_inc(combine_turned, 1)
            pe.wait_ge(comb_split, 1)
            spread_combine(0)
            spread_combine(1)
            hidden_in(EP - 1)
            for j in range(EP):
                hidden_out(j, j == 0, False)
                if j + 2 < EP:
                    spread_combine(j + 2)
                if j == 1:
                    hidden_in(EP)
            hidden_out(EP, False, True)

        @block.scalar
        def _(act):
            nc.scalar.preload_act_table_set("natural_log_exp_and_others")

            def inv_std(n):
                act.wait_ge(ln_moments, n + 1)
                act.activation(ln_var[:, :], moments[:, :, 1], ACT.Ln, bias=EPS).then_inc(act_step, 1)
                act.wait_ge(act_step, n + 1)
                act.activation(rstd[:, :], ln_var[:, :], ACT.Exp, scale=-0.5).then_inc(ln_rstd, 1)

            def keep_ctx(b, late):
                act.wait_ge(ctx_turned, b + 1)
                if late:
                    act.wait_ge(v_projected, b)
                act.copy(ctx_cols[:, :], proj_bank[0][:, :]).then_inc(ctx_kept, 1)

            def keep_k(b, u, late):
                act.wait_ge(k_projected, b + 1)
                if late:
                    act.wait_ge(scores_done, G * (b - 1))
                act.activation(k_high[u][:, :], proj_bank[1][:, :], ACT.Identity,
                               bias=bk[:, 0:1]).then_inc(k_ready, 1)

            def keep_v(b, u, late):
                act.wait_ge(v_projected, b + 1)
                if late:
                    act.wait_ge(attended, b - 1)
                act.copy(v_rows[u][:, :, :], v_bank[:, :].rearrange("p (c d) -> p c d", c=KC)).then_inc(v_ready, 1)

            def exponentials(b, u, g, late, first):
                act.wait_ge(masked_ready, G * b + g + 1)
                if late or g >= 2:
                    act.wait_ge(p_turned, G * b + g - 1)
                if late and not first and g == 0:
                    act.wait_ge(inv_ready, b - 1)
                act.activation(probs[g % 2][:, :], masked[g % 2][:, :], ACT.Exp, bias=neg_max[u][:, g:g + 1],
                               scale=-1.0, accum_out=row_sum[u][:, g:g + 1]).then_inc(probs_ready, 1)

            def keep_pt(b, u, g, late):
                act.wait_ge(p_turned, G * b + g + 1)
                if late and g == 0:
                    act.wait_ge(attended, b - 1)
                act.copy(probs_t[u][:, g, :, :], turn_bank[0][:, :].rearrange("p (c m) -> p c m", c=KC)).then_inc(pt_even, 1)

            inv_std(0)
            keep_ctx(0, False)
            act.wait_ge(attn_w_in, 16 * ATTN_LOADS)
            keep_k(0, 0, False)
            keep_v(0, 0, False)
            keep_ctx(1, True)
            act.wait_ge(q_ready, 1)
            for m, rows in enumerate((slice(0, HALF), slice(HALF, P))):
                last = act.copy(q_parts[rows, m, :], q_cols[rows, :])
            last.then_inc(q_parts_kept, 1)
            keep_k(1, 1, False)

            def sequence(b, u, late, left, first=False):
                exponentials(b, u, 0, late, first)
                exponentials(b, u, 1, late, first)
                keep_pt(b, u, 0, late and not first)
                exponentials(b, u, 2, late, first)
                if left == 2:
                    keep_ctx(b + 2, True)
                if left:
                    keep_v(b + 1, 1 - u, late)
                exponentials(b, u, 3, late, first)
                keep_pt(b, u, 2, late)
                if left == 2:
                    keep_k(b + 2, u, True)

            sequence(0, 0, False, 2)
            sequence(1, 1, True, 2, first=True)
            with act.Fori(1, PAIRS - 1) as i:
                for u in range(2):
                    sequence(2 * i + u, u, True, 2)
            sequence(B - 2, 0, True, 1)
            sequence(B - 1, 1, True, 0)

            act.wait_ge(weights_turned, 1)
            act.copy(w_in[:, :, :], bank[4][:, :].rearrange("p (c m) -> p c m", m=P)).then_inc(weights_kept, 1)
            act.wait_ge(weights_turned, 2)
            W = R + 2 * N
            turned = bank[5][:, 0:DIRS * NH * W].rearrange("p (d h w) -> p d h w", d=DIRS, h=NH)
            act.copy(wx_dt[:, :, :, :], turned[:, :, :, 0:R]).then_inc(act_step, 1)
            for d in range(DIRS):
                for h in range(NH):
                    last = act.copy(wx_bc[:, d, h, :, :], turned[:, d, h, R:W].unsqueeze(1).to_broadcast([P, 4, 2 * N]))
            last.then_inc(weights_kept, 1)
            act.wait_ge(weights_turned, 3)
            act.copy(w_out[:, :, :], bank[7][:, 0:NH * P].rearrange("p (h m) -> p h m", h=NH)).then_inc(act_step, 1)
            act.copy(gate_w[:, :], bank[7][:, NH * P:NH * P + E]).then_inc(weights_kept, 1)
            act.wait_ge(weights_turned, 4)
            act.copy(wdt[:, :, :, :], bank[3][0:R, :].rearrange("p (d h m) -> p d h m", d=DIRS, h=NH)).then_inc(weights_kept, 1)
            act.wait_ge(mamba_w_in, 16 * MAMBA_LOADS)
            act.activation(a_exp[:, :, :, :], a_log[:, :, :, :], ACT.Exp).then_inc(act_step, 1)
            act.wait_ge(act_step, 4)
            act.mul(a_neg[:, :, :, :], a_exp[:, :, :, :], -1.0).then_inc(a_ready, 1)

            def keep_dt_low(d):
                act.wait_ge(low_done, d + 1)
                act.copy(dt_low[:, d, :], bank[6 + d][0:R, :]).then_inc(dt_low_kept, 1)

            def keep_z(h):
                act.wait_ge(z_done, h + 1)
                act.copy(z_cols[:, h, :], bank[4 + h]).then_inc(z_kept, 1)

            def bc_first_part(d):
                act.wait_ge(bc_done, d + 1)
                act.copy(bc_parts[d][:, :], bank[4 + d]).then_inc(bc_high, 1)

            def bc_second_part(d):
                act.wait_ge(bc_rested, d + 1)
                act.copy(bc_mid[:, d, :], bc_rest[:, d, :])
                act.copy(bc_parts[d][32:64, :], bc_rest[32:64, d, :]).then_inc(bc_middle, 1)

            def absolutes(d):
                for h in range(NH):
                    act.wait_ge(dt_raw, d * NH + h + 1)
                    act.activation(sp_abs[d][:, h, :], bank[2 * d + h], ACT.Abs,
                                   bias=bdt[:, d, h:h + 1]).then_inc(abs_ready, 1)

            def exps_and_logs(d):
                for h in range(NH):
                    act.wait_ge(abs_ready, d * NH + h + 1)
                    act.activation(sp_exp[d][:, h, :], sp_abs[d][:, h, :], ACT.Exp, scale=-1.0).then_inc(exp_ready, 1)
                for h in range(NH):
                    act.wait_ge(exp_ready, d * NH + h + 1)
                    act.activation(sp_ln[d][:, h, :], sp_exp[d][:, h, :], ACT.Ln, bias=1.0).then_inc(ln_ready, 1)

            inv_std_steps = 5
            act.wait_ge(ln_moments, 2)
            act.activation(ln_var[:, :], moments[:, :, 1], ACT.Ln, bias=EPS).then_inc(act_step, 1)
            act.wait_ge(act_step, inv_std_steps)
            act.activation(rstd[:, :], ln_var[:, :], ACT.Exp, scale=-0.5).then_inc(ln_rstd, 1)
            for h in range(NH):
                act.wait_ge(conv_turned, h + 1)
                act.copy(w_conv[:, h, :, :], bank[2 + 4 * h].rearrange("p (j m) -> p j m", j=TAPS)).then_inc(conv_kept, 1)
            for h in range(NH):
                for d in (1, 0):
                    act.wait_ge(conv_done[d], h + 1)
                    act.activation(u_cols[:, d, h, :], bank[h] if d == 0 else u_cols[:, d, h, :], ACT.Silu,
                                   bias=conv_b[:, d, h:h + 1]).then_inc(u_ready[d], 1)
            nc.scalar.preload_act_table_set("natural_log_exp_and_others")
            keep_z(0)
            keep_dt_low(0)
            bc_first_part(0)
            absolutes(0)
            exps_and_logs(0)
            bc_second_part(0)
            keep_z(1)
            keep_dt_low(1)
            bc_first_part(1)

            steps_of = lambda t: t.rearrange("p (b s) -> p b s", s=S)

            def no_decay(d, k, u, late):
                if late:
                    act.wait_ge(scanned, k - 1)
                first = 0 if d == 0 else S - 1
                act.copy(duo[u][:, :, :].rearrange("p h (b s) -> p (h b) s", s=S)[:, :, first:first + 1],
                         zeros[:, :].unsqueeze(2)).then_inc(act_step, 1)

            def decays(d, n, k, u, late):
                if late:
                    act.wait_ge(scanned, k - 1)
                steps = slice(1, S) if d == 0 else slice(0, S - 1)
                for h in range(NH):
                    act.wait_ge(dt_ready, NH * d + h + 1)
                    act.activation(steps_of(duo[u][:, h, :])[:, :, steps], steps_of(dt_cols[:, d, h, :])[:, :, steps],
                                   ACT.Exp, scale=a_neg[:, d, h, bass.ds(n, 1)]).then_inc(decayed, 1)

            def keep_b(k, u, late):
                act.wait_ge(b_spread, k + 1)
                if late:
                    act.wait_ge(fed, k - 1)
                act.copy(b_wide[u][:, :], bank[4]).then_inc(b_kept, 1)

            act.wait_ge(a_ready, 1)
            act.wait_ge(pads_cleared, 2)
            act.wait_ge(pos_ready, NH)
            no_decay(0, 0, 0, False)
            keep_b(0, 0, False)
            decays(0, 0, 0, 0, False)
            absolutes(1)
            for h in range(NH):
                act.activation(sp_pos[:, 1, h, :], bank[2 + h], ACT.Relu, bias=bdt[:, 1, h:h + 1]).then_inc(pos_ready, 1)
            act.wait_ge(pos_ready, DIRS * NH)
            act.wait_ge(abs_ready, DIRS * NH)
            no_decay(0, 1, 1, False)
            keep_b(1, 1, False)
            decays(0, 1, 1, 1, False)
            bc_second_part(1)
            exps_and_logs(1)
            keep_b(2, 0, True)
            for d in range(DIRS):
                if d == 1:
                    for u in range(2):
                        no_decay(1, N + u, u, True)
                    for u in range(2):
                        decays(1, u, N + u, u, True)
                        keep_b(N + u + 1, 1 - u, True)
                with act.Fori(1, NP - 1) as i:
                    for u in range(2):
                        decays(d, 2 * i + u, N * d + 2 * i + u, u, True)
                        keep_b(N * d + 2 * i + u + 1, 1 - u, True)
                for u in range(2):
                    decays(d, N - 2 + u, N * d + N - 2 + u, u, True)
                    if d == 0 or u == 0:
                        keep_b(N * d + N - 2 + u + 1, 1 - u, True)
            for h in range(NH):
                act.activation(z_act[:, h, :], z_cols[:, h, :], ACT.Silu).then_inc(z_ready, 1)
            nc.scalar.preload_act_table_set("natural_log_exp_and_others")

            act.wait_ge(ln_moments, 3)
            act.activation(ln_var[:, :], moments[:, :, 1], ACT.Ln, bias=EPS).then_inc(act_step, 1)
            act.wait_ge(act_step, inv_std_steps + 2 * DIRS + 1)
            act.activation(rstd[:, :], ln_var[:, :], ACT.Exp, scale=-0.5).then_inc(ln_rstd, 1)
            act.wait_ge(gate_done, 1)
            act.activation(gates[:, :, :], bank[4][:, 0:TT * E].rearrange("p (t e) -> p t e", e=E),
                           ACT.Sigmoid).then_inc(gates_ready, 1)
            for j in range(EP + 1):
                act.wait_ge(h_done, j + 1)
                if j >= 2:
                    act.wait_ge(h_mixed, j - 1)
                act.activation(act_in[j % 2][:, :], bank[j % 2][:, :], ACT.Silu).then_inc(h_act, 1)
                act.copy(v_in[j % 2][:, :], bank[2 + j % 2][:, :]).then_inc(v_kept, 1)

        @block.vector
        def _(dve):
            steps = [0]

            def link(ins):
                steps[0] += 1
                ins.then_inc(dve_step, 1)
                dve.wait_ge(dve_step, steps[0])

            def layer_norm(n, rows):
                if n:
                    dve.wait_ge(ln_turned, n)
                for t in range(TT):
                    last = dve.bn_stats(stats[:, t, :], rows[:, t, :])
                link(last)
                for t in range(TT):
                    last = dve.bn_aggr(moments[:, t, :], stats[:, t, :])
                last.then_inc(ln_moments, 1)
                dve.wait_ge(ln_moments, n + 1)
                link(dve.tensor_scalar(newton[:, 0, :], moments[:, :, 1], EPS, None, ALU.add))
                dve.wait_ge(ln_rstd, n + 1)
                link(dve.tensor_tensor(newton[:, 1, :], rstd[:, :], rstd[:, :], ALU.mult))
                link(dve.tensor_tensor(newton[:, 1, :], newton[:, 1, :], newton[:, 0, :], ALU.mult))
                link(dve.tensor_scalar(newton[:, 1, :], newton[:, 1, :], -0.5, 1.5, ALU.mult, ALU.add))
                link(dve.tensor_tensor(newton[:, 2, :], newton[:, 1, :], rstd[:, :], ALU.mult))
                for t in range(TT):
                    dve.tensor_scalar(norm_rows[:, t, :], rows[:, t, :], moments[:, t, 0:1],
                                      newton[:, 2, t:t + 1], ALU.subtract, ALU.mult).then_inc(ln_rows, 1)
                dve.wait_ge(ln_turned, n + 1)
                if n == 1:
                    dve.wait_ge(pads_cleared, 2)
                to = norm_pad[:, :, PAD:PAD + S] if n == 1 else norm_cols[:, :].rearrange("p (b s) -> p b s", s=S)
                dve.tensor_copy(to, bank[(2, 1, 5)[n]][:, :].rearrange("p (b s) -> p b s", s=S)).then_inc(ln_cols, 1)

            def mask_scores(b, u, g, late):
                dve.wait_ge(scores_done, G * b + g + 1)
                if late or g >= 2:
                    dve.wait_ge(probs_ready, G * b + g - 1)
                dve.memset(turnstile[g][:, :], 0.0)
                dve.tensor_tensor_reduce(masked[g % 2][:, :].rearrange("p (c m) -> p c m", c=KC),
                                         score_bank[g % 2][:, :].rearrange("p (c m) -> p c m", c=KC),
                                         mask_neg[:, :, :], -1.0, 3.0e38, ALU.add, ALU.min,
                                         neg_max[u][:, g:g + 1]).then_inc(masked_ready, 1)

            def keep_k_low(b, u, late):
                dve.wait_ge(k_ready, b + 1)
                if late:
                    dve.wait_ge(scores_done, G * (b - 1))
                for m, rows in enumerate((slice(0, HALF), slice(HALF, P))):
                    last = dve.scalar_tensor_tensor(k_mix[u][rows, m, :], proj_bank[1][rows, :],
                                                    bk[rows, 0:1], k_high[u][rows, :], ALU.add, ALU.subtract)
                last.then_inc(k_low_ready, 1)

            def keep_pt(b, u, g, late):
                dve.wait_ge(p_turned, G * b + g + 1)
                if late and g == 1:
                    dve.wait_ge(attended, b - 1)
                dve.tensor_copy(probs_t[u][:, g, :, :], turn_bank[1][:, :].rearrange("p (c m) -> p c m", c=KC)).then_inc(pt_odd, 1)

            def spread_sums(b, u, late):
                dve.wait_ge(probs_ready, G * b + G)
                if late:
                    dve.wait_ge(attended, b - 1)
                dve.reciprocal(row_inv[u][:, :], row_sum[u][:, :]).then_inc(own_step, 1)
                dve.wait_ge(own_step, 3 * b + 1)
                dve.tensor_copy(row_inv_wide[u][:, :, :],
                                row_inv[u][:, :].unsqueeze(2).to_broadcast([P, G, S])).then_inc(inv_ready, 1)

            def own_heads(b, u):
                dve.wait_ge(attended, b + 1)
                at = lambda lo: out_bank[:, lo:lo + P].rearrange("p (h s) -> p h s", h=HG)
                dve.tensor_tensor(own_inv[:, :, :], at(P),
                                  groupmask[:, :].unsqueeze(2).to_broadcast([P, HG, S]), ALU.mult).then_inc(own_step, 1)
                dve.wait_ge(own_step, 3 * b + 2)
                dve.tensor_tensor(own_out[:, :, :], at(0), own_inv[:, :, :], ALU.mult).then_inc(own_step, 1)
                dve.wait_ge(own_step, 3 * b + 3)
                dve.tensor_reduce(heads_cols[:, bass.ds(b * S, S)], own_out[:, :, :].rearrange("p h s -> p s h"),
                                  AX.X, ALU.add).then_inc(heads_ready, 1)

            dve.wait_ge(x_in, 16)
            layer_norm(0, x_rows)
            dve.wait_ge(attn_w_in, 16 * ATTN_LOADS)
            keep_k_low(0, 0, False)
            dve.wait_ge(q_projected, 1)
            dve.wait_ge(attn_w_in, 16 * ATTN_LOADS)
            dve.tensor_scalar(q_cols[:, :], bank[3][:, :], bq[:, 0:1], SCALE, ALU.add, ALU.mult).then_inc(q_ready, 1)
            dve.wait_ge(q_ready, 1)
            dve.tensor_copy(q_high[:, :], q_cols[:, :]).then_inc(q_split, 1)
            dve.wait_ge(q_split, 1)
            for m, rows, others in ((0, slice(0, HALF), slice(HALF, P)), (1, slice(HALF, P), slice(0, HALF))):
                last = dve.tensor_tensor(q_parts[others, m, :], q_cols[rows, :], q_high[rows, :], ALU.subtract)
            last.then_inc(q_split, 1)
            dve.wait_ge(consts_built, 1)
            dve.tensor_reduce(groupmask[:, :], headmask[:, :].rearrange("p (g h) -> p h g", g=G), AX.X,
                              ALU.add).then_inc(heads_ready, 1)
            dve.wait_ge(heads_ready, 1)
            dve.wait_ge(mask_loaded, 16 * HG)
            dve.tensor_scalar(mask_neg[:, :, :], mask_in[:, :].rearrange("p (m c) -> p c m", c=KC),
                              NEG_BIG, None, ALU.mult).then_inc(mask_scaled, 1)
            dve.wait_ge(mask_scaled, 1)

            def sequence(b, u, late, last_one, first=False):
                mask_scores(b, u, 0, late)
                mask_scores(b, u, 1, late)
                if late:
                    keep_pt(b - 1, 1 - u, 3, True)
                    spread_sums(b - 1, 1 - u, not first)
                mask_scores(b, u, 2, late)
                if not last_one:
                    keep_k_low(b + 1, 1 - u, late)
                mask_scores(b, u, 3, late)
                keep_pt(b, u, 1, late and not first)
                if late:
                    own_heads(b - 1, 1 - u)

            sequence(0, 0, False, False)
            sequence(1, 1, True, False, first=True)
            with dve.Fori(1, PAIRS - 1) as i:
                for u in range(2):
                    sequence(2 * i + u, u, True, False)
            sequence(B - 2, 0, True, False)
            sequence(B - 1, 1, True, True)
            keep_pt(B - 1, 1, 3, True)
            spread_sums(B - 1, 1, True)
            own_heads(B - 1, 1)
            dve.wait_ge(heads_ready, B + 1)
            dve.tensor_scalar(heads_cols[:, :], heads_cols[:, :], bv[:, 0:1], None, ALU.add).then_inc(bv_added, 1)
            dve.wait_ge(attn_out, 1)
            dve.wait_ge(bo_added, 1)
            link(dve.tensor_tensor(x1_rows[:, :, :], bank[0][:, :].rearrange("p (t d) -> p t d", t=TT),
                                   xb_rows[:, :, :], ALU.add))

            layer_norm(1, x1_rows)
            for h in range(NH):
                steps_in = lambda t: t.rearrange("p (b s) -> p b s", s=S)
                dve.wait_ge(x_done, h + 1)
                dve.tensor_scalar(u_cols[:, 1, h, :], bank[2 + h], conv_w[:, 1, h, PAD:TAPS], None,
                                  ALU.mult).then_inc(conv_step, 1)
                for ahead in range(1, TAPS):
                    dve.wait_ge(conv_step, PAD * h + ahead)
                    so_far = steps_in(u_cols[:, 1, h, :])[:, :, 0:S - ahead]
                    dve.scalar_tensor_tensor(so_far, steps_in(bank[2 + h])[:, :, ahead:S],
                                             conv_w[:, 1, h, PAD - ahead:TAPS - ahead], so_far, ALU.mult,
                                             ALU.add).then_inc(conv_step if ahead < PAD else conv_done[1], 1)

            def bc_remainder(d):
                dve.wait_ge(bc_high, d + 1)
                dve.tensor_tensor(bc_rest[:, d, :], bank[4 + d], bc_parts[d][:, :], ALU.subtract).then_inc(bc_rested, 1)

            def bc_third_part(d):
                dve.wait_ge(bc_middle, d + 1)
                dve.tensor_tensor(bc_parts[d][64:96, :], bc_rest[64:96, d, :], bc_mid[64:96, d, :],
                                  ALU.subtract).then_inc(bc_split, 1)

            def lost_in_logs(d):
                for h in range(NH):
                    dve.wait_ge(exp_ready, d * NH + h + 1)
                    last = dve.tensor_scalar(dt_cols[:, d, h, :], sp_exp[d][:, h, :], 1.0, -1.0, ALU.add, ALU.add)
                link(last)
                for h in range(NH):
                    last = dve.tensor_tensor(dt_cols[:, d, h, :], sp_exp[d][:, h, :], dt_cols[:, d, h, :], ALU.subtract)
                link(last)

            def finish_dt(d):
                for h in range(NH):
                    dve.wait_ge(sp_summed, NH * d + h + 1)
                    dve.tensor_tensor(dt_cols[:, d, h, :], dt_cols[:, d, h, :], sp_pos[:, d, h, :], ALU.add).then_inc(dt_ready, 1)
                for h in range(NH):
                    dve.wait_ge(dt_ready, NH * d + h + 1)
                    dve.tensor_tensor(dtu[:, d, h, :], dt_cols[:, d, h, :], u_cols[:, d, h, :], ALU.mult).then_inc(dtu_ready, 1)

            bc_remainder(0)
            for h in range(NH):
                dve.wait_ge(abs_ready, h + 1)
                dve.tensor_scalar(sp_pos[:, 0, h, :], bank[h], bdt[:, 0, h:h + 1], 0.0,
                                  ALU.add, ALU.max).then_inc(pos_ready, 1)
            lost_in_logs(0)
            bc_third_part(0)
            finish_dt(0)
            bc_remainder(1)

            ends = lambda t, d: t[:, :] if d == 0 else t[:, ::-1]

            def scan(d, k, v, late):
                u = v % 2
                dve.wait_ge(decayed, NH * (k + 1))
                dve.wait_ge(fed, k + 1)
                if late:
                    dve.wait_ge(was_read, k - 3)
                dve.tensor_tensor_scan(ends(states[v], d), ends(duo[u][:, :, :].rearrange("p h t -> p (h t)"), d),
                                       ends(feed[u], d), 0.0, ALU.mult, ALU.add).then_inc(scanned, 1)

            def read_states(k, v, late):
                dve.wait_ge(c_spread, k + 1)
                dve.wait_ge(scanned, k + 1)
                if late:
                    dve.wait_ge(summed, k - 1)
                dve.tensor_tensor(both(read[v % 2]), both(states[v]),
                                  bank[5].unsqueeze(1).to_broadcast([P, NH, T]), ALU.mult).then_inc(was_read, 1)

            def step(d, k, v, scans_late=True, reads_late=True):
                scan(d, k + 1, (v + 1) % 4, scans_late)
                read_states(k, v, reads_late)

            scan(0, 0, 0, False)
            step(0, 0, 0, False, False)
            bc_third_part(1)
            lost_in_logs(1)
            finish_dt(1)
            dve.wait_ge(skip_summed, 1)
            for v in range(1, 4):
                step(0, v, v, v == 3, v >= 2)
            for d in range(DIRS):
                if d == 1:
                    for v in range(4):
                        step(1, N + v, v)
                with dve.Fori(1, N // 4 - 1) as i:
                    for v in range(4):
                        step(d, N * d + 4 * i + v, v)
                for v in range(3):
                    step(d, N * d + N - 4 + v, v)
                if d == 0:
                    step(1, N - 1, 3)
                else:
                    read_states(2 * N - 1, 3, True)
            dve.wait_ge(z_ready, NH)
            for h in range(NH):
                dve.wait_ge(halves_done, h + 1)
                last = dve.tensor_tensor(gated[:, h, :], bank[6 + h][:, :], z_act[:, h, :], ALU.mult)
            last.then_inc(gated_ready, 1)
            dve.wait_ge(mamba_out, 1)
            dve.scalar_tensor_tensor(x2_rows[:, :, :], bank[4][:, :].rearrange("p (t d) -> p t d", t=TT), 0.5,
                                     x1_rows[:, :, :], ALU.mult, ALU.add).then_inc(x2_ready, 1)
            dve.wait_ge(x2_ready, 1)

            layer_norm(2, x2_rows)
            dve.wait_ge(gates_ready, 1)
            for t in range(TT):
                mine = gates[:, t, :].unsqueeze(2).to_broadcast([P, E, E])
                other = gates[:, t, :].unsqueeze(1).to_broadcast([P, E, E])
                dve.tensor_tensor(beats[:, t, :, :], other, mine, ALU.is_gt)
                last = dve.tensor_tensor(ties[:, t, :, :], other, mine, ALU.is_equal)
            link(last)
            link(dve.tensor_tensor(ties[:, :, :, :], ties[:, :, :, :],
                                   earlier[:, :, :].unsqueeze(1).to_broadcast([P, TT, E, E]), ALU.mult))
            link(dve.tensor_tensor(beats[:, :, :, :], beats[:, :, :, :], ties[:, :, :, :], ALU.add))
            link(dve.tensor_reduce(rank[:, :, :], beats[:, :, :, :], AX.X, ALU.add))
            link(dve.scalar_tensor_tensor(kept[:, :, :], rank[:, :, :], float(TOPK), gates[:, :, :], ALU.is_lt, ALU.mult))
            link(dve.tensor_reduce(kept_sum[:, :], kept[:, :, :], AX.X, ALU.add))
            link(dve.reciprocal(kept_inv[:, :], kept_sum[:, :]))
            dve.tensor_tensor(combine[:, :, :], kept[:, :, :],
                              kept_inv[:, :].unsqueeze(2).to_broadcast([P, TT, E]), ALU.mult).then_inc(combine_ready, 1)
            link(dve.memset(comb_parts[:, :], 0.0))
            dve.wait_ge(combine_turned, 1)
            link(dve.tensor_copy(comb_parts[0:E, :], bank[4][0:E, :]))
            link(dve.tensor_tensor(comb_rest, bank[4][0:E, :], comb_parts[0:E, :], ALU.subtract))
            link(dve.tensor_copy(comb_mid, comb_rest))
            dve.tensor_copy(comb_parts[32:32 + E, :], comb_mid)
            dve.tensor_tensor(comb_parts[64:64 + E, :], comb_rest, comb_mid, ALU.subtract).then_inc(comb_split, 1)
            for j in range(EP):
                dve.wait_ge(h_mixed, j + 1)
                dve.wait_ge(comb_spread, j + 1)
                if j >= 2:
                    dve.wait_ge(h_used, j - 1)
                dve.tensor_tensor(hidden[j % 2][:, :], bank[6 + j % 2][:, :], mixed[j], ALU.mult).then_inc(h_ready, 1)
            dve.wait_ge(h_used, EP + 1)
            dve.tensor_tensor(y_rows[:, :, :], bank[5][:, :].rearrange("p (t d) -> p t d", t=TT), x2_rows[:, :, :],
                              ALU.add).then_inc(y_ready, 1)


_INS = ['x', 'ctx_1024', 'mask_1x1xSxS2_fk1', 'L0_xattn_wq_w', 'L0_xattn_wq_b', 'L0_xattn_wk_w', 'L0_xattn_wk_b',
        'L0_xattn_wv_w', 'L0_xattn_wv_b', 'L0_xattn_wo_w', 'L0_xattn_wo_b', 'L0_attn_W_in', 'L0_attn_conv_w',
        'L0_attn_conv_b', 'L0_attn_Wx', 'L0_attn_Wdt', 'L0_attn_bdt', 'L0_attn_A_log', 'L0_attn_D',
        'L0_attn_conv_w_b', 'L0_attn_conv_b_b', 'L0_attn_Wx_b', 'L0_attn_Wdt_b', 'L0_attn_bdt_b',
        'L0_attn_A_b_log', 'L0_attn_D_b', 'L0_attn_W_out', 'L0_ffn_gate_w', 'L0_ffn_ws_in', 'L0_ffn_vs_in',
        'L0_ffn_ws_out', 'L0_ffn_e_win', 'L0_ffn_e_vin', 'L0_ffn_e_wout']


def kernel(**inputs):
    import numpy as _np
    import concourse.bacc as _bacc
    from concourse import mybir as _mybir
    from concourse.bass_utils import run_bass_kernel_spmd as _run

    nc = _bacc.Bacc("TRN2", target_bir_lowering=False, num_devices=1)
    arrays, args = {}, {}
    for name in _INS:
        v = _np.ascontiguousarray(inputs[name])
        arrays[f"in_{name}_dram"] = v
        args[name] = nc.dram_tensor(f"in_{name}_dram", v.shape, _mybir.dt.from_np(v.dtype), kind="ExternalInput").ap()
    out = nc.dram_tensor("out_0_dram", (16, 32, 128), _mybir.dt.float32, kind="ExternalOutput").ap()
    perceiver_block(nc, args, out)
    r = _run(nc, [arrays], core_ids=[0])
    return r.results[0]["out_0_dram"]
```

```python
from contextlib import ExitStack

import concourse.bass as bass
from concourse import mybir

F32 = mybir.dt.float32
F32R = mybir.dt.float32r
BF16 = mybir.dt.bfloat16
ALU = mybir.AluOpType
ACT = mybir.ActivationFunctionType
AX = mybir.AxisListType

P = 128
EPS = 1e-5
NEG_BIG = -1e9


def perceiver_block(nc: bass.Bass, a: dict, out: bass.AP):
    B, S, D = a["x"].shape
    K = a["ctx_1024"].shape[1]
    T = B * S
    TT = T // P
    H = 16
    DH = D // H
    G = 4
    HG = H // G
    KC = K // P
    DI = a["L0_attn_W_in"].shape[0] // 2
    NH = DI // P
    N = a["L0_attn_A_log"].shape[1]
    R = a["L0_attn_Wdt"].shape[1]
    TAPS = a["L0_attn_conv_w"].shape[2]
    PAD = TAPS - 1
    E, _, HE = a["L0_ffn_e_win"].shape
    TOPK = 4
    EP = E * HE // P
    SCALE = float(DH) ** -0.5
    PAIRS = B // 2
    NP = N // 2
    DIRS = 2
    assert T == 512 and D == P and HG * S == P and K == 512 and 2 * N == 32

    with ExitStack() as ctx:
        def sb(name, shape, dt=F32):
            return ctx.enter_context(nc.sbuf_tensor(name, shape, dt))

        def sem(name):
            return ctx.enter_context(nc.semaphore(name))

        duo = [ctx.enter_context(nc.psum_tensor(f"duo{i}", [P, 2, 512], F32)) for i in range(4)]
        bank = [duo[i // 2][:, i % 2, :] for i in range(8)]

        ident = sb("ident", [P, P])
        headmask = sb("headmask", [P, H])
        groupmask = sb("groupmask", [P, HG])
        pick = sb("pick", [P, 32])
        pick_bc = sb("pick_bc", [P, 2 * N, P], BF16)
        pick_ex = sb("pick_ex", [P, E, HE], BF16)
        mixmask = sb("mixmask", [P, H // 2])
        earlier = sb("earlier", [P, E, E])

        wq = sb("wq", [P, D])
        wk = sb("wk", [P, D])
        wv = sb("wv", [P, D])
        wo = sb("wo", [P, D])
        bq = sb("bq", [P, 1])
        bk = sb("bk", [P, 1])
        bv = sb("bv", [P, 1])
        bo = sb("bo", [P, D])
        mask_in = sb("mask_in", [P, K])
        mask_neg = sb("mask_neg", [P, KC, P])
        w_in_rows = sb("w_in_rows", [P, 2 * NH, D])
        w_in = sb("w_in", [P, 2 * NH, P])
        wx_rows = sb("wx_rows", [R + 2 * N, DIRS, DI])
        wx_dt = sb("wx_dt", [P, DIRS, NH, R])
        wx_bc = sb("wx_bc", [P, DIRS, NH, 4, 2 * N])
        wdt_rows = sb("wdt_rows", [P, DIRS, NH, R])
        wdt = sb("wdt", [R, DIRS, NH, P])
        w_out_rows = sb("w_out_rows", [P, DI])
        w_out = sb("w_out", [P, NH, P])
        conv_w = sb("conv_w", [P, DIRS, NH, TAPS])
        conv_b = sb("conv_b", [P, DIRS, NH])
        bdt = sb("bdt", [P, DIRS, NH])
        a_log = sb("a_log", [P, DIRS, NH, N])
        a_exp = sb("a_exp", [P, DIRS, NH, N])
        a_neg = sb("a_neg", [P, DIRS, NH, N])
        d_skip = sb("d_skip", [P, DIRS, NH])
        gate_rows = sb("gate_rows", [E, D])
        gate_w = sb("gate_w", [P, E])
        ws_in = sb("ws_in", [P, P])
        vs_in = sb("vs_in", [P, P])
        ws_out = sb("ws_out", [P, D])
        win_parts = sb("win_parts", [P, 2, E * HE + P], F32R)
        vin_parts = sb("vin_parts", [P, 2, E * HE + P], F32R)
        ctx_high, ctx_low = vin_parts[:, 0, 0:K], vin_parts[:, 0, K:2 * K]
        wk_parts = vin_parts[:, 1, 0:2 * D].rearrange("p (m d) -> p m d", m=2)
        e_wout = sb("e_wout", [P, EP, D])

        x_rows = sb("x_rows", [P, TT, D])
        xb_rows = sb("xb_rows", [P, TT, D])
        x1_rows = sb("x1_rows", [P, TT, D])
        x2_rows = sb("x2_rows", [P, TT, D])
        y_rows = sb("y_rows", [P, TT, D])
        norm_rows = sb("norm_rows", [P, TT, D])
        norm_cols = sb("norm_cols", [P, T])
        stats = sb("stats", [P, TT, 6])
        moments = sb("moments", [P, TT, 2])
        ln_var = sb("ln_var", [P, TT])
        rstd = sb("rstd", [P, TT])
        newton = sb("newton", [P, 3, TT])
        q_cols = sb("q_cols", [P, T])
        heads_cols = sb("heads_cols", [P, T])

        def two(name, shape):
            t = sb(name, [P, 2, *shape])
            return t, [t[:, u] for u in range(2)]

        ctx_rows_all, ctx_rows = two("ctx_rows", [KC, D])
        ctx_cols = sb("ctx_cols", [P, K])
        HALF = P // 2
        k_high = [sb(f"k_high{u}", [P, K], F32R) for u in range(2)]
        k_mix = [sb(f"k_mix{u}", [P, 2, K], F32R) for u in range(2)]
        q_high = sb("q_high", [P, T], F32R)
        q_parts = sb("q_parts", [P, 2, T], F32R)
        v_rows_all, v_rows = two("v_rows", [KC, D])
        q_block = [sb(f"q_block{u}", [P, H, S], F32R) for u in range(2)]
        q_mix = [sb(f"q_mix{u}", [P, H, S], F32R) for u in range(2)]
        masked_all, masked = two("masked", [K])
        probs_all, probs = two("probs", [K])
        probs_t_all, probs_t = two("probs_t", [G, KC, P])
        neg_max = [sb(f"neg_max{u}", [P, G]) for u in range(2)]
        row_sum = [sb(f"row_sum{u}", [P, G]) for u in range(2)]
        row_inv = [sb(f"row_inv{u}", [P, G]) for u in range(2)]
        row_inv_wide = [sb(f"row_inv_wide{u}", [P, G, S]) for u in range(2)]
        turnstile = [sb(f"turnstile{s}", [P, 1]) for s in range(4)]
        own_inv = sb("own_inv", [P, HG, S])
        own_out = sb("own_out", [P, HG, S])

        norm_pad = sb("norm_pad", [P, B, S + 2 * PAD])
        zeros = sb("zeros", [P, NH * B])
        z_cols = sb("z_cols", [P, NH, T])
        z_act = probs_t_all[:, 1, 2:4].rearrange("p g c m -> p g (c m)")
        u_cols = sb("u_cols", [P, DIRS, NH, T])
        dt_low = sb("dt_low", [R, DIRS, T])
        bc_parts = [sb(f"bc_parts{d}", [P, T], BF16) for d in range(DIRS)]
        bc_rest = sb("bc_rest", [P, DIRS, T])
        bc_mid = sb("bc_mid", [P, DIRS, T], BF16)
        feed_all = sb("feed", [P, 2, NH * T])
        state_all = sb("state", [P, 2, NH * T])
        read_all = sb("read", [P, 2, NH * T])
        sp_pos = probs_t_all[:, 0].rearrange("p g c m -> p (g c m)").rearrange("p (d h t) -> p d h t", d=DIRS, h=NH)
        dt_cols = sb("dt_cols", [P, DIRS, NH, T])
        dtu = sb("dtu", [P, DIRS, NH, T])
        w_conv_rows = dt_cols[:, 0, 0, :].rearrange("p (j m) -> p j m", j=TAPS)
        w_conv = state_all[:, 0, 0:T].rearrange("p (j m) -> p j m", j=TAPS)
        e_win, e_vin = (feed_all[:, u, :].rearrange("p (e f) -> p e f", e=E) for u in range(2))
        b_wide = [sb("b_wide", [P, T]), mask_neg[:, :, :].rearrange("p c m -> p (c m)")]
        both = lambda t: t.rearrange("p (h t) -> p h t", h=NH)
        feed, state, read = ([t[:, u, :] for u in range(2)] for t in (feed_all, state_all, read_all))
        states = state + [t.rearrange("p u k -> p (u k)") for t in (masked_all, probs_all)]
        flat = lambda t: t.rearrange("p u c d -> p (u c d)")
        sp_abs, sp_exp, sp_ln = ([both(t[:, 1, :]), both(other)] for t, other in (
            (feed_all, flat(ctx_rows_all)), (state_all, flat(v_rows_all)),
            (read_all, probs_t_all[:, 1, 0:2].rearrange("p g c m -> p (g c m)"))))
        gated = probs_t_all[:, 1, 0:2].rearrange("p g c m -> p g (c m)")
        skip_parts = [both(t.rearrange("p u k -> p (u k)")) for t in (masked_all, probs_all)]

        norm_high, norm_low = k_high
        gates = sb("gates", [P, TT, E])
        beats, ties = (t[:, :, :].rearrange("p u k -> p (u k)").rearrange("p (t e f) -> p t e f", t=TT, e=E)
                       for t in (masked_all, probs_all))
        rank = sb("rank", [P, TT, E])
        kept = sb("kept", [P, TT, E])
        kept_sum = sb("kept_sum", [P, TT])
        kept_inv = sb("kept_inv", [P, TT])
        combine = sb("combine", [P, TT, E])
        comb_parts = bc_parts[0]
        comb_mid = bc_mid[0:E, 0, :]
        comb_rest = bc_rest[0:E, 0, :]
        act_in, v_in = [q_cols, heads_cols], b_wide
        mixed = [t[:, u, h * T:(h + 1) * T] for t in (feed_all, state_all, read_all) for u in range(2) for h in range(NH)]
        hidden = [v_rows_all[:, u].rearrange("p c d -> p (c d)") for u in range(2)]

        x_in, attn_w_in, out_w_in, mask_loaded, mamba_w_in, ffn_w_in = (
            sem(n) for n in ("x_in", "attn_w_in", "out_w_in", "mask_loaded", "mamba_w_in", "ffn_w_in"))
        ctx_in = [sem("ctx_in0"), sem("ctx_in1")]
        out_written = sem("out_written")
        consts_step, ident_built, consts_built, pads_cleared, bo_added = (
            sem(n) for n in ("consts_step", "ident_built", "consts_built", "pads_cleared", "bo_added"))
        picks_spread, groupmask_built, mask_scaled, a_ready = (
            sem(n) for n in ("picks_spread", "groupmask_built", "mask_scaled", "a_ready"))
        dve_step, act_step = sem("dve_step"), sem("act_step")
        ln_moments, ln_rstd, ln_rows, ln_turned, ln_cols = (
            sem(n) for n in ("ln_moments", "ln_rstd", "ln_rows", "ln_turned", "ln_cols"))
        weights_turned, weights_kept = sem("weights_turned"), sem("weights_kept")
        q_projected, q_ready, q_split, q_parts_kept, q_blocked = (
            sem(n) for n in ("q_projected", "q_ready", "q_split", "q_parts_kept", "q_blocked"))
        ctx_turned, ctx_kept, k_projected, k_ready, v_projected, v_ready = (
            sem(n) for n in ("ctx_turned", "ctx_kept", "k_projected", "k_ready", "v_projected", "v_ready"))
        k_low_ready, k_moved = sem("k_low_ready"), [sem("k_moved0"), sem("k_moved1")]
        x1_ready = sem("x1_ready")
        bv_added, wk_split, ctx_split = sem("bv_added"), sem("wk_split"), sem("ctx_split")
        scores_done, masked_ready, probs_ready, p_turned, pt_even, pt_odd = (
            sem(n) for n in ("scores_done", "masked_ready", "probs_ready", "p_turned", "pt_even", "pt_odd"))
        inv_ready, attended, own_step, heads_ready = (
            sem(n) for n in ("inv_ready", "attended", "own_step", "heads_ready"))
        attn_out, x_done, z_done, z_kept, z_ready = (
            sem(n) for n in ("attn_out", "x_done", "z_done", "z_kept", "z_ready"))
        u_ready = [sem(f"u_ready{d}") for d in range(DIRS)]
        conv_by_pe, conv_by_dve = sem("conv_by_pe"), sem("conv_by_dve")
        low_done, dt_low_kept, bc_done, bc_high, bc_rested, bc_middle, bc_split = (
            sem(n) for n in ("low_done", "dt_low_kept", "bc_done", "bc_high", "bc_rested", "bc_middle", "bc_split"))
        dt_raw, abs_ready, exp_ready, ln_ready, dt_ready, dtu_ready = (
            sem(n) for n in ("dt_raw", "abs_ready", "exp_ready", "ln_ready", "dt_ready", "dtu_ready"))
        pos_ready = [sem(f"pos_ready{d}") for d in range(DIRS)]
        sp_summed = [sem(f"sp_summed{d}") for d in range(DIRS)]
        taps_in, conv_turned, conv_kept, conv_step, b_kept = (
            sem(n) for n in ("taps_in", "conv_turned", "conv_kept", "conv_step", "b_kept"))
        b_spread, c_spread, decayed, fed, scanned, was_read, summed, skip_ready = (
            sem(n) for n in ("b_spread", "c_spread", "decayed", "fed", "scanned", "was_read", "summed",
                             "skip_ready"))
        skip_summed, w_high_ready, w_split, norm_split = (
            sem(n) for n in ("skip_summed", "w_high_ready", "w_split", "norm_split"))
        halves_done, gated_ready, mamba_out, x2_ready = (
            sem(n) for n in ("halves_done", "gated_ready", "mamba_out", "x2_ready"))
        gate_done, gates_ready, combine_ready, combine_turned, comb_split = (
            sem(n) for n in ("gate_done", "gates_ready", "combine_ready", "combine_turned", "comb_split"))
        h_done, h_act, v_kept, h_mixed, h_ready, comb_spread, h_used, y_ready = (
            sem(n) for n in ("h_done", "h_act", "v_kept", "h_mixed", "h_ready", "comb_spread", "h_used",
                             "y_ready"))

        score_bank, turn_bank, proj_bank, out_bank, v_bank = bank[0:2], bank[2:4], bank[4:6], bank[6], bank[7]
        rows_of = lambda t: t.rearrange("b s d -> (b s) d").rearrange("(t p) d -> p t d", p=P)
        column = lambda v: v.rearrange("(p o) -> p o", o=1)
        halves = lambda v: v.rearrange("(h p) -> p h", p=P)
        MAMBA = [("L0_attn_conv_w", "L0_attn_conv_b", "L0_attn_Wx", "L0_attn_Wdt", "L0_attn_bdt",
                  "L0_attn_A_log", "L0_attn_D"),
                 ("L0_attn_conv_w_b", "L0_attn_conv_b_b", "L0_attn_Wx_b", "L0_attn_Wdt_b",
                  "L0_attn_bdt_b", "L0_attn_A_b_log", "L0_attn_D_b")]
        ATTN_LOADS, OUT_LOADS, MAMBA_LOADS, FFN_LOADS = 5, 3, 2 + 8 * DIRS, 7

        block = ctx.enter_context(nc.Block())

        @block.sync
        def _(sp):
            def load_ctx(b, u, late):
                if late:
                    sp.wait_ge(ctx_turned, b - 1)
                src = a["ctx_1024"][bass.ds(b, 1)].rearrange("o (p c) d -> (o p) c d", c=KC)
                sp.dma_start(ctx_rows[u][:, :, :], src).then_inc(ctx_in[u], 16)

            sp.dma_start(x_rows[:, :, :], rows_of(a["x"])).then_inc(x_in, 16)
            load_ctx(0, 0, False)
            sp.dma_start(wk[:, :], a["L0_xattn_wk_w"]).then_inc(attn_w_in, 16)
            sp.dma_start(bk[:, :], column(a["L0_xattn_wk_b"])).then_inc(attn_w_in, 16)
            sp.dma_start(wq[:, :], a["L0_xattn_wq_w"]).then_inc(attn_w_in, 16)
            sp.dma_start(bq[:, :], column(a["L0_xattn_wq_b"])).then_inc(attn_w_in, 16)
            sp.dma_start(wv[:, :], a["L0_xattn_wv_w"]).then_inc(attn_w_in, 16)
            load_ctx(1, 1, False)
            for g in range(HG):
                sp.dma_start(mask_in[g * S:(g + 1) * S, :],
                             a["mask_1x1xSxS2_fk1"].rearrange("a b s k -> (a b s) k")).then_inc(mask_loaded, 16)

            def move_k(b, u):
                sp.wait_ge(k_ready, b + 1)
                sp.dma_start(k_mix[u][HALF:P, 0, :].bitcast(F32), k_high[u][0:HALF, :].bitcast(F32)).then_inc(k_moved[u], 16)
                sp.dma_start(k_mix[u][0:HALF, 1, :].bitcast(F32), k_high[u][HALF:P, :].bitcast(F32)).then_inc(k_moved[u], 16)

            for u in range(2):
                load_ctx(2 + u, u, True)
                move_k(u, u)
            sp.dma_start(wo[:, :], a["L0_xattn_wo_w"]).then_inc(out_w_in, 16)
            sp.dma_start(bv[:, :], column(a["L0_xattn_wv_b"])).then_inc(out_w_in, 16)
            sp.dma_start(bo[:, :], a["L0_xattn_wo_b"].partition_broadcast(P)).then_inc(out_w_in, 16)
            sp.dma_start(w_in_rows[:, :, :], a["L0_attn_W_in"].rearrange("(c p) d -> p c d", p=P)).then_inc(mamba_w_in, 16)
            sp.dma_start(w_out_rows[:, :], a["L0_attn_W_out"]).then_inc(mamba_w_in, 16)
            for d, (cw, cb, wx, wd, bd, al, ds) in enumerate(MAMBA):
                sp.dma_start(wx_rows[:, d, :], a[wx]).then_inc(mamba_w_in, 16)
                sp.dma_start(wdt_rows[:, d, :, :], a[wd].rearrange("(h p) r -> p h r", p=P)).then_inc(mamba_w_in, 16)
                sp.dma_start(conv_w[:, d, :, :], a[cw].rearrange("(h p) o j -> p h (o j)", p=P)).then_inc(mamba_w_in, 16)
                sp.dma_start(a_log[:, d, :, :], a[al].rearrange("(h p) n -> p h n", p=P)).then_inc(mamba_w_in, 16)
                sp.dma_start(conv_b[:, d, :], halves(a[cb]), allow_slow_non_contiguous=True).then_inc(mamba_w_in, 16)
                sp.dma_start(bdt[:, d, :], halves(a[bd]), allow_slow_non_contiguous=True).then_inc(mamba_w_in, 16)
                sp.dma_start(d_skip[:, d, :], halves(a[ds]), allow_slow_non_contiguous=True).then_inc(mamba_w_in, 16)
                sp.dma_start(gate_rows[:, :], a["L0_ffn_gate_w"]).then_inc(mamba_w_in, 16) if d == 0 else \
                    sp.dma_start(ws_out[:, :], a["L0_ffn_ws_out"]).then_inc(mamba_w_in, 16)
            with sp.Fori(2, PAIRS) as i:
                for u in range(2):
                    load_ctx(2 * i + u, u, True)
                    move_k(2 * i - 2 + u, u)
            for u in range(2):
                move_k(B - 2 + u, u)
            sp.dma_start(e_win, a["L0_ffn_e_win"].rearrange("e d h -> d e h")).then_inc(ffn_w_in, 16)
            sp.dma_start(e_vin, a["L0_ffn_e_vin"].rearrange("e d h -> d e h")).then_inc(ffn_w_in, 16)
            sp.dma_start(e_wout[:, :, :], a["L0_ffn_e_wout"].rearrange("(j e) h d -> (e h) j d", j=EP)).then_inc(ffn_w_in, 16)
            sp.dma_start(ws_in[:, :], a["L0_ffn_ws_in"]).then_inc(ffn_w_in, 16)
            sp.dma_start(vs_in[:, :], a["L0_ffn_vs_in"]).then_inc(ffn_w_in, 16)
            sp.wait_ge(y_ready, 1)
            sp.dma_start(rows_of(out), y_rows[:, :, :]).then_inc(out_written, 16)
            sp.wait_ge(out_written, 16)

        @block.gpsimd
        def _(pool):
            built = [0]

            def link(ins):
                built[0] += 1
                ins.then_inc(consts_step, 1)
                pool.wait_ge(consts_step, built[0])

            def where(t, pattern, base, step, compare, fill):
                return nc.gpsimd.affine_select(out=t, in_=t, compare_op=compare, fill=fill, base=base,
                                               pattern=pattern, channel_multiplier=step)

            link(pool.memset(ident[:, :], 0.0))
            where(ident[:, :], [[-1, P]], 0, 1, ALU.not_equal, 1.0).then_inc(ident_built, 1)
            link(pool.memset(headmask[:, :], 1.0))
            link(where(headmask[:, :], [[-DH, H]], 0, 1, ALU.is_ge, 0.0))
            link(where(headmask[:, :], [[DH, H]], DH - 1, -1, ALU.is_ge, 0.0))
            link(pool.tensor_tensor(mixmask[:, :], headmask[:, 0:H // 2], headmask[:, H // 2:H], ALU.add))
            link(pool.memset(pick[:, :], 0.0))
            for part in range(3):
                link(where(pick[:, :], [[-1, 32]], -32 * part, 1, ALU.not_equal, 1.0))
            link(pool.memset(earlier[:, :, :], 1.0))
            where(earlier[:, :, :], [[1, E], [-1, E]], -1, 0, ALU.is_ge, 0.0).then_inc(consts_built, 1)
            pool.memset(norm_pad[:, :, :], 0.0).then_inc(pads_cleared, 1)
            pool.memset(zeros[:, :], 0.0).then_inc(pads_cleared, 1)

            def block_q(b, u, late, first=False):
                if late:
                    pool.wait_ge(scores_done, G * (b - 1))
                pool.tensor_tensor(q_block[u][:, :, :],
                                   q_high[:, bass.ds(b * S, S)].unsqueeze(1).to_broadcast([P, H, S]),
                                   headmask[:, :].unsqueeze(2).to_broadcast([P, H, S]), ALU.mult)
                if first:
                    pool.wait_ge(q_split, 2)
                    pool.wait_ge(q_parts_kept, 1)
                for m in range(2):
                    last = pool.tensor_tensor(q_mix[u][:, m * H // 2:(m + 1) * H // 2, :],
                                              q_parts[:, m, bass.ds(b * S, S)].unsqueeze(1).to_broadcast([P, H // 2, S]),
                                              mixmask[:, :].unsqueeze(2).to_broadcast([P, H // 2, S]), ALU.mult)
                last.then_inc(q_blocked, 1)

            def split_ctx(b):
                pool.wait_ge(ctx_kept, b + 1)
                pool.wait_ge(k_projected, b)
                pool.tensor_tensor(ctx_low, ctx_cols[:, :], ctx_high, ALU.subtract).then_inc(ctx_split, 1)

            pool.wait_ge(attn_w_in, 16 * ATTN_LOADS)
            pool.tensor_copy(wk_parts[:, 0, :], wk[:, :]).then_inc(wk_split, 1)
            pool.wait_ge(wk_split, 1)
            pool.tensor_tensor(wk_parts[:, 1, :], wk[:, :], wk_parts[:, 0, :], ALU.subtract).then_inc(wk_split, 1)
            pool.wait_ge(q_split, 1)
            for u in range(2):
                block_q(u, u, False, u == 0)
            with pool.Fori(1, PAIRS) as i:
                for u in range(2):
                    split_ctx(2 * i + u)
                    block_q(2 * i + u, u, True)
            pool.wait_ge(x_in, 16)
            pool.wait_ge(out_w_in, 16 * OUT_LOADS)
            pool.tensor_tensor(xb_rows[:, :, :], x_rows[:, :, :],
                               bo[:, :].unsqueeze(1).to_broadcast([P, TT, D]), ALU.add).then_inc(bo_added, 1)
            pool.wait_ge(mamba_w_in, 16 * MAMBA_LOADS)
            pool.tensor_tensor(w_conv_rows, w_in_rows[:, 0, :].unsqueeze(1).to_broadcast([P, TAPS, D]),
                               conv_w[:, 0, 0, :].unsqueeze(2).to_broadcast([P, TAPS, D]), ALU.mult).then_inc(taps_in, 1)
            pool.tensor_copy(pick_bc[:, :, :], pick[:, :].unsqueeze(2).to_broadcast([P, 2 * N, P])).then_inc(picks_spread, 1)
            pool.tensor_copy(pick_ex[:, :, :], pick[:, 0:E].unsqueeze(2).to_broadcast([P, E, HE])).then_inc(picks_spread, 1)

            pool.wait_ge(k_projected, B)
            pool.wait_ge(ffn_w_in, 16 * (FFN_LOADS - 2))
            pieces = [(feed_all[:, u, :], parts, slice(0, E * HE)) for u, parts in enumerate((win_parts, vin_parts))]
            pieces += [(t[:, :], parts, slice(E * HE, E * HE + P)) for t, parts in ((ws_in, win_parts), (vs_in, vin_parts))]
            for whole, parts, at in pieces:
                pool.tensor_copy(parts[:, 0, at], whole).then_inc(w_high_ready, 1)
            for n, (whole, parts, at) in enumerate(pieces):
                pool.wait_ge(w_high_ready, n + 1)
                pool.tensor_tensor(parts[:, 1, at], whole, parts[:, 0, at], ALU.subtract).then_inc(w_split, 1)

            for d in range(DIRS):
                pool.wait_ge(u_ready[d], NH)
                pool.tensor_tensor(skip_parts[d], u_cols[:, d, :, :],
                                   d_skip[:, d, :].unsqueeze(2).to_broadcast([P, NH, T]), ALU.mult).then_inc(skip_ready, 1)

            def sum_softplus(d, halves):
                for h in halves:
                    pool.wait_ge(pos_ready[d], h + 1)
                    pool.wait_ge(ln_ready, NH * d + h + 1)
                    pool.tensor_tensor(sp_pos[:, d, h, :], sp_pos[:, d, h, :], sp_ln[d][:, h, :],
                                       ALU.add).then_inc(sp_summed[d], 1)

            def feed_states(d, k, u, late):
                pool.wait_ge(b_kept, k + 1)
                if late:
                    pool.wait_ge(scanned, k - 1)
                pool.tensor_tensor(both(feed[u]), dtu[:, d, :, :],
                                   b_wide[u][:, :].unsqueeze(1).to_broadcast([P, NH, T]), ALU.mult).then_inc(fed, 1)

            sum_softplus(0, [1])
            pool.wait_ge(bc_middle, 1)
            pool.wait_ge(sp_summed[0], 1)
            pool.tensor_tensor(bc_parts[0][64:96, :], bc_rest[64:96, 0, :], bc_mid[64:96, 0, :],
                               ALU.subtract).then_inc(bc_split, 1)
            for d in range(DIRS):
                pool.wait_ge(dtu_ready, NH * (d + 1))
                for u in range(2):
                    feed_states(d, N * d + u, u, d == 1)
                feed_states(d, N * d + 2, 0, True)
                if d == 0:
                    sum_softplus(1, range(NH))
                feed_states(d, N * d + 3, 1, True)
                with pool.Fori(2, NP) as i:
                    for u in range(2):
                        feed_states(d, N * d + 2 * i + u, u, True)

            pool.wait_ge(halves_done, NH)
            for j in range(EP + 1):
                pool.wait_ge(h_act, j + 1)
                pool.wait_ge(v_kept, j + 1)
                pool.tensor_tensor(mixed[j], act_in[j % 2][:, :], v_in[j % 2][:, :], ALU.mult).then_inc(h_mixed, 1)

        @block.tensor
        def _(pe):
            def keep_warm(to, products):
                for _ in range(products):
                    pe.matmul(to[:, 0:P], ident[:, :], ident[:, :], start=True, stop=True)

            def turn_norm(n):
                to = bank[(2, 1, 5)[n]]
                for t in range(TT):
                    pe.wait_ge(ln_rows, TT * n + t + 1)
                    last = pe.transpose(to[:, t * P:(t + 1) * P], norm_rows[:, t, :], ident[:, :])
                last.then_inc(ln_turned, 1)

            def turn_ctx(b, u, i, late):
                pe.wait_ge(ctx_in[u], 16 * (i + 1))
                if late:
                    pe.wait_ge(ctx_kept, b)
                for c in range(KC):
                    last = pe.transpose(proj_bank[0][:, c * P:(c + 1) * P], ctx_rows[u][:, c, :], ident[:, :])
                last.then_inc(ctx_turned, 1)

            def first_k(b):
                pe.wait_ge(ctx_kept, b + 1)
                if b:
                    pe.wait_ge(k_low_ready, b)
                pe.matmul(proj_bank[1][:, :], wk[:, :], ctx_cols[:, :], start=True, stop=True).then_inc(k_projected, 1)

            def project_k(b):
                pe.wait_ge(ctx_split, b - 1)
                pe.wait_ge(k_low_ready, b)
                for n, (part, ctx_part) in enumerate(((0, ctx_high), (1, ctx_high), (0, ctx_low))):
                    last = pe.matmul(proj_bank[1][:, :], wk_parts[:, part, :], ctx_part, start=(n == 0), stop=(n == 2))
                last.then_inc(k_projected, 1)

            def project_v(b, late):
                if late:
                    pe.wait_ge(v_ready, b)
                for c in range(KC):
                    last = pe.matmul(v_bank[:, c * P:(c + 1) * P], ctx_cols[:, c * P:(c + 1) * P],
                                     wv[:, :], start=True, stop=True)
                last.then_inc(v_projected, 1)

            def score(b, u, i, g, late):
                if g == 0:
                    pe.wait_ge(q_blocked, b + 1)
                    pe.wait_ge(k_ready, b + 1)
                    pe.wait_ge(k_low_ready, b + 1)
                    pe.wait_ge(k_moved[u], 32 * (i + 1))
                if late or g >= 2:
                    pe.wait_ge(masked_ready, G * b + g - 1)
                pe.matmul(score_bank[g % 2][:, :], q_block[u][:, g * HG:(g + 1) * HG, :],
                          k_high[u][:, :], start=True, stop=False)
                pe.matmul(score_bank[g % 2][:, :], q_mix[u][:, g * HG:(g + 1) * HG, :],
                          k_mix[u][:, g // 2, :], start=False, stop=True).then_inc(scores_done, 1)

            def turn_p(b, g, late):
                pe.wait_ge(probs_ready, G * b + g + 1)
                if late or g >= 2:
                    pe.wait_ge((pt_even, pt_odd)[g % 2], 2 * b + g // 2)
                for c in range(KC):
                    last = pe.transpose(turn_bank[g % 2][:, c * P:(c + 1) * P],
                                        probs[g % 2][:, c * P:(c + 1) * P], ident[:, :])
                last.then_inc(p_turned, 1)

            def attend(b, u):
                pe.wait_ge(pt_even, 2 * b + 2)
                pe.wait_ge(pt_odd, 2 * b + 2)
                pe.wait_ge(v_ready, b + 1)
                pe.wait_ge(inv_ready, b + 1)
                pe.wait_ge(heads_ready, b + 1)
                pe.matmul(out_bank[:, P:2 * P], row_inv_wide[u][:, :, :], ident[:, :], start=True, stop=True)
                for c in range(KC):
                    for g in range(G):
                        rows = slice(g * 32, g * 32 + 32)
                        last = pe.matmul(out_bank[rows, 0:P], v_rows[u][:, c, rows], probs_t[u][:, g, c, :],
                                         start=(c == 0), stop=(c == KC - 1))
                last.then_inc(attended, 1)

            def turn_weights():
                pe.wait_ge(mamba_w_in, 16 * MAMBA_LOADS)
                pe.wait_ge(v_ready, B)
                pe.wait_ge(x1_ready, 1)
                for c in range(2 * NH):
                    last = pe.transpose(bank[4][:, c * P:(c + 1) * P], w_in_rows[:, c, :], ident[:, :])
                last.then_inc(weights_turned, 1)
                W = R + 2 * N
                for d in range(DIRS):
                    for h in range(NH):
                        at = (d * NH + h) * W
                        last = pe.transpose(bank[5][:, at:at + W], wx_rows[:, d, h * P:(h + 1) * P], ident[0:W, 0:W])
                last.then_inc(weights_turned, 1)
                for h in range(NH):
                    pe.transpose(bank[7][:, h * P:(h + 1) * P], w_out_rows[:, h * P:(h + 1) * P], ident[:, :])
                pe.transpose(bank[7][:, NH * P:NH * P + E], gate_rows[:, :], ident[0:E, 0:E]).then_inc(weights_turned, 1)

            def turn_wdt():
                for d in range(DIRS):
                    for h in range(NH):
                        at = (d * NH + h) * P
                        last = pe.transpose(bank[3][0:R, at:at + P], wdt_rows[:, d, h, :], ident[:, :])
                last.then_inc(weights_turned, 1)

            pe.wait_ge(ident_built, 1)
            keep_warm(bank[0], 6)
            turn_ctx(0, 0, 0, False)
            keep_warm(bank[0], 3)
            pe.wait_ge(attn_w_in, 16 * ATTN_LOADS)
            first_k(0)
            turn_norm(0)
            project_v(0, False)
            pe.wait_ge(ln_cols, 1)
            pe.matmul(bank[3][:, :], wq[:, :], norm_cols[:, :], start=True, stop=True).then_inc(q_projected, 1)
            turn_ctx(1, 1, 0, True)
            first_k(1)
            pe.wait_ge(wk_split, 2)

            def project_out(tiles, n):
                pe.wait_ge(bv_added, n)
                pe.wait_ge(ctx_kept, B)
                pe.wait_ge(out_w_in, 16 * OUT_LOADS)
                if n == 2:
                    pe.wait_ge(weights_kept, 1)
                for t in tiles:
                    last = pe.matmul(bank[4][:, t * P:(t + 1) * P] if n == 1 else bank[0][:, t * P:(t + 1) * P],
                                     heads_cols[:, t * P:(t + 1) * P], wo[:, :], start=True, stop=True)
                last.then_inc(attn_out, 1)

            def sequence(b, u, i, late, left, beside=None):
                score(b, u, i, 0, late)
                score(b, u, i, 1, late)
                if late:
                    turn_p(b - 1, 3, True)
                if left:
                    project_v(b + 1, True)
                if left == 2:
                    turn_ctx(b + 2, u, i + 1, True)
                score(b, u, i, 2, late)
                turn_p(b, 0, late)
                score(b, u, i, 3, late)
                if late:
                    attend(b - 1, 1 - u)
                turn_p(b, 1, late)
                if beside:
                    beside()
                turn_p(b, 2, late)
                if left == 2:
                    project_k(b + 2)

            sequence(0, 0, 0, False, 2)
            sequence(1, 1, 0, True, 2)
            with pe.Fori(1, PAIRS - 1) as i:
                for u in range(2):
                    sequence(2 * i + u, u, i, True, 2)
            sequence(B - 2, 0, PAIRS - 1, True, 1)
            sequence(B - 1, 1, PAIRS - 1, True, 0, beside=lambda: project_out(range(TT - 1), 1))
            turn_p(B - 1, 3, True)
            attend(B - 1, 1)
            turn_weights()
            turn_wdt()

            project_out([TT - 1], 2)

            pe.wait_ge(taps_in, 1)
            for j in range(TAPS):
                last = pe.transpose(bank[2][:, j * P:(j + 1) * P], w_conv_rows[:, j, :], ident[:, :])
            last.then_inc(conv_turned, 1)
            pe.wait_ge(weights_kept, 3)
            keep_warm(bank[7], 14)
            turn_norm(1)
            pe.wait_ge(ln_cols, 2)
            here = norm_pad[:, :, PAD:PAD + S]
            pe.wait_ge(weights_kept, 4)
            pe.wait_ge(conv_kept, 1)
            for h in (1, 0):
                pe.matmul(bank[2 + h], w_in[:, h, :], here, start=True, stop=True).then_inc(x_done, 1)
            for back in range(TAPS):
                last = pe.matmul(bank[0], w_conv[:, PAD - back, :], norm_pad[:, :, PAD - back:PAD - back + S],
                                 start=(back == 0), stop=(back == TAPS - 1))
            last.then_inc(conv_by_pe, 1)

            def project_z(h):
                pe.matmul(bank[4 + h], w_in[:, NH + h, :], here, start=True, stop=True).then_inc(z_done, 1)

            def project_low(d):
                pe.wait_ge(u_ready[d], NH)
                for h in range(NH):
                    last = pe.matmul(bank[6 + d][0:R, :], wx_dt[:, d, h, :], u_cols[:, d, h, :],
                                     start=(h == 0), stop=(h == NH - 1))
                last.then_inc(low_done, 1)

            def project_bc(d):
                pe.wait_ge(z_kept, d + 1)
                for h in range(NH):
                    last = pe.matmul(bank[4 + d], wx_bc[:, d, h, :, :], u_cols[:, d, h, :],
                                     start=(h == 0), stop=(h == NH - 1))
                last.then_inc(bc_done, 1)

            def project_dt(d):
                pe.wait_ge(dt_low_kept, d + 1)
                for h in range(NH):
                    pe.matmul(bank[2 * d + h], wdt[:, d, h, :], dt_low[:, d, :],
                              start=True, stop=True).then_inc(dt_raw, 1)

            project_z(0)
            project_low(0)
            project_bc(0)
            project_dt(0)
            project_z(1)
            project_low(1)
            project_dt(1)
            keep_warm(bank[7], 8)
            pe.wait_ge(picks_spread, 2)
            pe.wait_ge(bc_split, 1)
            pe.matmul(bank[4], pick_bc[:, 0, :], bc_parts[0][:, :], start=True, stop=True).then_inc(b_spread, 1)
            project_bc(1)

            def spread_b(d, n, k):
                pe.wait_ge(b_kept, k)
                pe.matmul(bank[4], pick_bc[:, bass.ds(n, 1), :].rearrange("p o m -> p (o m)"),
                          bc_parts[d][:, :], start=True, stop=True).then_inc(b_spread, 1)

            def spread_c(d, n, k):
                pe.wait_ge(was_read, k)
                pe.matmul(bank[5], pick_bc[:, bass.ds(n + N, 1), :].rearrange("p o m -> p (o m)"),
                          bc_parts[d][:, :], start=True, stop=True).then_inc(c_spread, 1)

            def add_up(k, u, stop):
                pe.wait_ge(was_read, k + 1)
                for h in range(NH):
                    last = pe.matmul(bank[6 + h], ident[:, :], read[u][:, h * T:(h + 1) * T],
                                     start=False, stop=stop)
                last.then_inc(summed, 1)

            spread_b(0, 1, 1)
            pe.wait_ge(skip_ready, DIRS)
            pe.wait_ge(z_kept, NH)

            def add_skip(h):
                for d in range(DIRS):
                    last = pe.matmul(bank[6 + h], ident[:, :], skip_parts[d][:, h, :], start=(d == 0), stop=False)
                last.then_inc(skip_summed, 1)

            add_skip(0)
            pe.wait_ge(bc_rested, DIRS)
            pe.matmul(bank[5], pick_bc[:, N, :], bc_parts[0][:, :], start=True, stop=True).then_inc(c_spread, 1)
            add_skip(1)
            spread_b(0, 2, 2)
            spread_b(0, 3, 3)

            def unit(k, u, d_b, n_b, d_c, n_c):
                spread_c(d_c, n_c, k + 1)
                if n_b is not None:
                    spread_b(d_b, n_b, k + 4)
                add_up(k, u, False)

            for d in range(DIRS):
                with pe.Fori(0, NP - 2) as i:
                    for u in range(2):
                        unit(N * d + 2 * i + u, u, d, 2 * i + u + 4, d, 2 * i + u + 1)
                if d == 0:
                    pe.wait_ge(bc_split, DIRS)
                for n in range(N - 4, N - 1):
                    unit(N * d + n, n % 2, 1, n + 4 - N if d == 0 else None, d, n + 1)
                if d == 0:
                    unit(N - 1, 1, 1, 3, 1, 0)
            pe.wait_ge(was_read, 2 * N)
            for h in range(NH):
                pe.matmul(bank[6 + h], ident[:, :], read[1][:, h * T:(h + 1) * T],
                          start=False, stop=True).then_inc(halves_done, 1)
            pe.wait_ge(gated_ready, 1)
            for t in range(TT):
                for h in range(NH):
                    last = pe.matmul(bank[4][:, t * P:(t + 1) * P], gated[:, h, t * P:(t + 1) * P], w_out[:, h, :],
                                     start=(h == 0), stop=(h == NH - 1))
            last.then_inc(mamba_out, 1)

            keep_warm(bank[0], 17)
            turn_norm(2)
            keep_warm(bank[0], 4)
            pe.wait_ge(ln_cols, 3)
            pe.wait_ge(x2_ready, 1)
            for t in range(TT):
                last = pe.matmul(bank[4][:, t * E:(t + 1) * E], norm_cols[:, t * P:(t + 1) * P], gate_w[:, :],
                                 start=True, stop=True)
            last.then_inc(gate_done, 1)
            keep_warm(bank[0], 2)
            pe.wait_ge(w_split, 4)
            pe.wait_ge(norm_split, 2)

            def hidden_in(j):
                if j >= 2:
                    pe.wait_ge(h_act, j - 1)
                    pe.wait_ge(v_kept, j - 1)
                at = slice(j * P, (j + 1) * P)
                products = ((0, norm_high), (0, norm_low), (1, norm_high))
                for to, parts in ((bank[j % 2], win_parts), (bank[2 + j % 2], vin_parts)):
                    for n, (part, norm_part) in enumerate(products):
                        last = pe.matmul(to[:, :], parts[:, part, at], norm_part[:, :], start=(n == 0), stop=(n == 2))
                last.then_inc(h_done, 1)

            def spread_combine(j):
                if j >= 2:
                    pe.wait_ge(h_ready, j - 1)
                pe.matmul(bank[6 + j % 2][:, :], pick_ex[:, 2 * j:2 * j + 2, :], comb_parts[:, :],
                          start=True, stop=True).then_inc(comb_spread, 1)

            def hidden_out(j, first, stop):
                if j < EP:
                    pe.wait_ge(h_ready, j + 1)
                else:
                    pe.wait_ge(h_mixed, EP + 1)
                w = e_wout[:, j, :] if j < EP else ws_out[:, :]
                left = hidden[j % 2] if j < EP else mixed[EP]
                for t in range(TT):
                    last = pe.matmul(bank[5][:, t * P:(t + 1) * P], left[:, t * P:(t + 1) * P], w,
                                     start=(first and t == 0), stop=stop, skip_group_check=True)
                last.then_inc(h_used, 1)

            for j in range(EP + 1):
                if j == EP:
                    pe.wait_ge(comb_split, 1)
                    spread_combine(0)
                    spread_combine(1)
                hidden_in(j)
                if j == EP // 2 + 1:
                    pe.wait_ge(combine_ready, 1)
                    for t in range(TT):
                        last = pe.transpose(bank[4][0:E, t * P:(t + 1) * P], combine[:, t, :], ident[:, :])
                    last.then_inc(combine_turned, 1)
            for j in range(EP):
                hidden_out(j, j == 0, False)
                if j + 2 < EP:
                    spread_combine(j + 2)
            hidden_out(EP, False, True)

        @block.scalar
        def _(act):
            nc.scalar.preload_act_table_set("natural_log_exp_and_others")

            def inv_std(n):
                act.wait_ge(ln_moments, n + 1)
                act.activation(ln_var[:, :], moments[:, :, 1], ACT.Ln, bias=EPS).then_inc(act_step, 1)
                act.wait_ge(act_step, n + 1)
                act.activation(rstd[:, :], ln_var[:, :], ACT.Exp, scale=-0.5).then_inc(ln_rstd, 1)

            def keep_ctx(b, late, parts=False):
                act.wait_ge(ctx_turned, b + 1)
                if late:
                    act.wait_ge(v_projected, b)
                if parts:
                    act.copy(ctx_high, proj_bank[0][:, :])
                act.copy(ctx_cols[:, :], proj_bank[0][:, :]).then_inc(ctx_kept, 1)

            def keep_k(b, u, late):
                act.wait_ge(k_projected, b + 1)
                if late:
                    act.wait_ge(scores_done, G * (b - 1))
                act.activation(k_high[u][:, :], proj_bank[1][:, :], ACT.Identity,
                               bias=bk[:, 0:1]).then_inc(k_ready, 1)

            def keep_v(b, u, late):
                act.wait_ge(v_projected, b + 1)
                if late:
                    act.wait_ge(attended, b - 1)
                act.copy(v_rows[u][:, :, :], v_bank[:, :].rearrange("p (c d) -> p c d", c=KC)).then_inc(v_ready, 1)

            def exponentials(b, u, g, late, first):
                act.wait_ge(masked_ready, G * b + g + 1)
                if late or g >= 2:
                    act.wait_ge(p_turned, G * b + g - 1)
                if late and not first and g == 0:
                    act.wait_ge(inv_ready, b - 1)
                act.activation(probs[g % 2][:, :], masked[g % 2][:, :], ACT.Exp, bias=neg_max[u][:, g:g + 1],
                               scale=-1.0, accum_out=row_sum[u][:, g:g + 1]).then_inc(probs_ready, 1)

            def keep_pt(b, u, g, late):
                act.wait_ge(p_turned, G * b + g + 1)
                if late and g == 0:
                    act.wait_ge(attended, b - 1)
                act.copy(probs_t[u][:, g, :, :], turn_bank[0][:, :].rearrange("p (c m) -> p c m", c=KC)).then_inc(pt_even, 1)

            inv_std(0)
            keep_ctx(0, False)
            act.wait_ge(attn_w_in, 16 * ATTN_LOADS)
            keep_k(0, 0, False)
            keep_v(0, 0, False)
            keep_ctx(1, True)
            act.wait_ge(q_ready, 1)
            for m, rows in enumerate((slice(0, HALF), slice(HALF, P))):
                last = act.copy(q_parts[rows, m, :], q_cols[rows, :])
            last.then_inc(q_parts_kept, 1)
            keep_k(1, 1, False)

            def sequence(b, u, late, left, first=False):
                exponentials(b, u, 0, late, first)
                exponentials(b, u, 1, late, first)
                if left == 2:
                    keep_ctx(b + 2, True, parts=True)
                keep_pt(b, u, 0, late and not first)
                exponentials(b, u, 2, late, first)
                if left:
                    keep_v(b + 1, 1 - u, late)
                exponentials(b, u, 3, late, first)
                keep_pt(b, u, 2, late)
                if left == 2:
                    keep_k(b + 2, u, True)

            sequence(0, 0, False, 2)
            sequence(1, 1, True, 2, first=True)
            with act.Fori(1, PAIRS - 1) as i:
                for u in range(2):
                    sequence(2 * i + u, u, True, 2)
            sequence(B - 2, 0, True, 1)
            sequence(B - 1, 1, True, 0)

            act.wait_ge(weights_turned, 1)
            act.copy(w_in[:, :, :], bank[4][:, :].rearrange("p (c m) -> p c m", m=P)).then_inc(weights_kept, 1)
            act.wait_ge(weights_turned, 2)
            W = R + 2 * N
            turned = bank[5][:, 0:DIRS * NH * W].rearrange("p (d h w) -> p d h w", d=DIRS, h=NH)
            act.copy(wx_dt[:, :, :, :], turned[:, :, :, 0:R]).then_inc(act_step, 1)
            for d in range(DIRS):
                for h in range(NH):
                    last = act.copy(wx_bc[:, d, h, :, :], turned[:, d, h, R:W].unsqueeze(1).to_broadcast([P, 4, 2 * N]))
            last.then_inc(weights_kept, 1)
            act.wait_ge(weights_turned, 3)
            act.copy(w_out[:, :, :], bank[7][:, 0:NH * P].rearrange("p (h m) -> p h m", h=NH)).then_inc(act_step, 1)
            act.copy(gate_w[:, :], bank[7][:, NH * P:NH * P + E]).then_inc(weights_kept, 1)
            act.wait_ge(weights_turned, 4)
            act.copy(wdt[:, :, :, :], bank[3][0:R, :].rearrange("p (d h m) -> p d h m", d=DIRS, h=NH)).then_inc(weights_kept, 1)
            act.wait_ge(mamba_w_in, 16 * MAMBA_LOADS)
            act.activation(a_exp[:, :, :, :], a_log[:, :, :, :], ACT.Exp).then_inc(act_step, 1)
            act.wait_ge(act_step, 4)
            act.mul(a_neg[:, :, :, :], a_exp[:, :, :, :], -1.0).then_inc(a_ready, 1)

            def keep_dt_low(d):
                act.wait_ge(low_done, d + 1)
                act.copy(dt_low[:, d, :], bank[6 + d][0:R, :]).then_inc(dt_low_kept, 1)

            def keep_z(h):
                act.wait_ge(z_done, h + 1)
                act.copy(z_cols[:, h, :], bank[4 + h]).then_inc(z_kept, 1)

            def bc_first_part(d):
                act.wait_ge(bc_done, d + 1)
                act.copy(bc_parts[d][:, :], bank[4 + d]).then_inc(bc_high, 1)

            def bc_second_part(d):
                act.wait_ge(bc_rested, d + 1)
                act.copy(bc_mid[:, d, :], bc_rest[:, d, :])
                act.copy(bc_parts[d][32:64, :], bc_rest[32:64, d, :]).then_inc(bc_middle, 1)

            def absolutes(d):
                for h in range(NH):
                    act.wait_ge(dt_raw, d * NH + h + 1)
                    act.activation(sp_abs[d][:, h, :], bank[2 * d + h], ACT.Abs,
                                   bias=bdt[:, d, h:h + 1]).then_inc(abs_ready, 1)

            def exps(d):
                for h in range(NH):
                    act.wait_ge(abs_ready, d * NH + h + 1)
                    act.activation(sp_exp[d][:, h, :], sp_abs[d][:, h, :], ACT.Exp, scale=-1.0).then_inc(exp_ready, 1)

            def logs(d):
                for h in range(NH):
                    act.wait_ge(exp_ready, d * NH + h + 1)
                    act.activation(sp_ln[d][:, h, :], sp_exp[d][:, h, :], ACT.Ln, bias=1.0).then_inc(ln_ready, 1)

            inv_std_steps = 5
            act.wait_ge(ln_moments, 2)
            act.activation(ln_var[:, :], moments[:, :, 1], ACT.Ln, bias=EPS).then_inc(act_step, 1)
            act.wait_ge(act_step, inv_std_steps)
            act.activation(rstd[:, :], ln_var[:, :], ACT.Exp, scale=-0.5).then_inc(ln_rstd, 1)
            act.wait_ge(conv_turned, 1)
            act.copy(w_conv, bank[2].rearrange("p (j m) -> p j m", j=TAPS)).then_inc(conv_kept, 1)

            def silu_u(d, h):
                act.activation(u_cols[:, d, h, :], bank[0] if d + h == 0 else u_cols[:, d, h, :], ACT.Silu,
                               bias=conv_b[:, d, h:h + 1]).then_inc(u_ready[d], 1)

            act.wait_ge(conv_by_dve, 1)
            silu_u(0, 1)
            act.wait_ge(conv_by_pe, 1)
            silu_u(0, 0)
            act.wait_ge(conv_by_dve, 2)
            silu_u(1, 1)
            keep_z(0)
            keep_dt_low(0)
            act.wait_ge(conv_by_dve, 3)
            silu_u(1, 0)
            bc_first_part(0)
            nc.scalar.preload_act_table_set("natural_log_exp_and_others")
            act.wait_ge(w_split, 4)
            absolutes(0)
            exps(0)
            keep_dt_low(1)
            logs(0)
            bc_second_part(0)
            keep_z(1)
            absolutes(1)

            steps_of = lambda t: t.rearrange("p (b s) -> p b s", s=S)

            def no_decay(d, k, u, late):
                if late:
                    act.wait_ge(scanned, k - 1)
                first = 0 if d == 0 else S - 1
                act.copy(duo[u][:, :, :].rearrange("p h (b s) -> p (h b) s", s=S)[:, :, first:first + 1],
                         zeros[:, :].unsqueeze(2)).then_inc(act_step, 1)

            def decays(d, n, k, u, late):
                if late:
                    act.wait_ge(scanned, k - 1)
                steps = slice(1, S) if d == 0 else slice(0, S - 1)
                for h in range(NH):
                    act.wait_ge(dt_ready, NH * d + h + 1)
                    act.activation(steps_of(duo[u][:, h, :])[:, :, steps], steps_of(dt_cols[:, d, h, :])[:, :, steps],
                                   ACT.Exp, scale=a_neg[:, d, h, bass.ds(n, 1)]).then_inc(decayed, 1)

            def keep_b(k, u, late):
                act.wait_ge(b_spread, k + 1)
                if late:
                    act.wait_ge(fed, k - 1)
                act.copy(b_wide[u][:, :], bank[4]).then_inc(b_kept, 1)

            act.wait_ge(a_ready, 1)
            act.wait_ge(pads_cleared, 2)
            act.wait_ge(pos_ready[0], NH)
            keep_b(0, 0, False)
            no_decay(0, 0, 0, False)
            decays(0, 0, 0, 0, False)
            bc_first_part(1)
            keep_b(1, 1, False)
            for h in range(NH):
                act.activation(sp_pos[:, 1, h, :], bank[2 + h], ACT.Relu, bias=bdt[:, 1, h:h + 1]).then_inc(pos_ready[1], 1)
            act.wait_ge(pos_ready[1], NH)
            act.wait_ge(abs_ready, DIRS * NH)
            no_decay(0, 1, 1, False)
            decays(0, 1, 1, 1, False)
            bc_second_part(1)
            keep_b(2, 0, True)
            exps(1)
            logs(1)
            for d in range(DIRS):
                if d == 1:
                    for u in range(2):
                        no_decay(1, N + u, u, True)
                        decays(1, u, N + u, u, True)
                        keep_b(N + u + 1, 1 - u, True)
                with act.Fori(1, NP - 1) as i:
                    for u in range(2):
                        decays(d, 2 * i + u, N * d + 2 * i + u, u, True)
                        keep_b(N * d + 2 * i + u + 1, 1 - u, True)
                for u in range(2):
                    decays(d, N - 2 + u, N * d + N - 2 + u, u, True)
                    if d == 0 or u == 0:
                        keep_b(N * d + N - 2 + u + 1, 1 - u, True)
            for h in range(NH):
                act.activation(z_act[:, h, :], z_cols[:, h, :], ACT.Silu).then_inc(z_ready, 1)
            nc.scalar.preload_act_table_set("natural_log_exp_and_others")

            act.wait_ge(ln_moments, 3)
            act.activation(ln_var[:, :], moments[:, :, 1], ACT.Ln, bias=EPS).then_inc(act_step, 1)
            act.wait_ge(act_step, inv_std_steps + 2 * DIRS + 1)
            act.activation(rstd[:, :], ln_var[:, :], ACT.Exp, scale=-0.5).then_inc(ln_rstd, 1)
            act.wait_ge(gate_done, 1)
            act.activation(gates[:, :, :], bank[4][:, 0:TT * E].rearrange("p (t e) -> p t e", e=E),
                           ACT.Sigmoid).then_inc(gates_ready, 1)
            for j in range(EP + 1):
                act.wait_ge(h_done, j + 1)
                if j >= 2:
                    act.wait_ge(h_mixed, j - 1)
                act.activation(act_in[j % 2][:, :], bank[j % 2][:, :], ACT.Silu).then_inc(h_act, 1)
                act.copy(v_in[j % 2][:, :], bank[2 + j % 2][:, :]).then_inc(v_kept, 1)

        @block.vector
        def _(dve):
            steps = [0]

            def link(ins):
                steps[0] += 1
                ins.then_inc(dve_step, 1)
                dve.wait_ge(dve_step, steps[0])

            def layer_norm(n, rows, tiles=range(TT)):
                if n:
                    dve.wait_ge(ln_turned, n)
                for t in tiles:
                    last = dve.bn_stats(stats[:, t, :], rows[:, t, :])
                link(last)
                for t in range(TT):
                    last = dve.bn_aggr(moments[:, t, :], stats[:, t, :])
                last.then_inc(ln_moments, 1)
                dve.wait_ge(ln_moments, n + 1)
                link(dve.tensor_scalar(newton[:, 0, :], moments[:, :, 1], EPS, None, ALU.add))
                dve.wait_ge(ln_rstd, n + 1)
                link(dve.tensor_tensor(newton[:, 1, :], rstd[:, :], rstd[:, :], ALU.mult))
                link(dve.tensor_tensor(newton[:, 1, :], newton[:, 1, :], newton[:, 0, :], ALU.mult))
                link(dve.tensor_scalar(newton[:, 1, :], newton[:, 1, :], -0.5, 1.5, ALU.mult, ALU.add))
                link(dve.tensor_tensor(newton[:, 2, :], newton[:, 1, :], rstd[:, :], ALU.mult))
                for t in range(TT):
                    dve.tensor_scalar(norm_rows[:, t, :], rows[:, t, :], moments[:, t, 0:1],
                                      newton[:, 2, t:t + 1], ALU.subtract, ALU.mult).then_inc(ln_rows, 1)
                dve.wait_ge(ln_turned, n + 1)
                if n == 1:
                    dve.wait_ge(pads_cleared, 2)
                to = norm_pad[:, :, PAD:PAD + S] if n == 1 else norm_cols[:, :].rearrange("p (b s) -> p b s", s=S)
                dve.tensor_copy(to, bank[(2, 1, 5)[n]][:, :].rearrange("p (b s) -> p b s", s=S)).then_inc(ln_cols, 1)

            def mask_scores(b, u, g, late):
                dve.wait_ge(scores_done, G * b + g + 1)
                if late or g >= 2:
                    dve.wait_ge(probs_ready, G * b + g - 1)
                dve.memset(turnstile[g][:, :], 0.0)
                dve.tensor_tensor_reduce(masked[g % 2][:, :].rearrange("p (c m) -> p c m", c=KC),
                                         score_bank[g % 2][:, :].rearrange("p (c m) -> p c m", c=KC),
                                         mask_neg[:, :, :], -1.0, 3.0e38, ALU.add, ALU.min,
                                         neg_max[u][:, g:g + 1]).then_inc(masked_ready, 1)

            def keep_k_low(b, u, late):
                dve.wait_ge(k_ready, b + 1)
                if late:
                    dve.wait_ge(scores_done, G * (b - 1))
                for m, rows in enumerate((slice(0, HALF), slice(HALF, P))):
                    last = dve.scalar_tensor_tensor(k_mix[u][rows, m, :], proj_bank[1][rows, :],
                                                    bk[rows, 0:1], k_high[u][rows, :], ALU.add, ALU.subtract)
                last.then_inc(k_low_ready, 1)

            def keep_pt(b, u, g, late):
                dve.wait_ge(p_turned, G * b + g + 1)
                if late and g == 1:
                    dve.wait_ge(attended, b - 1)
                dve.tensor_copy(probs_t[u][:, g, :, :], turn_bank[1][:, :].rearrange("p (c m) -> p c m", c=KC)).then_inc(pt_odd, 1)

            def spread_sums(b, u, late):
                dve.wait_ge(probs_ready, G * b + G)
                if late:
                    dve.wait_ge(attended, b - 1)
                dve.reciprocal(row_inv[u][:, :], row_sum[u][:, :]).then_inc(own_step, 1)
                dve.wait_ge(own_step, 3 * b + 1)
                dve.tensor_copy(row_inv_wide[u][:, :, :],
                                row_inv[u][:, :].unsqueeze(2).to_broadcast([P, G, S])).then_inc(inv_ready, 1)

            def own_heads(b, u):
                dve.wait_ge(attended, b + 1)
                at = lambda lo: out_bank[:, lo:lo + P].rearrange("p (h s) -> p h s", h=HG)
                dve.tensor_tensor(own_inv[:, :, :], at(P),
                                  groupmask[:, :].unsqueeze(2).to_broadcast([P, HG, S]), ALU.mult).then_inc(own_step, 1)
                dve.wait_ge(own_step, 3 * b + 2)
                dve.tensor_tensor(own_out[:, :, :], at(0), own_inv[:, :, :], ALU.mult).then_inc(own_step, 1)
                dve.wait_ge(own_step, 3 * b + 3)
                dve.tensor_reduce(heads_cols[:, bass.ds(b * S, S)], own_out[:, :, :].rearrange("p h s -> p s h"),
                                  AX.X, ALU.add).then_inc(heads_ready, 1)

            dve.wait_ge(x_in, 16)
            layer_norm(0, x_rows)
            dve.wait_ge(attn_w_in, 16 * ATTN_LOADS)
            keep_k_low(0, 0, False)
            dve.wait_ge(q_projected, 1)
            dve.wait_ge(attn_w_in, 16 * ATTN_LOADS)
            dve.tensor_scalar(q_cols[:, :], bank[3][:, :], bq[:, 0:1], SCALE, ALU.add, ALU.mult).then_inc(q_ready, 1)
            dve.wait_ge(q_ready, 1)
            dve.tensor_copy(q_high[:, :], q_cols[:, :]).then_inc(q_split, 1)
            dve.wait_ge(q_split, 1)
            for m, rows, others in ((0, slice(0, HALF), slice(HALF, P)), (1, slice(HALF, P), slice(0, HALF))):
                last = dve.tensor_tensor(q_parts[others, m, :], q_cols[rows, :], q_high[rows, :], ALU.subtract)
            last.then_inc(q_split, 1)
            dve.wait_ge(consts_built, 1)
            dve.tensor_reduce(groupmask[:, :], headmask[:, :].rearrange("p (g h) -> p h g", g=G), AX.X,
                              ALU.add).then_inc(heads_ready, 1)
            dve.wait_ge(heads_ready, 1)
            dve.wait_ge(mask_loaded, 16 * HG)
            dve.tensor_scalar(mask_neg[:, :, :], mask_in[:, :].rearrange("p (m c) -> p c m", c=KC),
                              NEG_BIG, None, ALU.mult).then_inc(mask_scaled, 1)
            dve.wait_ge(mask_scaled, 1)

            def add_bv(tiles, n):
                at = slice(tiles[0] * P, (tiles[-1] + 1) * P)
                dve.wait_ge(out_w_in, 16 * OUT_LOADS)
                dve.tensor_scalar(heads_cols[:, at], heads_cols[:, at], bv[:, 0:1], None, ALU.add).then_inc(bv_added, 1)

            def finish_x1(tiles, n):
                at = slice(tiles[0], tiles[-1] + 1)
                dve.wait_ge(attn_out, n)
                dve.wait_ge(bo_added, 1)
                dve.tensor_tensor(x1_rows[:, at, :], bank[4 if n == 1 else 0].rearrange("p (t d) -> p t d", t=TT)[:, at, :],
                                  xb_rows[:, at, :], ALU.add).then_inc(x1_ready, 1)
                dve.wait_ge(x1_ready, n)

            def sequence(b, u, late, last_one, first=False):
                mask_scores(b, u, 0, late)
                mask_scores(b, u, 1, late)
                if late:
                    keep_pt(b - 1, 1 - u, 3, True)
                    spread_sums(b - 1, 1 - u, not first)
                mask_scores(b, u, 2, late)
                if not last_one:
                    keep_k_low(b + 1, 1 - u, late)
                mask_scores(b, u, 3, late)
                keep_pt(b, u, 1, late and not first)
                if late:
                    own_heads(b - 1, 1 - u)

            sequence(0, 0, False, False)
            sequence(1, 1, True, False, first=True)
            with dve.Fori(1, PAIRS - 1) as i:
                for u in range(2):
                    sequence(2 * i + u, u, True, False)
            sequence(B - 2, 0, True, False)
            dve.wait_ge(heads_ready, B - 2)
            add_bv(range(TT - 1), 1)
            sequence(B - 1, 1, True, True)
            keep_pt(B - 1, 1, 3, True)
            spread_sums(B - 1, 1, True)
            finish_x1(range(TT - 1), 1)
            for t in range(TT - 1):
                dve.bn_stats(stats[:, t, :], x1_rows[:, t, :])
            own_heads(B - 1, 1)
            dve.wait_ge(heads_ready, B + 1)
            add_bv([TT - 1], 2)
            finish_x1([TT - 1], 2)

            layer_norm(1, x1_rows, tiles=[TT - 1])
            steps_in = lambda t: t.rearrange("p (b s) -> p b s", s=S)
            for n, (d, h) in enumerate(((0, 1), (1, 1), (1, 0))):
                dve.wait_ge(x_done, 2 - h)
                x_in_bank, convolved = steps_in(bank[2 + h]), steps_in(u_cols[:, d, h, :])
                dve.tensor_scalar(u_cols[:, d, h, :], bank[2 + h], conv_w[:, d, h, PAD:TAPS], None,
                                  ALU.mult).then_inc(conv_step, 1)
                for by in range(1, TAPS):
                    dve.wait_ge(conv_step, PAD * n + by)
                    to, fro = (slice(by, S), slice(0, S - by)) if d == 0 else (slice(0, S - by), slice(by, S))
                    dve.scalar_tensor_tensor(convolved[:, :, to], x_in_bank[:, :, fro],
                                             conv_w[:, d, h, PAD - by:TAPS - by], convolved[:, :, to], ALU.mult,
                                             ALU.add).then_inc(conv_step if by < PAD else conv_by_dve, 1)

            def bc_remainder(d):
                dve.wait_ge(bc_high, d + 1)
                dve.tensor_tensor(bc_rest[:, d, :], bank[4 + d], bc_parts[d][:, :], ALU.subtract).then_inc(bc_rested, 1)

            def lost_in_logs(d):
                for h in range(NH):
                    dve.wait_ge(exp_ready, d * NH + h + 1)
                    last = dve.tensor_scalar(dt_cols[:, d, h, :], sp_exp[d][:, h, :], 1.0, -1.0, ALU.add, ALU.add)
                link(last)
                for h in range(NH):
                    last = dve.tensor_tensor(dt_cols[:, d, h, :], sp_exp[d][:, h, :], dt_cols[:, d, h, :], ALU.subtract)
                link(last)

            def finish_dt(d):
                if d == 0:
                    dve.wait_ge(ln_ready, 1)
                    link(dve.tensor_tensor(sp_pos[:, 0, 0, :], sp_pos[:, 0, 0, :], sp_ln[0][:, 0, :], ALU.add))
                for h in range(NH):
                    if d == 1 or h == 1:
                        dve.wait_ge(sp_summed[d], h + 1 if d == 1 else 1)
                    dve.tensor_tensor(dt_cols[:, d, h, :], dt_cols[:, d, h, :], sp_pos[:, d, h, :], ALU.add).then_inc(dt_ready, 1)
                for h in range(NH):
                    dve.wait_ge(dt_ready, NH * d + h + 1)
                    dve.tensor_tensor(dtu[:, d, h, :], dt_cols[:, d, h, :], u_cols[:, d, h, :], ALU.mult).then_inc(dtu_ready, 1)

            bc_remainder(0)
            for h in range(NH):
                dve.wait_ge(abs_ready, h + 1)
                dve.tensor_scalar(sp_pos[:, 0, h, :], bank[h], bdt[:, 0, h:h + 1], 0.0,
                                  ALU.add, ALU.max).then_inc(pos_ready[0], 1)
            lost_in_logs(0)
            finish_dt(0)
            bc_remainder(1)

            ends = lambda t, d: t[:, :] if d == 0 else t[:, ::-1]

            def scan(d, k, v, late):
                u = v % 2
                dve.wait_ge(decayed, NH * (k + 1))
                dve.wait_ge(fed, k + 1)
                if late:
                    dve.wait_ge(was_read, k - 3)
                dve.tensor_tensor_scan(ends(states[v], d), ends(duo[u][:, :, :].rearrange("p h t -> p (h t)"), d),
                                       ends(feed[u], d), 0.0, ALU.mult, ALU.add).then_inc(scanned, 1)

            def read_states(k, v, late):
                dve.wait_ge(c_spread, k + 1)
                dve.wait_ge(scanned, k + 1)
                if late:
                    dve.wait_ge(summed, k - 1)
                dve.tensor_tensor(both(read[v % 2]), both(states[v]),
                                  bank[5].unsqueeze(1).to_broadcast([P, NH, T]), ALU.mult).then_inc(was_read, 1)

            def step(d, k, v, scans_late=True, reads_late=True):
                scan(d, k + 1, (v + 1) % 4, scans_late)
                read_states(k, v, reads_late)

            scan(0, 0, 0, False)
            read_states(0, 0, False)
            scan(0, 1, 1, False)
            dve.wait_ge(bc_middle, DIRS)
            dve.tensor_tensor(bc_parts[1][64:96, :], bc_rest[64:96, 1, :], bc_mid[64:96, 1, :],
                              ALU.subtract).then_inc(bc_split, 1)
            lost_in_logs(1)
            dve.wait_ge(skip_summed, NH)
            step(0, 1, 1, False, False)
            finish_dt(1)
            for v in range(2, 4):
                step(0, v, v, v == 3, True)
            for d in range(DIRS):
                if d == 1:
                    for v in range(4):
                        step(1, N + v, v)
                with dve.Fori(1, N // 4 - 1) as i:
                    for v in range(4):
                        step(d, N * d + 4 * i + v, v)
                for v in range(3):
                    step(d, N * d + N - 4 + v, v)
                if d == 0:
                    step(1, N - 1, 3)
                else:
                    read_states(2 * N - 1, 3, True)
            dve.wait_ge(z_ready, NH)
            for h in range(NH):
                dve.wait_ge(halves_done, h + 1)
                last = dve.tensor_tensor(gated[:, h, :], bank[6 + h][:, :], z_act[:, h, :], ALU.mult)
            last.then_inc(gated_ready, 1)
            dve.wait_ge(mamba_out, 1)
            dve.scalar_tensor_tensor(x2_rows[:, :, :], bank[4][:, :].rearrange("p (t d) -> p t d", t=TT), 0.5,
                                     x1_rows[:, :, :], ALU.mult, ALU.add).then_inc(x2_ready, 1)
            dve.wait_ge(x2_ready, 1)

            layer_norm(2, x2_rows)
            dve.wait_ge(ln_cols, 3)
            dve.tensor_copy(norm_high[:, :], norm_cols[:, :]).then_inc(norm_split, 1)
            dve.wait_ge(norm_split, 1)
            dve.tensor_tensor(norm_low[:, :], norm_cols[:, :], norm_high[:, :], ALU.subtract).then_inc(norm_split, 1)
            dve.wait_ge(gates_ready, 1)
            for t in range(TT):
                mine = gates[:, t, :].unsqueeze(2).to_broadcast([P, E, E])
                other = gates[:, t, :].unsqueeze(1).to_broadcast([P, E, E])
                dve.tensor_tensor(beats[:, t, :, :], other, mine, ALU.is_gt)
                last = dve.tensor_tensor(ties[:, t, :, :], other, mine, ALU.is_equal)
            link(last)
            link(dve.tensor_tensor(ties[:, :, :, :], ties[:, :, :, :],
                                   earlier[:, :, :].unsqueeze(1).to_broadcast([P, TT, E, E]), ALU.mult))
            link(dve.tensor_tensor(beats[:, :, :, :], beats[:, :, :, :], ties[:, :, :, :], ALU.add))
            link(dve.tensor_reduce(rank[:, :, :], beats[:, :, :, :], AX.X, ALU.add))
            link(dve.scalar_tensor_tensor(kept[:, :, :], rank[:, :, :], float(TOPK), gates[:, :, :], ALU.is_lt, ALU.mult))
            link(dve.tensor_reduce(kept_sum[:, :], kept[:, :, :], AX.X, ALU.add))
            link(dve.reciprocal(kept_inv[:, :], kept_sum[:, :]))
            dve.tensor_tensor(combine[:, :, :], kept[:, :, :],
                              kept_inv[:, :].unsqueeze(2).to_broadcast([P, TT, E]), ALU.mult).then_inc(combine_ready, 1)
            link(dve.memset(comb_parts[:, :], 0.0))
            dve.wait_ge(combine_turned, 1)
            link(dve.tensor_copy(comb_parts[0:E, :], bank[4][0:E, :]))
            link(dve.tensor_tensor(comb_rest, bank[4][0:E, :], comb_parts[0:E, :], ALU.subtract))
            link(dve.tensor_copy(comb_mid, comb_rest))
            dve.tensor_copy(comb_parts[32:32 + E, :], comb_mid)
            dve.tensor_tensor(comb_parts[64:64 + E, :], comb_rest, comb_mid, ALU.subtract).then_inc(comb_split, 1)
            for j in range(EP):
                dve.wait_ge(h_mixed, j + 1)
                dve.wait_ge(comb_spread, j + 1)
                if j >= 2:
                    dve.wait_ge(h_used, j - 1)
                dve.tensor_tensor(hidden[j % 2][:, :], bank[6 + j % 2][:, :], mixed[j], ALU.mult).then_inc(h_ready, 1)
            dve.wait_ge(h_used, EP + 1)
            dve.tensor_tensor(y_rows[:, :, :], bank[5][:, :].rearrange("p (t d) -> p t d", t=TT), x2_rows[:, :, :],
                              ALU.add).then_inc(y_ready, 1)


_INS = ['x', 'ctx_1024', 'mask_1x1xSxS2_fk1', 'L0_xattn_wq_w', 'L0_xattn_wq_b', 'L0_xattn_wk_w', 'L0_xattn_wk_b',
        'L0_xattn_wv_w', 'L0_xattn_wv_b', 'L0_xattn_wo_w', 'L0_xattn_wo_b', 'L0_attn_W_in', 'L0_attn_conv_w',
        'L0_attn_conv_b', 'L0_attn_Wx', 'L0_attn_Wdt', 'L0_attn_bdt', 'L0_attn_A_log', 'L0_attn_D',
        'L0_attn_conv_w_b', 'L0_attn_conv_b_b', 'L0_attn_Wx_b', 'L0_attn_Wdt_b', 'L0_attn_bdt_b',
        'L0_attn_A_b_log', 'L0_attn_D_b', 'L0_attn_W_out', 'L0_ffn_gate_w', 'L0_ffn_ws_in', 'L0_ffn_vs_in',
        'L0_ffn_ws_out', 'L0_ffn_e_win', 'L0_ffn_e_vin', 'L0_ffn_e_wout']


def kernel(**inputs):
    import numpy as _np
    import concourse.bacc as _bacc
    from concourse import mybir as _mybir
    from concourse.bass_utils import run_bass_kernel_spmd as _run

    nc = _bacc.Bacc("TRN2", target_bir_lowering=False, num_devices=1)
    arrays, args = {}, {}
    for name in _INS:
        v = _np.ascontiguousarray(inputs[name])
        arrays[f"in_{name}_dram"] = v
        args[name] = nc.dram_tensor(f"in_{name}_dram", v.shape, _mybir.dt.from_np(v.dtype), kind="ExternalInput").ap()
    out = nc.dram_tensor("out_0_dram", (16, 32, 128), _mybir.dt.float32, kind="ExternalOutput").ap()
    perceiver_block(nc, args, out)
    r = _run(nc, [arrays], core_ids=[0])
    return r.results[0]["out_0_dram"]
```
